# Optimizing a Trainium2 kernel written in Bass

```python
import numpy as np
import jax
import jax.numpy as jnp

def _softmax(x, axis=-1):
    return jax.nn.softmax(x, axis=axis)

def _gelu(x):
    return jax.nn.gelu(x, approximate=True)

def _silu(x):
    return jax.nn.silu(x)

def _sigmoid(x):
    return jax.nn.sigmoid(x)

def _layernorm(x, axis=-1, eps=1e-05):
    m = jnp.mean(x, axis=axis, keepdims=True)
    v = jnp.var(x, axis=axis, keepdims=True)
    return (x - m) / jnp.sqrt(v + eps)

def _scatter_add(tgt, idx, src, axis=0):
    return tgt.at[idx].add(src)

def _segment_sum(src, seg, n):
    return jax.ops.segment_sum(src, seg, n)
kernel_name = 'mk_seq_postln_d2_jaxref_r8_89d953'

def setup_inputs(seed: int=0):
    np.random.seed(seed)
    _w = jnp.asarray

    def _L0_attn_setup():
        import jax, jax.numpy as jnp
        import numpy as np
        DIM = 128
        NUM_HEADS = 16
        HEAD_DIM = DIM // NUM_HEADS

        def _rope_tables(seq_len, dim, dtype):
            inv_freq = 1.0 / 10000.0 ** (jnp.arange(0, dim, 2, dtype=jnp.float32) / dim)
            t = jnp.arange(seq_len, dtype=jnp.float32)
            freqs = jnp.outer(t, inv_freq)
            return (jnp.cos(freqs).astype(dtype), jnp.sin(freqs).astype(dtype))

        def _apply_rope(x, cos_emb, sin_emb):
            x1 = x[..., 0::2]
            x2 = x[..., 1::2]
            return jnp.concatenate((x1 * cos_emb - x2 * sin_emb, x1 * sin_emb + x2 * cos_emb), axis=-1)
        key = jax.random.key(seed)
        k_x, k_qkv, k_out, k_b = jax.random.split(key, 4)
        B, S, D = (2, 256, DIM)
        x = jax.random.normal(k_x, (B, S, D), dtype=jnp.float32)
        w_qkv = jax.random.normal(k_qkv, (3 * D, D), dtype=jnp.float32) * (1.0 / np.sqrt(D))
        w_out = jax.random.normal(k_out, (D, D), dtype=jnp.float32) * (1.0 / np.sqrt(D))
        b_out = jax.random.normal(k_b, (D,), dtype=jnp.float32) * 0.01
        return {'x': x, 'w_qkv': w_qkv, 'w_out': w_out, 'b_out': b_out}
    _L0_attn_in = _L0_attn_setup()

    def _L0_ffn_setup():
        import jax, jax.numpy as jnp
        import numpy as np
        EPS = 1e-06
        LN_EPS = 1e-05

        def _absmean_core(W):
            gamma = jnp.mean(jnp.abs(W)) + EPS
            Ws = W / gamma
            Wq = jnp.sign(Ws) * jnp.minimum(jnp.round(jnp.abs(Ws)), 1.0)
            return (Wq, gamma)

        @jax.custom_vjp
        def absmean(W):
            return _absmean_core(W)[0]

        def _absmean_fwd(W):
            Wq, gamma = _absmean_core(W)
            return (Wq, gamma)

        def _absmean_bwd(gamma, g):
            return (g / gamma,)
        absmean.defvjp(_absmean_fwd, _absmean_bwd)

        def layernorm(x, w, b, eps=LN_EPS):
            mu = jnp.mean(x, axis=-1, keepdims=True)
            var = jnp.mean((x - mu) ** 2, axis=-1, keepdims=True)
            return (x - mu) * jax.lax.rsqrt(var + eps) * w + b
        key = jax.random.key(seed)
        k1, k2, k3 = jax.random.split(key, 3)
        d, h = (128, 512)
        B, T = (8, 256)
        return {'x': jax.random.normal(k1, (B, T, d), jnp.float32), 'W_fc': jax.random.normal(k2, (h, d), jnp.float32), 'ln_w': jnp.ones((h,), jnp.float32), 'ln_b': jnp.zeros((h,), jnp.float32), 'W_proj': jax.random.normal(k3, (d, h), jnp.float32)}
    _L0_ffn_in = _L0_ffn_setup()

    def _L1_attn_setup():
        import jax, jax.numpy as jnp
        import numpy as np
        EPS = 1e-05

        def _layernorm(x, g, b):
            mu = jnp.mean(x, axis=-1, keepdims=True)
            var = jnp.mean(jnp.square(x - mu), axis=-1, keepdims=True)
            return (x - mu) * jax.lax.rsqrt(var + EPS) * g + b
        key = jax.random.key(seed)
        ks = jax.random.split(key, 5)
        dims, head = (128, 16)
        b, n = (2, 256)
        s = 0.02
        return {'x': jax.random.normal(ks[0], (b, n, dims), dtype=jnp.float32), 'ln_g': jnp.ones((dims,), dtype=jnp.float32), 'ln_b': jnp.zeros((dims,), dtype=jnp.float32), 'W_kv': jax.random.normal(ks[1], (dims, 2 * dims), dtype=jnp.float32) * s, 'W_x': jax.random.normal(ks[2], (head, head), dtype=jnp.float32) * s, 'W_xa': jax.random.normal(ks[3], (head, head), dtype=jnp.float32) * s, 'W_out': jax.random.normal(ks[4], (dims, dims), dtype=jnp.float32) * s}
    _L1_attn_in = _L1_attn_setup()

    def _L1_ffn_setup():
        import jax, jax.numpy as jnp
        import numpy as np
        DIM = 128
        HIDDEN = 384
        SCALE = 1.0 / 127.0

        def _dequant(w_int, dtype):
            return w_int.astype(dtype) * jnp.asarray(SCALE, dtype)
        key = jax.random.key(seed)
        k_x, k_g, k_u, k_d = jax.random.split(key, 4)
        x = jax.random.normal(k_x, (4, 256, DIM), dtype=jnp.float32)
        w_gate = jax.random.randint(k_g, (HIDDEN, DIM), -127, 128, dtype=jnp.int32)
        w_up = jax.random.randint(k_u, (HIDDEN, DIM), -127, 128, dtype=jnp.int32)
        w_down = jax.random.randint(k_d, (DIM, HIDDEN), -127, 128, dtype=jnp.int32)
        return {'x': x, 'w_gate': w_gate, 'w_up': w_up, 'w_down': w_down}
    _L1_ffn_in = _L1_ffn_setup()
    _d = {'L0_attn_x': _L0_attn_in['x'], 'L0_attn_w_qkv': _L0_attn_in['w_qkv'], 'L0_attn_w_out': _L0_attn_in['w_out'], 'L0_attn_b_out': _L0_attn_in['b_out'], 'L0_ffn_W_fc': _L0_ffn_in['W_fc'], 'L0_ffn_ln_w': _L0_ffn_in['ln_w'], 'L0_ffn_ln_b': _L0_ffn_in['ln_b'], 'L0_ffn_W_proj': _L0_ffn_in['W_proj'], 'L1_attn_ln_g': _L1_attn_in['ln_g'], 'L1_attn_ln_b': _L1_attn_in['ln_b'], 'L1_attn_W_kv': _L1_attn_in['W_kv'], 'L1_attn_W_x': _L1_attn_in['W_x'], 'L1_attn_W_xa': _L1_attn_in['W_xa'], 'L1_attn_W_out': _L1_attn_in['W_out'], 'L1_ffn_w_gate': _L1_ffn_in['w_gate'], 'L1_ffn_w_up': _L1_ffn_in['w_up'], 'L1_ffn_w_down': _L1_ffn_in['w_down']}
    _x0 = _d['L0_attn_x']
    _d['L0_attn_x'] = jax.random.normal(jax.random.fold_in(jax.random.key(seed), 1), (32, 256, 128), dtype=_x0.dtype)
    del _x0
    return _d

def reference(L0_attn_x, L0_attn_w_qkv, L0_attn_w_out, L0_attn_b_out, L0_ffn_W_fc, L0_ffn_ln_w, L0_ffn_ln_b, L0_ffn_W_proj, L1_attn_ln_g, L1_attn_ln_b, L1_attn_W_kv, L1_attn_W_x, L1_attn_W_xa, L1_attn_W_out, L1_ffn_w_gate, L1_ffn_w_up, L1_ffn_w_down):

    def _L0_attn_ref(x, w_qkv, w_out, b_out):
        import jax, jax.numpy as jnp
        import numpy as np
        DIM = 128
        NUM_HEADS = 16
        HEAD_DIM = DIM // NUM_HEADS

        def _rope_tables(seq_len, dim, dtype):
            inv_freq = 1.0 / 10000.0 ** (jnp.arange(0, dim, 2, dtype=jnp.float32) / dim)
            t = jnp.arange(seq_len, dtype=jnp.float32)
            freqs = jnp.outer(t, inv_freq)
            return (jnp.cos(freqs).astype(dtype), jnp.sin(freqs).astype(dtype))

        def _apply_rope(x, cos_emb, sin_emb):
            x1 = x[..., 0::2]
            x2 = x[..., 1::2]
            return jnp.concatenate((x1 * cos_emb - x2 * sin_emb, x1 * sin_emb + x2 * cos_emb), axis=-1)
        B, S, D = x.shape
        H, hd = (NUM_HEADS, HEAD_DIM)
        qkv = jnp.einsum('bsd,ed->bse', x, w_qkv)
        q, k, v = jnp.split(qkv, 3, axis=-1)
        q, k, v = (t.reshape(B, S, H, hd).transpose(0, 2, 1, 3) for t in (q, k, v))
        cos_emb, sin_emb = _rope_tables(S, hd, x.dtype)
        q = _apply_rope(q, cos_emb, sin_emb)
        k = _apply_rope(k, cos_emb, sin_emb)
        scores = jnp.einsum('bhqd,bhkd->bhqk', q, k) / jnp.sqrt(jnp.asarray(hd, x.dtype))
        attn = jax.nn.softmax(scores, axis=-1)
        out = jnp.einsum('bhqk,bhkd->bhqd', attn, v)
        out = out.transpose(0, 2, 1, 3).reshape(B, S, D)
        return jnp.einsum('bsd,ed->bse', out, w_out) + b_out

    def _L0_ffn_ref(x, W_fc, ln_w, ln_b, W_proj):
        import jax, jax.numpy as jnp
        import numpy as np
        EPS = 1e-06
        LN_EPS = 1e-05

        def _absmean_core(W):
            gamma = jnp.mean(jnp.abs(W)) + EPS
            Ws = W / gamma
            Wq = jnp.sign(Ws) * jnp.minimum(jnp.round(jnp.abs(Ws)), 1.0)
            return (Wq, gamma)

        @jax.custom_vjp
        def absmean(W):
            return _absmean_core(W)[0]

        def _absmean_fwd(W):
            Wq, gamma = _absmean_core(W)
            return (Wq, gamma)

        def _absmean_bwd(gamma, g):
            return (g / gamma,)
        absmean.defvjp(_absmean_fwd, _absmean_bwd)

        def layernorm(x, w, b, eps=LN_EPS):
            mu = jnp.mean(x, axis=-1, keepdims=True)
            var = jnp.mean((x - mu) ** 2, axis=-1, keepdims=True)
            return (x - mu) * jax.lax.rsqrt(var + eps) * w + b
        h = jnp.einsum('btd,hd->bth', x, absmean(W_fc))
        h = jax.nn.gelu(h, approximate=False)
        h = layernorm(h, ln_w, ln_b)
        return jnp.einsum('bth,dh->btd', h, absmean(W_proj))

    def _L1_attn_ref(x, ln_g, ln_b, W_kv, W_x, W_xa, W_out):
        import jax, jax.numpy as jnp
        import numpy as np
        EPS = 1e-05

        def _layernorm(x, g, b):
            mu = jnp.mean(x, axis=-1, keepdims=True)
            var = jnp.mean(jnp.square(x - mu), axis=-1, keepdims=True)
            return (x - mu) * jax.lax.rsqrt(var + EPS) * g + b
        b, n, dims = x.shape
        head = W_x.shape[0]
        hd = dims // head
        h = _layernorm(x, ln_g, ln_b)
        kv = h @ W_kv
        qk, v = jnp.split(kv, 2, axis=-1)
        qk = qk.reshape(b, n, head, hd).transpose(0, 2, 1, 3)
        v = v.reshape(b, n, head, hd).transpose(0, 2, 1, 3)
        scores = jnp.einsum('bhqd,bhkd->bhqk', qk, qk)
        a1 = jax.nn.softmax(scores, axis=-1)
        a2 = jax.nn.softmax(scores, axis=-2)
        a1 = jnp.einsum('gh,bhqk->bgqk', W_x, a1)
        a2 = jnp.einsum('gh,bhqk->bgqk', W_xa, a2)
        o1 = jnp.einsum('bhij,bhjd->bhid', a1, v)
        _o2 = jnp.einsum('bhji,bhjd->bhid', a2, v)
        o1 = o1.transpose(0, 2, 1, 3).reshape(b, n, dims)
        return o1 @ W_out

    def _L1_ffn_ref(x, w_gate, w_up, w_down):
        import jax, jax.numpy as jnp
        import numpy as np
        DIM = 128
        HIDDEN = 384
        SCALE = 1.0 / 127.0

        def _dequant(w_int, dtype):
            return w_int.astype(dtype) * jnp.asarray(SCALE, dtype)
        wg = _dequant(w_gate, x.dtype)
        wu = _dequant(w_up, x.dtype)
        wd = _dequant(w_down, x.dtype)
        gate = jnp.einsum('bsd,hd->bsh', x, wg)
        up = jnp.einsum('bsd,hd->bsh', x, wu)
        h = jax.nn.silu(gate) * up
        return jnp.einsum('bsh,dh->bsd', h, wd)
    x = L0_attn_x
    x = _layernorm(x + _L0_attn_ref(x, L0_attn_w_qkv, L0_attn_w_out, L0_attn_b_out), axis=-1)
    x = _layernorm(x + _L0_ffn_ref(x, L0_ffn_W_fc, L0_ffn_ln_w, L0_ffn_ln_b, L0_ffn_W_proj), axis=-1)
    x = _layernorm(x + _L1_attn_ref(x, L1_attn_ln_g, L1_attn_ln_b, L1_attn_W_kv, L1_attn_W_x, L1_attn_W_xa, L1_attn_W_out), axis=-1)
    x = _layernorm(x + _L1_ffn_ref(x, L1_ffn_w_gate, L1_ffn_w_up, L1_ffn_w_down), axis=-1)
    return x

_drawn_inputs = setup_inputs


def setup_inputs(seed=0):
    import zlib

    import numpy as np

    out = dict(_drawn_inputs(seed))
    spreads = {'L0_ffn_ln_w': (1.0, 0.2),
     'L0_ffn_ln_b': (0.0, 0.1),
     'L1_attn_ln_g': (1.0, 0.6),
     'L1_attn_ln_b': (0.0, 0.8)}
    factors = {'L0_attn_b_out': 2.971, 'L1_attn_W_kv': 8.0, 'L1_attn_W_x': 8.0, 'L1_attn_W_out': 8.0}
    for name, (base, spread) in spreads.items():
        noise = np.random.default_rng([zlib.crc32(name.encode()), seed]).standard_normal(out[name].shape)
        drawn = base * np.exp(spread * noise) if base else spread * noise
        out[name] = jnp.asarray(drawn.astype(out[name].dtype))
    for name, factor in factors.items():
        out[name] = (out[name] * factor).astype(out[name].dtype)
    return out
```

```python
import numpy as np
import concourse.bass as bass
from concourse import mybir
from contextlib import ExitStack

FP32 = mybir.dt.float32
BF16 = mybir.dt.bfloat16
INT32 = mybir.dt.int32
ALU = mybir.AluOpType
ACT = mybir.ActivationFunctionType
AX = mybir.AxisListType

P = 128
D = 128
TOK = 256
TILES = TOK // P
HEADS = 16
HD = D // HEADS
PAIRS = HEADS // 2
BANK = 512
LN_EPS = 1e-5

K_PART = (0, 0, 0, 1, 1, 2)
Q_PART = (0, 1, 2, 0, 1, 0)
SLOTS = len(K_PART)
RUNS = ((0, 3), (3, 2), (5, 1))
HEAD_ROWS = SLOTS * HD
PAIR_ROWS = 2 * HEAD_ROWS
SHIFT_ROW = PAIR_ROWS
RING = 8
VW = 32


class Batch:

    def __init__(self, half, odd):
        self.half, self.odd = half, odd

    def plus(self, k):
        n = self.odd + k
        return Batch(self.half + n // 2 if n // 2 else self.half, n % 2)

    def number(self):
        return self.half * 2 + self.odd if self.odd else self.half * 2


def wait(eng, sem, count):
    if isinstance(count, int) and count <= 0:
        return
    eng.wait_ge(sem, count)


def wait_apart(eng, sem, count):
    if not isinstance(count, int):
        count = eng.to_reg(count)
        eng.wait_ge(sem, 1)
    wait(eng, sem, count)


def steps(eng, n, ahead, behind, step):
    def peeled(i):
        step(Batch(i // 2, i % 2), lambda k: 0 <= i + k < n)

    start = max(2, behind + behind % 2)
    end = start + (n - ahead - start) // 2 * 2
    for i in range(-ahead, start):
        peeled(i)
    with eng.Fori(start // 2, end // 2) as half:
        step(Batch(half, 0), lambda k: True)
        step(Batch(half, 1), lambda k: True)
    for i in range(end, n + behind):
        peeled(i)


def times(i, k, n):
    if isinstance(i.half, int):
        return max(0, min(n, 2 * i.half + i.odd + k + 1))
    assert i.odd + k + 1 > -2, "a loop's first step is 2 or later, and no wait is for less than one"
    return i.half * 2 + (i.odd + k + 1)


def rope_tables():
    inv = (1.0 / 10000.0 ** (np.arange(0, HD, 2, dtype=np.float32) / HD)).astype(np.float32)
    angle = np.outer(np.arange(TOK, dtype=np.float32), inv).astype(np.float32)
    table = np.zeros((2, HD, PAIRS, 2, TOK), np.float32)
    for d in range(HD):
        table[:, d, :, 0, :] = np.cos(angle[:, d // 2])
        table[:, d, :, 1, :] = np.sin(angle[:, d // 2]) * (1 if d % 2 else -1)
    return table.reshape(P, 2, TOK)


class Core:

    def __init__(self, nc, ctx, n):
        self.nc, self.ctx, self.n = nc, ctx, n
        sb = self.sb
        self.bank = [ctx.enter_context(nc.psum_tensor(f"bank{k}", [P, BANK], FP32)) for k in range(8)]
        self.x_all = sb("x_all", [P, n, TILES, D])
        self.xh_all = sb("xh_all", [P, n, TILES, D])
        self.ident = sb("ident", [P, P])
        self.ident_bf = sb("ident_bf", [P, P], BF16)
        self.w0_qk = sb("w0_qk", [P, 2, 2, D])
        self.w0_v = sb("w0_v", [P, D])
        self.w0_out = sb("w0_out", [P, D])
        self.b0_out = sb("b0_out", [P, D])
        self.rope = sb("rope", [P, 2, TOK])
        self.w0_fc = sb("w0_fc", [P, 4, D])
        self.w0_proj = sb("w0_proj", [P, 4, D])
        self.cols = sb("cols", [P, 10])
        self.w1_kv = sb("w1_kv", [P, 2, D])
        self.w1_qk = sb("w1_qk", [P, D])
        self.w1_out = sb("w1_out", [P, D])
        self.mix = sb("mix", [P, HEADS, D])
        self.w1_gate = sb("w1_gate", [P, 3, D])
        self.w1_up = sb("w1_up", [P, 3, D])
        self.w1_down = sb("w1_down", [P, 3, D])
        self.zeros = sb("zeros", [P, TOK])
        self.eps = sb("eps", [P, 2])
        self.minus_half = sb("minus_half", [P, 2])
        self.k_stack = [sb(f"k_stack{k}", [P, PAIRS, TOK], BF16) for k in range(2)]
        self.q_stack = [sb(f"q_stack{k}", [P, 2, PAIRS, TOK], BF16) for k in range(2)]

    def sb(self, name, shape, dt=FP32):
        return self.ctx.enter_context(self.nc.sbuf_tensor(name, shape, dt))

    def sem(self, name):
        return self.ctx.enter_context(self.nc.semaphore(name))


def prepare(nc, core, w):
    bank = core.bank
    with ExitStack() as ctx:
        def sb(name, shape, dt=FP32):
            return ctx.enter_context(nc.sbuf_tensor(name, shape, dt))

        def sem(name):
            return core.sem(name)

        raw_qkv = sb("raw_qkv", [P, 3, D])
        raw_out = sb("raw_out", [P, D])
        raw_rows = sb("raw_rows", [10, D])
        raw_mix = sb("raw_mix", [1, HEADS * HEADS])
        raw_bias = sb("raw_bias", [1, D])
        raw_fc = sb("raw_fc", [P, 4, D])
        raw_proj = sb("raw_proj", [P, 4, D])
        raw_int = sb("raw_int", [P, 3, 3, D], INT32)
        scaled = sb("scaled", [P, 3, 3, D])
        ternary = sb("ternary", [P, 2, 4, D])
        below = sb("below", [P, 2, 4, D])
        ones = sb("ones", [P, P])
        totals = sb("totals", [P, 2])
        gamma = sb("gamma", [P, 2])
        bounds = sb("bounds", [P, 2, 2])

        load_attn = sem("load_attn")
        load_ffn0 = sem("load_ffn0")
        load_ffn1 = sem("load_ffn1")
        load_rest = sem("load_rest")
        ident_step = sem("ident_step")
        ident_bf_ready = sem("ident_bf_ready")
        stacks_zero = sem("stacks_zero")
        consts_ready = sem("consts_ready")
        sums_ready = sem("sums_ready")
        gamma_total = sem("gamma_total")
        gamma_step = sem("gamma_step")
        below_ready = sem("below_ready")
        ternary_ready = sem("ternary_ready")
        scaled_ready = sem("scaled_ready")
        attn_turned = sem("attn_turned")
        small_turned = sem("small_turned")
        ffn0_turned = sem("ffn0_turned")
        ffn1_turned = sem("ffn1_turned")

        with nc.Block() as block:
            @block.sync
            def _(sp):
                sp.dma_start(raw_qkv[:, :, :], w["w_qkv"].rearrange("(t e) d -> e t d", e=D)).then_inc(load_attn, 16)
                sp.dma_start(raw_out[:, :], w["w_out0"]).then_inc(load_attn, 16)
                sp.dma_start(raw_fc[:, :, :], w["w_fc"].rearrange("(c p) d -> p c d", p=P)).then_inc(load_ffn0, 16)
                sp.dma_start(raw_proj[:, :, :], w["w_proj"].rearrange("p (c d) -> p c d", c=4)).then_inc(load_ffn0, 16)
                sp.dma_start(core.rope[:, :, :], w["rope"]).then_inc(load_rest, 16)
                sp.dma_start(core.w1_kv[:, :, :], w["w_kv"].rearrange("p (t e) -> p t e", t=2)).then_inc(load_rest, 16)
                sp.dma_start(core.w1_out[:, :], w["w_out1"]).then_inc(load_rest, 16)

            @block.scalar
            def _(act):
                act.dma_start(raw_rows[0:4, :], w["ln_w"].rearrange("(c p) -> c p", p=P)).then_inc(load_rest, 16)
                act.dma_start(raw_rows[4:8, :], w["ln_b"].rearrange("(c p) -> c p", p=P)).then_inc(load_rest, 16)
                act.dma_start(raw_rows[8:9, :], w["ln_g1"].rearrange("(a p) -> a p", a=1)).then_inc(load_rest, 16)
                act.dma_start(raw_rows[9:10, :], w["ln_b1"].rearrange("(a p) -> a p", a=1)).then_inc(load_rest, 16)
                act.dma_start(raw_mix[:, :], w["w_x"].rearrange("(a g) h -> a (g h)", a=1)).then_inc(load_rest, 16)
                act.dma_start(raw_bias[:, :], w["b_out"].rearrange("(a p) -> a p", a=1)).then_inc(load_rest, 16)
                act.dma_start(raw_int[:, 0, :, :], w["w_gate"].rearrange("(c p) d -> p c d", p=P)).then_inc(load_ffn1, 16)
                act.dma_start(raw_int[:, 1, :, :], w["w_up"].rearrange("(c p) d -> p c d", p=P)).then_inc(load_ffn1, 16)
                act.dma_start(raw_int[:, 2, :, :], w["w_down"].rearrange("p (c d) -> p c d", c=3)).then_inc(load_ffn1, 16)

            @block.gpsimd
            def _(pool):
                pool.memset(core.ident[:, :], 0.0).then_inc(ident_step, 1)
                pool.wait_ge(ident_step, 1)
                pool.affine_select(out=core.ident[:, :], in_=core.ident[:, :], compare_op=ALU.not_equal, fill=1.0,
                                   base=0, pattern=[[-1, P]], channel_multiplier=1).then_inc(ident_step, 1)

            @block.vector
            def _(dve):
                dve.memset(ones[:, :], 1.0).then_inc(consts_ready, 1)
                dve.memset(core.zeros[:, :], 0.0)
                dve.memset(core.eps[:, :], LN_EPS)
                dve.memset(core.minus_half[:, :], -0.5)
                for stack in core.q_stack:
                    dve.memset(stack[:, :, :, :], 0.0).then_inc(stacks_zero, 1)
                for k, stack in enumerate(core.k_stack):
                    dve.memset(stack[:, :, :], 0.0).then_inc(stacks_zero, 1)
                    dve.wait_ge(stacks_zero, 3 + k)
                    dve.memset(stack[SHIFT_ROW:SHIFT_ROW + 1, :, :], 1.0)
                dve.wait_ge(ident_step, 2)
                dve.tensor_copy(core.ident_bf[:, :], core.ident[:, :])
                dve.wait_ge(load_ffn0, 32)
                for k, raw in enumerate((raw_fc, raw_proj)):
                    dve.tensor_reduce(totals[:, k:k + 1], raw[:, :, :], op=ALU.add, axis=AX.XY,
                                      apply_absolute_value=True).then_inc(sums_ready, 1)
                dve.wait_ge(gamma_total, 1)
                dve.tensor_scalar(gamma[:, :], bank[7][:, 0:2], 1.0 / (4 * P * D), 1e-6,
                                  ALU.mult, ALU.add).then_inc(gamma_step, 1)
                dve.wait_ge(gamma_step, 1)
                dve.tensor_scalar(bounds[:, 0, :], gamma[:, :], 0.5, None, ALU.mult).then_inc(gamma_step, 1)
                dve.tensor_scalar(bounds[:, 1, :], gamma[:, :], -0.5, None, ALU.mult).then_inc(gamma_step, 1)
                dve.wait_ge(gamma_step, 3)
                for k, raw in enumerate((raw_fc, raw_proj)):
                    dve.tensor_scalar(below[:, k, :, :], raw[:, :, :], bounds[:, 1, k:k + 1], None,
                                      ALU.is_lt).then_inc(below_ready, 1)
                for k, raw in enumerate((raw_fc, raw_proj)):
                    dve.wait_ge(below_ready, k + 1)
                    dve.scalar_tensor_tensor(ternary[:, k, :, :].rearrange("p c d -> p (c d)"),
                                             raw[:, :, :].rearrange("p c d -> p (c d)"), bounds[:, 0, k:k + 1],
                                             below[:, k, :, :].rearrange("p c d -> p (c d)"),
                                             op0=ALU.is_gt, op1=ALU.subtract).then_inc(ternary_ready, 1)
                dve.wait_ge(load_ffn1, 48)
                dve.tensor_scalar(scaled[:, :, :, :].rearrange("p a c d -> p (a c d)"),
                                  raw_int[:, :, :, :].rearrange("p a c d -> p (a c d)"), float(np.float32(1.0 / 127.0)), None,
                                  ALU.mult).then_inc(scaled_ready, 1)
                dve.wait_ge(attn_turned, 1)
                for side in range(2):
                    turned = bank[0][:, side * D:(side + 1) * D].rearrange("p (r a d) -> p a d r", a=2, d=HD)
                    dve.tensor_copy(core.w0_qk[:, side, 0, :].rearrange("p (a d r) -> p a d r", a=2, d=HD), turned)
                    swapped = core.w0_qk[:, side, 1, :].rearrange("p (a c t r) -> p a c t r", a=2, c=HD // 2, t=2)
                    source = bank[0][:, side * D:(side + 1) * D].rearrange("p (r a c t) -> p a c t r", a=2, c=HD // 2, t=2)
                    for t in range(2):
                        dve.tensor_copy(swapped[:, :, :, t, :], source[:, :, :, 1 - t, :])
                dve.tensor_copy(core.w0_v[:, :], bank[0][:, 2 * D:3 * D])
                dve.tensor_copy(core.w0_out[:, :], bank[0][:, 3 * D:4 * D])
                dve.wait_ge(small_turned, 1)
                dve.tensor_copy(core.cols[:, :], bank[1][:, 0:10])
                dve.tensor_copy(core.b0_out[:, :], bank[1][:, 384:512])
                mixed = bank[1][:, 128:384].rearrange("p (g h) -> p h g", h=HEADS)
                for d in range(HD):
                    dve.tensor_copy(core.mix[:, :, :].rearrange("p h (g d) -> p h g d", d=HD)[:, :, :, d], mixed)
                dve.wait_ge(load_rest, 16 * 9)
                dve.tensor_copy(core.w1_qk[:, :].rearrange("p (a d r) -> p a d r", a=2, d=HD),
                                core.w1_kv[:, 0, :].rearrange("p (r a d) -> p a d r", a=2, d=HD))
                dve.wait_ge(ffn0_turned, 2)
                dve.tensor_copy(core.w0_fc[:, :, :].rearrange("p c d -> p (c d)"), bank[2][:, :])
                dve.tensor_copy(core.w0_proj[:, :, :].rearrange("p c d -> p (c d)"), bank[3][:, :])
                dve.wait_ge(ffn1_turned, 1)
                for k, to in enumerate((core.w1_gate, core.w1_up, core.w1_down)):
                    dve.tensor_copy(to[:, :, :].rearrange("p c d -> p (c d)"), bank[4 + k][:, 0:3 * D])

            @block.tensor
            def _(pe):
                pe.wait_ge(ident_step, 2)
                pe.wait_ge(load_attn, 32)
                for t in range(3):
                    pe.transpose(bank[0][:, t * D:(t + 1) * D], raw_qkv[:, t, :], core.ident[:, :])
                pe.transpose(bank[0][:, 3 * D:4 * D], raw_out[:, :], core.ident[:, :]).then_inc(attn_turned, 1)
                pe.wait_ge(consts_ready, 1)
                pe.wait_ge(load_rest, 16 * 9)
                pe.transpose(bank[1][:, 0:10], raw_rows[:, :], core.ident[0:10, 0:10])
                pe.matmul(bank[1][:, 128:384], ones[0:1, :], raw_mix[:, :], start=True, stop=True)
                pe.matmul(bank[1][:, 384:512], ones[0:1, :], raw_bias[:, :], start=True, stop=True).then_inc(small_turned, 1)
                pe.wait_ge(sums_ready, 2)
                pe.matmul(bank[7][:, 0:2], ones[:, :], totals[:, :], start=True, stop=True).then_inc(gamma_total, 1)
                for k in range(2):
                    pe.wait_ge(ternary_ready, k + 1)
                    for c in range(4):
                        last = pe.transpose(bank[2 + k][:, c * D:(c + 1) * D], ternary[:, k, c, :], core.ident[:, :])
                    last.then_inc(ffn0_turned, 1)
                pe.wait_ge(scaled_ready, 1)
                for k in range(3):
                    for c in range(3):
                        last = pe.transpose(bank[4 + k][:, c * D:(c + 1) * D], scaled[:, k, c, :], core.ident[:, :])
                last.then_inc(ffn1_turned, 1)


def attention(nc, core, layer, x_dram, scratch):
    n = core.n
    first = layer == 0
    sides = 2 if first else 1
    scale = float(1.0 / np.sqrt(np.float32(HD))) if first else 1.0
    half_heads = HEADS // 2
    s1 = core.bank[0:2]
    s2 = core.bank[2:4]
    pv = core.bank[4:6]
    m0, m1 = core.bank[6], core.bank[7]
    groups = HEADS // 4

    with ExitStack() as ctx:
        def sb(name, shape, dt=FP32):
            return ctx.enter_context(nc.sbuf_tensor(f"{name}_{layer}", shape, dt))

        def sem(name):
            return core.sem(f"{name}_{layer}")

        x_in = [sb(f"x_in{k}", [P, TILES, D]) for k in range(2)]
        x_res = [sb(f"x_res{k}", [P, TILES, D]) for k in range(2)]
        x_t = [sb(f"x_t{k}", [P, TOK]) for k in range(2)]
        turned = sb("turned", [P, sides, 2, TOK])
        exact = sb("exact", [P, sides, TOK])
        rest = sb("rest", [P, sides, TOK])
        parts = sb("parts", [P, 3, sides, TOK], BF16)
        shifts = sb("shifts", [P, TILES, 2, half_heads], BF16)
        shift_rows = [sb(f"shift_rows{k}", [half_heads, TOK], BF16) for k in range(2)]
        probs = sb("probs", [P, RING, TILES, TOK])
        added = [sb(f"added{k}", [P, TILES, D]) for k in range(2)]
        y = sb("y", [P, TILES, D])
        stats = sb("stats", [P, TILES, 6])
        moments = sb("moments", [P, TILES, 2])
        shifted_var = sb("shifted_var", [P, TILES])
        rstd = sb("rstd", [P, TILES])
        x_out = sb("x_out", [P, TILES, D])
        o_t = sb("o_t", [P, TOK])
        if first:
            values = [sb(f"values{k}", [P, TILES, HEADS, VW]) for k in range(2)]
            heads_t = [sb(f"heads_t{k}", [P, groups, TOK]) for k in range(2)]
            recips = sb("recips", [P, 2, TILES, half_heads])
            o = sb("o", [P, TILES, D])
        else:
            v_in = sb("v_in", [P, TILES, D])
            values = [sb(f"values{k}", [P, TILES, HEADS, D + 1]) for k in range(2)]
            recips = sb("recips", [P, 2, TILES])
            o_sum = [sb(f"o_sum{k}", [P, TILES, D]) for k in range(2)]

        ones_ready = sem("ones_ready")
        x_loaded = [sem(f"x_loaded{k}") for k in range(2)]
        res_loaded = [sem(f"res_loaded{k}") for k in range(2)]
        xt_in_psum = sem("xt_in_psum")
        xt_ready = sem("xt_ready")
        qk_in_psum = sem("qk_in_psum")
        qk_taken = sem("qk_taken")
        exact_ready = sem("exact_ready")
        part0_ready = sem("part0_ready")
        rest_ready = sem("rest_ready")
        part1_ready = sem("part1_ready")
        var_ready = sem("var_ready")
        parts_ready = sem("parts_ready")
        parts_written = sem("parts_written")
        stacked = [sem(f"stacked{k}") for k in range(2)]
        v_in_psum = sem("v_in_psum")
        v_taken = sem("v_taken")
        values_ready = sem("values_ready")
        max_in_psum = sem("max_in_psum")
        max_done = sem("max_done")
        shifts_in_psum = sem("shifts_in_psum")
        shift_rows_ready = sem("shift_rows_ready")
        shifted = [sem(f"shifted{k}") for k in range(2)]
        s_in_psum = sem("s_in_psum")
        exp_done = sem("exp_done")
        pv_done = sem("pv_done")
        pv_taken = sem("pv_taken")
        heads_in_psum = sem("heads_in_psum")
        recips_ready = sem("recips_ready")
        o_ready = sem("o_ready")
        ot_in_psum = sem("ot_in_psum")
        ot_ready = sem("ot_ready")
        out_in_psum = sem("out_in_psum")
        added_ready = sem("added_ready")
        y_ready = sem("y_ready")
        stats_ready = sem("stats_ready")
        moments_ready = sem("moments_ready")
        rstd_ready = sem("rstd_ready")
        x_out_ready = sem("x_out_ready")
        x_stored = sem("x_stored")

        def stack_rows(parity):
            return slice(parity * HEAD_ROWS, (parity + 1) * HEAD_ROWS)

        with nc.Block() as block:
            @block.sync
            def _(sp):
                source = x_dram.rearrange("b (t p) d -> b p t d", p=P) if first else None

                def step(i, on):
                    b = i.plus(3)
                    if on(3):
                        wait_apart(sp, xt_in_psum, times(i, 1, n))
                        src = source[b.number(), :, :, :] if first else core.xh_all[:, b.number(), :, :]
                        sp.dma_start(x_in[b.odd][:, :, :], src).then_inc(x_loaded[b.odd], 16)
                    b = i
                    if on(0):
                        wait_apart(sp, added_ready, times(i, -2, n))
                        src = source[b.number(), :, :, :] if first else core.x_all[:, b.number(), :, :]
                        sp.dma_start(x_res[b.odd][:, :, :], src).then_inc(res_loaded[b.odd], 16)
                    b = i.plus(2)
                    if on(2):
                        wait_apart(sp, parts_ready, times(i, 2, n))
                        wait_apart(sp, stacked[0], times(i, 1, n) * 64)
                        wait_apart(sp, stacked[1], times(i, 1, n) * 64)
                        for s, m in RUNS:
                            k = K_PART[s]
                            src = parts[:, k:k + 1, sides - 1, :]
                            if m > 1:
                                src = src.broadcast_to([P, m, TOK])
                            sp.dma_start(scratch[0, s:s + m, :, :].rearrange("s r n -> r s n"), src).then_inc(parts_written, 16)
                            sp.dma_start(scratch[1, s:s + m, :, :].rearrange("s r n -> r s n"),
                                         parts[:, Q_PART[s]:Q_PART[s] + m, 0, :]).then_inc(parts_written, 16)
                        wait_apart(sp, parts_written, times(i, 2, n) * (32 * len(RUNS)))
                        for hf in range(2):
                            if on(0):
                                wait_apart(sp, s_in_psum, i.number() * HEADS + half_heads * (hf + 1))
                            prs = slice(4 * hf, 4 * hf + 4)
                            for parity in range(2):
                                for side, to in ((0, core.k_stack[b.odd][stack_rows(parity), prs, :]),
                                                 (1, core.q_stack[b.odd][stack_rows(parity), parity, prs, :])):
                                    src = scratch[side, :, parity * 64:(parity + 1) * 64, :].rearrange(
                                        "s (d r) n -> s d r n", r=PAIRS)[:, :, prs, :].rearrange("s d r n -> s d (r n)")
                                    sp.dma_start(to.rearrange("q r n -> q (r n)"), src).then_inc(stacked[hf], 16)
                    b = i.plus(-1)
                    if on(-1):
                        wait_apart(sp, x_out_ready, times(i, -1, n) * TILES)
                        sp.dma_start(core.x_all[:, b.number(), :, :], x_out[:, :, :]).then_inc(x_stored, 16)

                steps(sp, n, 3, 1, step)
                sp.wait_ge(x_stored, 16 * n)

            @block.gpsimd
            def _(pool):
                def step(i, on):
                    b = i.plus(-1)
                    if on(-1):
                        pool.wait_ge(res_loaded[b.odd], (b.half + 1) * 16)
                        wait(pool, y_ready, times(i, -2, n))
                        bias = core.b0_out[:, :] if first else core.zeros[:, 0:D]
                        pool.tensor_tensor(added[b.odd][:, :, :], x_res[b.odd][:, :, :],
                                           bias.unsqueeze(1).broadcast_to([P, TILES, D]), op=ALU.add).then_inc(added_ready, 1)
                    if on(2):
                        split(i)
                    if not first and on(1):
                        b = i.plus(1)
                        pool.wait_ge(v_taken, times(i, 1, n))
                        wait(pool, pv_done, times(i, -1, n) * HEADS)
                        for t in range(TILES):
                            pool.tensor_tensor(values[b.odd][:, t, :, 0:D], core.mix[:, :, :],
                                               v_in[:, t, :].unsqueeze(1).broadcast_to([P, HEADS, D]),
                                               op=ALU.mult).then_inc(values_ready, 1)
                    if on(-1):
                        pool.wait_ge(moments_ready, times(i, -1, n) * TILES)
                        pool.tensor_tensor(shifted_var[:, :], moments[:, :, 1], core.eps[:, :], op=ALU.add).then_inc(var_ready, 1)
                        pool.wait_ge(var_ready, times(i, -1, n))
                        pool.tensor_tensor(rstd[:, :], shifted_var[:, :], core.minus_half[:, :], op=ALU.pow).then_inc(rstd_ready, 1)

                def split(i):
                    zeros = core.zeros[:, :].unsqueeze(1).broadcast_to([P, sides, TOK])
                    pool.wait_ge(qk_taken, times(i, 2, n) * sides)
                    if first:
                        pool.tensor_tensor(exact[:, :, :], turned[:, :, 0, :], turned[:, :, 1, :], op=ALU.add).then_inc(exact_ready, 1)
                        pool.wait_ge(exact_ready, times(i, 2, n))
                    wait(pool, parts_written, times(i, 1, n) * (32 * len(RUNS)))
                    pool.tensor_tensor(parts[:, 0, :, :], exact[:, :, :], zeros, op=ALU.add).then_inc(part0_ready, 1)
                    pool.wait_ge(part0_ready, times(i, 2, n))
                    pool.tensor_tensor(rest[:, :, :], exact[:, :, :], parts[:, 0, :, :], op=ALU.subtract).then_inc(rest_ready, 1)
                    pool.wait_ge(rest_ready, times(i, 2, n))
                    pool.tensor_tensor(parts[:, 1, :, :], rest[:, :, :], zeros, op=ALU.add).then_inc(part1_ready, 1)
                    pool.wait_ge(part1_ready, times(i, 2, n))
                    pool.tensor_tensor(parts[:, 2, :, :], rest[:, :, :], parts[:, 1, :, :], op=ALU.subtract).then_inc(parts_ready, 1)

                steps(pool, n, 2, 1, step)

            @block.scalar
            def _(act):
                def shift_rows_out(b, hf):
                    act.wait_ge(shifts_in_psum, b.number() * 2 + (hf + 1))
                    wait(act, shifted[hf], b.number() * 32)
                    act.activation(shift_rows[hf][:, :], m0[:, :].bitcast(BF16)[0:half_heads, 0:TOK], ACT.Copy).then_inc(shift_rows_ready, 1)
                    act.wait_ge(shift_rows_ready, b.number() * 2 + (hf + 1))
                    for parity in range(2):
                        act.dma_start(core.q_stack[b.odd][SHIFT_ROW:SHIFT_ROW + 1, parity, 4 * hf:4 * hf + 4, :].rearrange("q r n -> q (r n)"),
                                      shift_rows[hf][4 * parity:4 * parity + 4, :]).then_inc(shifted[hf], 16)

                def take_heads(b, g):
                    act.wait_ge(pv_done, b.number() * groups + (g + 1))
                    act.activation(heads_t[b.odd][:, g, :], pv[g % 2][:, 0:TOK], ACT.Copy).then_inc(pv_taken, 1)

                def step(i, on):
                    for s in range(HEADS):
                        if s == 0 and on(2):
                            b = i.plus(2)
                            act.wait_ge(xt_in_psum, times(i, 2, n))
                            if first:
                                act.activation(x_t[b.odd][:, :], m1[:, 0:TOK], ACT.Copy).then_inc(xt_ready, 1)
                            else:
                                act.activation(x_t[b.odd][:, :], m1[:, 0:TOK], ACT.Identity, scale=core.cols[:, 8:9],
                                               bias=core.cols[:, 9:10]).then_inc(xt_ready, 1)
                        if s == 2 and on(0):
                            shift_rows_out(i, 1)
                        if s == 2 and first and on(-1):
                            take_heads(i.plus(-1), 3)
                        if s in (6, 10, 14) and first and on(0):
                            take_heads(i, (s - 6) // 4)
                        if s == 5 and on(1):
                            b = i.plus(1)
                            act.wait_ge(v_in_psum, times(i, 1, n))
                            if first:
                                wait(act, pv_done, times(i, -1, n) * groups)
                                act.activation(values[b.odd][:, :, :, 0:HD],
                                               m1[:, 0:TOK].rearrange("p (t h d) -> p t h d", t=TILES, d=HD),
                                               ACT.Copy).then_inc(v_taken, 1)
                            else:
                                wait(act, values_ready, times(i, 0, n) * TILES)
                                act.activation(v_in[:, :, :].rearrange("p t d -> p (t d)"), m1[:, 0:TOK], ACT.Copy).then_inc(v_taken, 1)
                        if s == (10 if first else 7) and on(-1):
                            act.wait_ge(ot_in_psum, times(i, -1, n))
                            act.activation(o_t[:, :], m1[:, 0:TOK], ACT.Copy).then_inc(ot_ready, 1)
                        if s == 11 and on(1):
                            shift_rows_out(i.plus(1), 0)
                        if on(0):
                            act.wait_ge(s_in_psum, i.number() * HEADS + (s + 1))
                            if first and s % 4 == 0:
                                wait(act, pv_done, i.number() * groups + (s // 4 - 1))
                            if not first:
                                wait(act, pv_done, i.number() * HEADS + (s + 1 - RING))
                            act.activation(probs[:, s % RING, :, :].rearrange("p t n -> p (t n)"), s2[s % 2][:, :], ACT.Exp,
                                           scale=scale).then_inc(exp_done, 1)

                steps(act, n, 2, 1, step)

            @block.vector
            def _(dve):
                def sum_head(b, h):
                    dve.wait_ge(recips_ready, b.number() * HEADS + (h + 1))
                    wait(dve, pv_taken, (b.number() * HEADS + h) * TILES)
                    for t in range(TILES):
                        part = pv[h % 2][:, t * (D + 1):t * (D + 1) + D]
                        if h == 0:
                            dve.tensor_scalar(o_sum[b.odd][:, t, :], part, recips[:, h % 2, t:t + 1], None,
                                              ALU.mult).then_inc(pv_taken, 1)
                        else:
                            dve.scalar_tensor_tensor(o_sum[b.odd][:, t, :], part, recips[:, h % 2, t:t + 1],
                                                     o_sum[b.odd][:, t, :], op0=ALU.mult, op1=ALU.add).then_inc(pv_taken, 1)

                def recip_head(b, h):
                    dve.wait_ge(pv_done, b.number() * HEADS + (h + 1))
                    sums = pv[h % 2][:, 0:TILES * (D + 1)].rearrange("p (t c) -> p t c", t=TILES)[:, :, D]
                    dve.reciprocal(recips[:, h % 2, :], sums).then_inc(recips_ready, 1)

                def step(i, on):
                    for s in range(HEADS):
                        lagged, h = (i, s - 3) if s >= 3 else (i.plus(-1), s + HEADS - 3)
                        summing = not first and (on(0) if s >= 3 else on(-1))
                        if summing:
                            recip_head(lagged, h)
                        if on(1):
                            b = i.plus(1)
                            hf, col = s // half_heads, s % 2 * 4 + s // 2 % 4
                            dve.wait_ge(max_in_psum, b.number() * HEADS + (s + 1))
                            dve.tensor_reduce(shifts[:, :, hf, col], s1[s % 2][:, :].rearrange("p (t n) -> p t n", t=TILES),
                                              op=ALU.max, axis=AX.X, negate=True).then_inc(max_done, 1)
                        if summing:
                            sum_head(lagged, h)
                        if first and s in (2, 3) and on(2):
                            side = s - 2
                            dve.wait_ge(qk_in_psum, times(i, 1, n) * 2 + (side + 1))
                            wait(dve, exact_ready, times(i, 1, n))
                            dve.tensor_tensor(turned[:, side, :, :], (m1, m0)[side][:, :].rearrange("p (v n) -> p v n", v=2),
                                              core.rope[:, :, :], op=ALU.mult).then_inc(qk_taken, 1)
                        if not first and s == 2 and on(2):
                            dve.wait_ge(qk_in_psum, times(i, 2, n))
                            wait(dve, rest_ready, times(i, 1, n))
                            dve.tensor_copy(exact[:, 0, :], m1[:, 0:TOK]).then_inc(qk_taken, 1)
                        if first and s == 7 and on(-1):
                            for k, m in enumerate((m0, m1)):
                                heads = m[:, :].rearrange("p (t h c) -> p t h c", t=TILES, c=VW)
                                dve.wait_ge(heads_in_psum, times(i, -2, n) * 2 + (k + 1))
                                dve.reciprocal(recips[:, k, :, :], heads[:, :, :, HD]).then_inc(recips_ready, 1)
                            for k, m in enumerate((m0, m1)):
                                heads = m[:, :].rearrange("p (t h c) -> p t h c", t=TILES, c=VW)
                                dve.wait_ge(recips_ready, times(i, -2, n) * 2 + (k + 1))
                                dve.tensor_tensor(o[:, :, k * 64:(k + 1) * 64].rearrange("p t (h d) -> p t h d", d=HD),
                                                  heads[:, :, :, 0:HD],
                                                  recips[:, k, :, :].unsqueeze(3).broadcast_to([P, TILES, half_heads, HD]),
                                                  op=ALU.mult).then_inc(o_ready, 1)
                        if s == (13 if first else 10) and on(-1):
                            b = i.plus(-1)
                            wait(dve, x_out_ready, times(i, -2, n) * TILES)
                            dve.wait_ge(out_in_psum, times(i, -1, n))
                            dve.wait_ge(added_ready, times(i, -1, n))
                            dve.tensor_tensor(y[:, :, :].rearrange("p t d -> p (t d)"), m1[:, 0:TOK],
                                              added[b.odd][:, :, :].rearrange("p t d -> p (t d)"), op=ALU.add).then_inc(y_ready, 1)
                            wait_apart(dve, y_ready, times(i, -1, n))
                            for t in range(TILES):
                                dve.bn_stats(stats[:, t, :], y[:, t, :]).then_inc(stats_ready, 1)
                            wait_apart(dve, var_ready, times(i, -2, n))
                            wait_apart(dve, stats_ready, times(i, -1, n) * TILES)
                            for t in range(TILES):
                                dve.bn_aggr(moments[:, t, :], stats[:, t, :]).then_inc(moments_ready, 1)
                    if on(-1):
                        dve.wait_ge(rstd_ready, times(i, -1, n))
                        dve.wait_ge(moments_ready, times(i, -1, n) * TILES)
                        wait(dve, x_stored, times(i, -2, n) * 16)
                        for t in range(TILES):
                            dve.tensor_scalar(x_out[:, t, :], y[:, t, :], moments[:, t, 0:1], rstd[:, t:t + 1],
                                              ALU.subtract, ALU.mult).then_inc(x_out_ready, 1)

                for v in values:
                    if first:
                        dve.memset(v[:, :, :, HD:VW], 0.0).then_inc(ones_ready, 1)
                    else:
                        dve.memset(v[:, :, :, D:D + 1], 1.0).then_inc(ones_ready, 1)
                if first:
                    for k, v in enumerate(values):
                        dve.wait_ge(ones_ready, k + 1)
                        dve.memset(v[:, :, :, HD:HD + 1], 1.0).then_inc(ones_ready, 1)
                steps(dve, n, 2, 1, step)

            @block.tensor
            def _(pe):
                def shifts_turned(b, hf):
                    pe.wait_ge(max_done, b.number() * HEADS + half_heads * (hf + 1))
                    for t in range(TILES):
                        last = pe.transpose(m0[:, :].bitcast(BF16)[0:half_heads, t * P:(t + 1) * P], shifts[:, t, hf, :],
                                            core.ident_bf[:, :])
                    last.then_inc(shifts_in_psum, 1)

                def products_by_group(b, g):
                    if g == 0:
                        pe.wait_ge(v_taken, b.number() + 1)
                    pe.wait_ge(exp_done, b.number() * HEADS + 4 * (g + 1))
                    wait(pe, pv_taken, b.number() * groups + (g - 1))
                    for t in range(TILES):
                        for a in range(4):
                            h = 4 * g + a
                            last = pe.matmul(pv[g % 2][VW * a:VW * (a + 1), 0:TOK], values[b.odd][:, t, h, :],
                                             probs[:, h % RING, t, :], start=(t == 0), stop=(t == TILES - 1),
                                             skip_group_check=True)
                    last.then_inc(pv_done, 1)

                def products_of_head(b, h):
                    if h == 0:
                        pe.wait_ge(values_ready, b.number() * TILES + TILES)
                    pe.wait_ge(exp_done, b.number() * HEADS + (h + 1))
                    wait(pe, pv_taken, (b.number() * HEADS + (h - 1)) * TILES)
                    for q in range(TILES):
                        for t in range(TILES):
                            last = pe.matmul(pv[h % 2][:, q * (D + 1):(q + 1) * (D + 1)], probs[:, h % RING, t, q * P:(q + 1) * P],
                                             values[b.odd][:, t, h, :], start=(t == 0), stop=(t == TILES - 1))
                    last.then_inc(pv_done, 1)

                def step(i, on):
                    for s in range(HEADS):
                        if s == 0 and on(2):
                            b = i.plus(2)
                            pe.wait_ge(x_loaded[b.odd], (b.half + 1) * 16)
                            wait(pe, y_ready, times(i, -2, n))
                            wait(pe, qk_taken, times(i, 1, n) * sides)
                            wait(pe, v_taken, times(i, 0, n))
                            for t in range(TILES):
                                last = pe.transpose(m1[:, t * P:(t + 1) * P], x_in[b.odd][:, t, :], core.ident[:, :])
                            last.then_inc(xt_in_psum, 1)
                        if s == 1 and on(-1):
                            if first:
                                products_by_group(i.plus(-1), 3)
                        if s == 1 and on(0):
                            pe.wait_ge(shift_rows_ready, i.number() * 2 + 1)
                            shifts_turned(i, 1)
                        if s == 1 and on(2):
                            b = i.plus(2)
                            pe.wait_ge(xt_ready, times(i, 2, n))
                            if first:
                                for v in range(2):
                                    last = pe.matmul(m1[:, v * TOK:(v + 1) * TOK], core.w0_qk[:, 0, v, :], x_t[b.odd][:, :],
                                                     start=True, stop=True)
                            else:
                                last = pe.matmul(m1[:, 0:TOK], core.w1_qk[:, :], x_t[b.odd][:, :], start=True, stop=True)
                            last.then_inc(qk_in_psum, 1)
                        if first and s == 2 and on(2):
                            b = i.plus(2)
                            wait(pe, shift_rows_ready, times(i, 0, n) * 2)
                            wait(pe, qk_taken, times(i, 1, n) * 2)
                            for v in range(2):
                                last = pe.matmul(m0[:, v * TOK:(v + 1) * TOK], core.w0_qk[:, 1, v, :], x_t[b.odd][:, :],
                                                 start=True, stop=True)
                            last.then_inc(qk_in_psum, 1)
                        if s == 4 and on(1):
                            b = i.plus(1)
                            wait(pe, qk_taken, times(i, 2, n) * sides - (sides - 1) if on(2) else times(i, 2, n) * sides)
                            wait(pe, y_ready, times(i, -2, n))
                            w_v = core.w0_v[:, :] if first else core.w1_kv[:, 1, :]
                            for t in range(TILES):
                                last = pe.matmul(m1[:, t * P:(t + 1) * P], x_t[b.odd][:, t * P:(t + 1) * P], w_v,
                                                 start=True, stop=True)
                            last.then_inc(v_in_psum, 1)
                        if first and s == 6 and on(-1):
                            b = i.plus(-1)
                            pe.wait_ge(pv_taken, times(i, -1, n) * groups)
                            for k, m in enumerate((m0, m1)):
                                if k == 0:
                                    wait(pe, qk_taken, times(i, 2, n) * 2)
                                    wait(pe, shift_rows_ready, times(i, 0, n) * 2)
                                else:
                                    wait(pe, v_taken, times(i, 1, n))
                                    wait(pe, y_ready, times(i, -2, n))
                                for t in range(TILES):
                                    for g in range(2):
                                        last = pe.transpose(m[:, (2 * t + g) * P:(2 * t + g + 1) * P],
                                                            heads_t[b.odd][:, 2 * k + g, t * P:(t + 1) * P], core.ident[:, :])
                                last.then_inc(heads_in_psum, 1)
                        if s == (9 if first else 6) and on(-1):
                            b = i.plus(-1)
                            if first:
                                pe.wait_ge(o_ready, times(i, -1, n) * 2)
                            else:
                                pe.wait_ge(pv_taken, times(i, -1, n) * (HEADS * TILES))
                                wait(pe, v_taken, times(i, 1, n))
                                wait(pe, y_ready, times(i, -2, n))
                            for t in range(TILES):
                                src = o[:, t, :] if first else o_sum[b.odd][:, t, :]
                                last = pe.transpose(m1[:, t * P:(t + 1) * P], src, core.ident[:, :])
                            last.then_inc(ot_in_psum, 1)
                        if s == 10 and on(1):
                            if first:
                                wait(pe, o_ready, times(i, -1, n) * 2)
                                wait(pe, qk_taken, times(i, 2, n) * 2)
                            wait(pe, shift_rows_ready, times(i, 0, n) * 2)
                            shifts_turned(i.plus(1), 0)
                        if s == (12 if first else 9) and on(-1):
                            pe.wait_ge(ot_ready, times(i, -1, n))
                            w_out = core.w0_out if first else core.w1_out
                            for t in range(TILES):
                                last = pe.matmul(m1[:, t * P:(t + 1) * P], o_t[:, t * P:(t + 1) * P], w_out[:, :],
                                                 start=True, stop=True)
                            last.then_inc(out_in_psum, 1)
                        if on(0):
                            b = i
                            if s % half_heads == 0:
                                pe.wait_ge(shifted[s // half_heads], b.number() * 32 + 32)
                            wait(pe, exp_done, b.number() * HEADS + (s - 1))
                            for t in range(TILES):
                                last = pe.matmul(s2[s % 2][:, t * TOK:(t + 1) * TOK],
                                                 core.k_stack[b.odd][0:SHIFT_ROW + 1, s // 2, t * P:(t + 1) * P],
                                                 core.q_stack[b.odd][0:SHIFT_ROW + 1, s % 2, s // 2, :], start=True, stop=True)
                            last.then_inc(s_in_psum, 1)
                        if on(1):
                            b = i.plus(1)
                            if s % half_heads == 0:
                                pe.wait_ge(stacked[s // half_heads], b.number() * 64 + 64)
                            wait(pe, max_done, b.number() * HEADS + (s - 1))
                            for t in range(TILES):
                                last = pe.matmul(s1[s % 2][:, t * TOK:(t + 1) * TOK],
                                                 core.q_stack[b.odd][0:PAIR_ROWS, s % 2, s // 2, t * P:(t + 1) * P],
                                                 core.k_stack[b.odd][0:PAIR_ROWS, s // 2, :], start=True, stop=True)
                            last.then_inc(max_in_psum, 1)
                        if first:
                            if s in (5, 9, 13) and on(0):
                                products_by_group(i, (s - 5) // 4)
                        elif s >= 2:
                            if on(0):
                                products_of_head(i, s - 2)
                        elif on(-1):
                            products_of_head(i.plus(-1), s + HEADS - 2)

                pe.wait_ge(ones_ready, 4 if first else 2)
                steps(pe, n, 2, 1, step)


def ffn0(nc, core):
    n = core.n
    chunks = 4
    xt_bank, out_bank = core.bank[0], core.bank[5]
    up_banks = (core.bank[1:3], core.bank[6:8])
    turn_banks = core.bank[3:5]

    with ExitStack() as ctx:
        def sb(name, shape, dt=FP32):
            return ctx.enter_context(nc.sbuf_tensor(f"{name}_f0", shape, dt))

        def sem(name):
            return core.sem(f"{name}_f0")

        x_in = [sb(f"x_in{k}", [P, TILES, D]) for k in range(2)]
        x_t = sb("x_t", [P, TOK])
        h = sb("h", [P, TILES, chunks * D])
        h_norm = [sb(f"h_norm{k}", [P, TILES, chunks * D]) for k in range(2)]
        h_t = sb("h_t", [P, chunks, TOK])
        y = sb("y", [P, TILES, D])
        h_stats, y_stats, x_stats = (sb(f"{v}_stats", [P, TILES, 6]) for v in "hyx")
        h_moments, y_moments, x_moments = (sb(f"{v}_moments", [P, TILES, 2]) for v in "hyx")
        h_var, y_var, x_var = (sb(f"{v}_var", [P, TILES]) for v in "hyx")
        h_rstd, y_rstd, x_rstd = (sb(f"{v}_rstd", [P, TILES]) for v in "hyx")

        x_loaded = [sem(f"x_loaded{k}") for k in range(2)]
        xt_in_psum = sem("xt_in_psum")
        xt_ready = sem("xt_ready")
        up_in_psum = sem("up_in_psum")
        h_ready = sem("h_ready")
        h_norm_ready = sem("h_norm_ready")
        turned_in_psum = sem("turned_in_psum")
        h_t_ready = sem("h_t_ready")
        out_in_psum = sem("out_in_psum")
        y_ready = sem("y_ready")
        x_ready = sem("x_ready")
        xh_ready = sem("xh_ready")
        h_sems, y_sems, x_sems = ({k: sem(f"{v}_{k}") for k in ("stats", "moments", "var", "rstd")} for v in "hyx")

        def rsqrt(pool, count, sems, moments, var, rstd):
            pool.wait_ge(sems["moments"], count * TILES)
            pool.tensor_tensor(var[:, :], moments[:, :, 1], core.eps[:, :], op=ALU.add).then_inc(sems["var"], 1)
            pool.wait_ge(sems["var"], count)
            pool.tensor_tensor(rstd[:, :], var[:, :], core.minus_half[:, :], op=ALU.pow).then_inc(sems["rstd"], 1)

        def measure(dve, before, sems, source, stats, moments):
            for t in range(TILES):
                dve.bn_stats(stats[:, t, :], source(t)).then_inc(sems["stats"], 1)
            wait_apart(dve, sems["var"], before)
            wait_apart(dve, sems["stats"], before * TILES + TILES)
            for t in range(TILES):
                dve.bn_aggr(moments[:, t, :], stats[:, t, :]).then_inc(sems["moments"], 1)

        with nc.Block() as block:
            @block.sync
            def _(sp):
                def step(i, on):
                    if on(2):
                        b = i.plus(2)
                        wait_apart(sp, xt_in_psum, times(i, 0, n))
                        sp.dma_start(x_in[b.odd][:, :, :], core.x_all[:, b.number(), :, :]).then_inc(x_loaded[b.odd], 16)

                steps(sp, n, 2, 0, step)

            @block.gpsimd
            def _(pool):
                def step(i, on):
                    if on(-1):
                        rsqrt(pool, times(i, -1, n), x_sems, x_moments, x_var, x_rstd)
                    if on(1):
                        rsqrt(pool, times(i, 1, n), h_sems, h_moments, h_var, h_rstd)
                    if on(0):
                        rsqrt(pool, times(i, 0, n), y_sems, y_moments, y_var, y_rstd)

                steps(pool, n, 1, 1, step)

            @block.scalar
            def _(act):
                def step(i, on):
                    if on(1):
                        act.wait_ge(xt_in_psum, times(i, 1, n))
                        act.activation(x_t[:, :], xt_bank[:, 0:TOK], ACT.Copy).then_inc(xt_ready, 1)
                    if on(0):
                        for c in range(chunks):
                            if c % 2 == 0:
                                act.wait_ge(turned_in_psum, times(i, -1, n) * 2 + (c // 2 + 1))
                            act.activation(h_t[:, c, :], turn_banks[c // 2][:, c % 2 * TOK:(c % 2 + 1) * TOK], ACT.Identity,
                                           scale=core.cols[:, c:c + 1], bias=core.cols[:, 4 + c:5 + c]).then_inc(h_t_ready, 1)
                    if on(1):
                        b = i.plus(1)
                        wait(act, h_norm_ready, times(i, 0, n) * TILES)
                        for t in range(TILES):
                            act.wait_ge(up_in_psum, times(i, 0, n) * TILES + (t + 1))
                            act.activation(h[:, t, :], up_banks[b.odd][t][:, :], ACT.Gelu).then_inc(h_ready, 1)

                steps(act, n, 1, 1, step)

            @block.vector
            def _(dve):
                def normalise(to, source, moments, rstd, sem_):
                    for t in range(TILES):
                        dve.tensor_scalar(to(t), source(t), moments[:, t, 0:1], rstd[:, t:t + 1],
                                          ALU.subtract, ALU.mult).then_inc(sem_, 1)

                def step(i, on):
                    last = i.plus(-1)
                    if on(-1):
                        wait_apart(dve, x_ready, times(i, -1, n) * TILES)
                        measure(dve, times(i, -2, n), x_sems, lambda t: core.x_all[:, last.number(), t, :], x_stats, x_moments)
                    if on(1):
                        wait_apart(dve, h_ready, times(i, 1, n) * TILES)
                        measure(dve, times(i, 0, n), h_sems, lambda t: h[:, t, :], h_stats, h_moments)
                    if on(-1):
                        dve.wait_ge(x_sems["rstd"], times(i, -1, n))
                        dve.wait_ge(x_sems["moments"], times(i, -1, n) * TILES)
                        normalise(lambda t: core.xh_all[:, last.number(), t, :], lambda t: core.x_all[:, last.number(), t, :],
                                  x_moments, x_rstd, xh_ready)
                    if on(0):
                        wait(dve, x_ready, times(i, -1, n) * TILES)
                        dve.wait_ge(out_in_psum, times(i, 0, n))
                        dve.tensor_tensor(y[:, :, :], out_bank[:, 0:TOK].rearrange("p (t d) -> p t d", t=TILES),
                                          core.x_all[:, i.number(), :, :], op=ALU.add).then_inc(y_ready, 1)
                        wait_apart(dve, y_ready, times(i, 0, n))
                        measure(dve, times(i, -1, n), y_sems, lambda t: y[:, t, :], y_stats, y_moments)
                    if on(1):
                        b = i.plus(1)
                        dve.wait_ge(h_sems["rstd"], times(i, 1, n))
                        dve.wait_ge(h_sems["moments"], times(i, 1, n) * TILES)
                        normalise(lambda t: h_norm[b.odd][:, t, :], lambda t: h[:, t, :], h_moments, h_rstd, h_norm_ready)
                    if on(0):
                        dve.wait_ge(y_sems["rstd"], times(i, 0, n))
                        dve.wait_ge(y_sems["moments"], times(i, 0, n) * TILES)
                        normalise(lambda t: core.x_all[:, i.number(), t, :], lambda t: y[:, t, :], y_moments, y_rstd, x_ready)

                steps(dve, n, 1, 1, step)
                dve.wait_ge(xh_ready, n * TILES)

            @block.tensor
            def _(pe):
                def step(i, on):
                    if on(1):
                        b = i.plus(1)
                        pe.wait_ge(x_loaded[b.odd], (b.half + 1) * 16)
                        wait(pe, xt_ready, times(i, 0, n))
                        for t in range(TILES):
                            last = pe.transpose(xt_bank[:, t * P:(t + 1) * P], x_in[b.odd][:, t, :], core.ident[:, :])
                        last.then_inc(xt_in_psum, 1)
                    if on(0):
                        pe.wait_ge(h_norm_ready, times(i, 0, n) * TILES)
                        wait(pe, h_t_ready, times(i, -1, n) * chunks)
                        for k in range(2):
                            for c in range(2):
                                for t in range(TILES):
                                    last = pe.transpose(turn_banks[k][:, (2 * c + t) * P:(2 * c + t + 1) * P],
                                                        h_norm[i.odd][:, t, (2 * k + c) * D:(2 * k + c + 1) * D],
                                                        core.ident[:, :])
                            last.then_inc(turned_in_psum, 1)
                    if on(1):
                        b = i.plus(1)
                        pe.wait_ge(xt_ready, times(i, 1, n))
                        wait(pe, h_ready, times(i, -1, n) * TILES)
                        for t in range(TILES):
                            pe.matmul(up_banks[b.odd][t][:, :], x_t[:, t * P:(t + 1) * P],
                                      core.w0_fc[:, :, :].rearrange("p c d -> p (c d)"), start=True, stop=True).then_inc(up_in_psum, 1)
                    if on(0):
                        pe.wait_ge(h_t_ready, times(i, 0, n) * chunks)
                        wait(pe, y_ready, times(i, -1, n))
                        for t in range(TILES):
                            for c in range(chunks):
                                last = pe.matmul(out_bank[:, t * P:(t + 1) * P], h_t[:, c, t * P:(t + 1) * P],
                                                 core.w0_proj[:, c, :], start=(c == 0), stop=(c == chunks - 1))
                        last.then_inc(out_in_psum, 1)

                steps(pe, n, 1, 1, step)


def ffn1(nc, core, out):
    n = core.n
    chunks = 3
    xt_bank, out_bank = core.bank[0], core.bank[4]
    up_banks = (core.bank[1:4], core.bank[5:8])
    out_v = out.rearrange("b (t p) d -> b p t d", p=P)

    with ExitStack() as ctx:
        def sb(name, shape, dt=FP32):
            return ctx.enter_context(nc.sbuf_tensor(f"{name}_f1", shape, dt))

        def sem(name):
            return core.sem(f"{name}_f1")

        x_in = [sb(f"x_in{k}", [P, TILES, D]) for k in range(2)]
        x_t = sb("x_t", [P, TOK])
        gate = sb("gate", [P, chunks, TOK])
        h_t = [sb(f"h_t{k}", [P, chunks, TOK]) for k in range(2)]
        y = sb("y", [P, TILES, D])
        stats = sb("stats", [P, TILES, 6])
        moments = sb("moments", [P, TILES, 2])
        var = sb("var", [P, TILES])
        rstd = sb("rstd", [P, TILES])
        x_out = [sb(f"x_out{k}", [P, TILES, D]) for k in range(2)]

        x_loaded = [sem(f"x_loaded{k}") for k in range(2)]
        xt_in_psum = sem("xt_in_psum")
        xt_ready = sem("xt_ready")
        up_in_psum = sem("up_in_psum")
        gate_ready = sem("gate_ready")
        h_ready = sem("h_ready")
        out_in_psum = sem("out_in_psum")
        y_ready = sem("y_ready")
        stats_ready = sem("stats_ready")
        moments_ready = sem("moments_ready")
        var_ready = sem("var_ready")
        rstd_ready = sem("rstd_ready")
        x_out_ready = sem("x_out_ready")
        stored = [sem(f"stored{k}") for k in range(2)]

        with nc.Block() as block:
            @block.sync
            def _(sp):
                def step(i, on):
                    if on(2):
                        b = i.plus(2)
                        wait_apart(sp, xt_in_psum, times(i, 0, n))
                        sp.dma_start(x_in[b.odd][:, :, :], core.x_all[:, b.number(), :, :]).then_inc(x_loaded[b.odd], 16)
                    if on(0):
                        wait_apart(sp, x_out_ready, times(i, 0, n) * TILES)
                        sp.dma_start(out_v[i.number(), :, :, :], x_out[i.odd][:, :, :]).then_inc(stored[i.odd], 16)

                steps(sp, n, 2, 0, step)
                for k in range(2):
                    sp.wait_ge(stored[k], (n - k + 1) // 2 * 16)

            @block.gpsimd
            def _(pool):
                def step(i, on):
                    if on(0):
                        pool.wait_ge(moments_ready, times(i, 0, n) * TILES)
                        pool.tensor_tensor(var[:, :], moments[:, :, 1], core.eps[:, :], op=ALU.add).then_inc(var_ready, 1)
                        pool.wait_ge(var_ready, times(i, 0, n))
                        pool.tensor_tensor(rstd[:, :], var[:, :], core.minus_half[:, :], op=ALU.pow).then_inc(rstd_ready, 1)

                steps(pool, n, 0, 0, step)

            @block.scalar
            def _(act):
                def step(i, on):
                    if on(1):
                        b = i.plus(1)
                        act.wait_ge(xt_in_psum, times(i, 1, n))
                        act.activation(x_t[:, :], xt_bank[:, 0:TOK], ACT.Copy).then_inc(xt_ready, 1)
                        wait(act, h_ready, times(i, 0, n) * chunks)
                        for c in range(chunks):
                            act.wait_ge(up_in_psum, times(i, 0, n) * chunks + (c + 1))
                            act.activation(gate[:, c, :], up_banks[b.odd][c][:, 0:TOK], ACT.Silu).then_inc(gate_ready, 1)

                steps(act, n, 1, 0, step)

            @block.vector
            def _(dve):
                def step(i, on):
                    if on(0):
                        wait(dve, x_out_ready, times(i, -1, n) * TILES)
                        dve.wait_ge(out_in_psum, times(i, 0, n))
                        dve.tensor_tensor(y[:, :, :], out_bank[:, 0:TOK].rearrange("p (t d) -> p t d", t=TILES),
                                          core.x_all[:, i.number(), :, :], op=ALU.add).then_inc(y_ready, 1)
                        wait_apart(dve, y_ready, times(i, 0, n))
                        for t in range(TILES):
                            dve.bn_stats(stats[:, t, :], y[:, t, :]).then_inc(stats_ready, 1)
                        wait_apart(dve, var_ready, times(i, -1, n))
                        wait_apart(dve, stats_ready, times(i, 0, n) * TILES)
                        for t in range(TILES):
                            dve.bn_aggr(moments[:, t, :], stats[:, t, :]).then_inc(moments_ready, 1)
                    if on(1):
                        b = i.plus(1)
                        for c in range(chunks):
                            dve.wait_ge(gate_ready, times(i, 0, n) * chunks + (c + 1))
                            dve.tensor_tensor(h_t[b.odd][:, c, :], up_banks[b.odd][c][:, TOK:2 * TOK], gate[:, c, :],
                                              op=ALU.mult).then_inc(h_ready, 1)
                    if on(0):
                        dve.wait_ge(rstd_ready, times(i, 0, n))
                        dve.wait_ge(moments_ready, times(i, 0, n) * TILES)
                        wait(dve, stored[i.odd], i.half * 16)
                        for t in range(TILES):
                            dve.tensor_scalar(x_out[i.odd][:, t, :], y[:, t, :], moments[:, t, 0:1], rstd[:, t:t + 1],
                                              ALU.subtract, ALU.mult).then_inc(x_out_ready, 1)

                steps(dve, n, 1, 0, step)

            @block.tensor
            def _(pe):
                def step(i, on):
                    if on(1):
                        b = i.plus(1)
                        pe.wait_ge(x_loaded[b.odd], (b.half + 1) * 16)
                        wait(pe, xt_ready, times(i, 0, n))
                        for t in range(TILES):
                            last = pe.transpose(xt_bank[:, t * P:(t + 1) * P], x_in[b.odd][:, t, :], core.ident[:, :])
                        last.then_inc(xt_in_psum, 1)
                    if on(0):
                        pe.wait_ge(h_ready, times(i, 0, n) * chunks)
                        wait(pe, y_ready, times(i, -1, n))
                        for t in range(TILES):
                            for c in range(chunks):
                                last = pe.matmul(out_bank[:, t * P:(t + 1) * P], h_t[i.odd][:, c, t * P:(t + 1) * P],
                                                 core.w1_down[:, c, :], start=(c == 0), stop=(c == chunks - 1))
                        last.then_inc(out_in_psum, 1)
                    if on(1):
                        b = i.plus(1)
                        pe.wait_ge(xt_ready, times(i, 1, n))
                        wait(pe, h_ready, times(i, -1, n) * chunks)
                        for c in range(chunks):
                            pe.matmul(up_banks[b.odd][c][:, 0:TOK], core.w1_gate[:, c, :], x_t[:, :], start=True, stop=True)
                            pe.matmul(up_banks[b.odd][c][:, TOK:2 * TOK], core.w1_up[:, c, :], x_t[:, :],
                                      start=True, stop=True).then_inc(up_in_psum, 1)

                steps(pe, n, 1, 0, step)


_WEIGHTS = {"w_qkv": "L0_attn_w_qkv", "w_out0": "L0_attn_w_out", "b_out": "L0_attn_b_out", "w_fc": "L0_ffn_W_fc",
            "ln_w": "L0_ffn_ln_w", "ln_b": "L0_ffn_ln_b", "w_proj": "L0_ffn_W_proj", "ln_g1": "L1_attn_ln_g",
            "ln_b1": "L1_attn_ln_b", "w_kv": "L1_attn_W_kv", "w_x": "L1_attn_W_x", "w_out1": "L1_attn_W_out",
            "w_gate": "L1_ffn_w_gate", "w_up": "L1_ffn_w_up", "w_down": "L1_ffn_w_down"}


def build(nc, x, weights, out):
    n = x.shape[0]
    scratch = nc.dram_tensor("score_parts", (2, SLOTS, P, TOK), BF16, kind="Internal").ap()
    w = dict(weights)
    w["rope"] = nc.inline_tensor(rope_tables(), name="rope_tables").ap()
    with ExitStack() as ctx:
        core = Core(nc, ctx, n)
        prepare(nc, core, w)
        attention(nc, core, 0, x, scratch)
        ffn0(nc, core)
        attention(nc, core, 1, None, scratch)
        ffn1(nc, core, out)


def kernel(**inputs):
    import numpy as _np
    import concourse.bacc as _bacc
    from concourse import mybir as _mybir
    from concourse.bass_utils import run_bass_kernel_spmd as _run

    nc = _bacc.Bacc("TRN2", target_bir_lowering=False, num_devices=1)
    arrays, aps = {}, {}
    for name in ["L0_attn_x", *_WEIGHTS.values()]:
        a = _np.ascontiguousarray(inputs[name])
        arrays[f"in_{name}"] = a
        aps[name] = nc.dram_tensor(f"in_{name}", a.shape, _mybir.dt.from_np(a.dtype), kind="ExternalInput").ap()
    shape = arrays["in_L0_attn_x"].shape
    out = nc.dram_tensor("out_x", shape, _mybir.dt.float32, kind="ExternalOutput").ap()
    build(nc, aps["L0_attn_x"], {k: aps[v] for k, v in _WEIGHTS.items()}, out)
    r = _run(nc, [arrays], core_ids=[0])
    return r.results[0]["out_x"]
```

```python
import numpy as np
import concourse.bass as bass
from concourse import mybir
from contextlib import ExitStack

FP32 = mybir.dt.float32
BF16 = mybir.dt.bfloat16
INT32 = mybir.dt.int32
ALU = mybir.AluOpType
ACT = mybir.ActivationFunctionType
AX = mybir.AxisListType

P = 128
D = 128
TOK = 256
TILES = TOK // P
HEADS = 16
HD = D // HEADS
PAIRS = HEADS // 2
BANK = 512
LN_EPS = 1e-5

K_PART = (0, 0, 0, 1, 1, 2)
Q_PART = (0, 1, 2, 0, 1, 0)
SLOTS = len(K_PART)
RUNS = ((0, 3), (3, 2), (5, 1))
HEAD_ROWS = SLOTS * HD
PAIR_ROWS = 2 * HEAD_ROWS
SHIFT_ROW = PAIR_ROWS
RING = 8
VW = 32

SHIFTS1 = 1
V_SLOT = 2
HEADS0, HEADS1 = 4, 5
OT_SLOT, OUT_SLOT, Y_SLOT = 8, 10, 11
SHIFTS0 = 9
XT_SLOT, Q_SLOT, K_SLOT = 12, 14, 15


class Batch:

    def __init__(self, half, odd):
        self.half, self.odd = half, odd

    def plus(self, k):
        n = self.odd + k
        return Batch(self.half + n // 2 if n // 2 else self.half, n % 2)

    def number(self):
        return self.half * 2 + self.odd if self.odd else self.half * 2


def wait(eng, sem, count):
    if isinstance(count, int) and count <= 0:
        return
    eng.wait_ge(sem, count)


def wait_apart(eng, sem, count):
    if not isinstance(count, int):
        count = eng.to_reg(count)
        eng.wait_ge(sem, 1)
    wait(eng, sem, count)


def steps(eng, n, ahead, behind, step):
    def peeled(i):
        step(Batch(i // 2, i % 2), lambda k: 0 <= i + k < n)

    start = max(2, behind + behind % 2)
    end = start + (n - ahead - start) // 2 * 2
    for i in range(-ahead, start):
        peeled(i)
    with eng.Fori(start // 2, end // 2) as half:
        step(Batch(half, 0), lambda k: True)
        step(Batch(half, 1), lambda k: True)
    for i in range(end, n + behind):
        peeled(i)


def times(i, k, n):
    if isinstance(i.half, int):
        return max(0, min(n, 2 * i.half + i.odd + k + 1))
    assert i.odd + k + 1 > -2, "a loop's first step is 2 or later, and no wait is for less than one"
    return i.half * 2 + (i.odd + k + 1)


def rope_tables():
    inv = (1.0 / 10000.0 ** (np.arange(0, HD, 2, dtype=np.float32) / HD)).astype(np.float32)
    angle = np.outer(np.arange(TOK, dtype=np.float32), inv).astype(np.float32)
    table = np.zeros((2, HD, PAIRS, 2, TOK), np.float32)
    for d in range(HD):
        table[:, d, :, 0, :] = np.cos(angle[:, d // 2])
        table[:, d, :, 1, :] = np.sin(angle[:, d // 2]) * (1 if d % 2 else -1)
    return table.reshape(P, 2, TOK)


class Core:

    def __init__(self, nc, ctx, n):
        self.nc, self.ctx, self.n = nc, ctx, n
        sb = self.sb
        self.bank = [ctx.enter_context(nc.psum_tensor(f"bank{k}", [P, BANK], FP32)) for k in range(8)]
        self.x_all = sb("x_all", [P, n, TILES, D])
        self.x_all_loads = 4
        self.x_all_loaded = self.sem("x_all_loaded")
        self.xh_all = sb("xh_all", [P, n, TILES, D])
        self.ident = sb("ident", [P, P])
        self.ident_bf = sb("ident_bf", [P, P], BF16)
        self.w0_qk = sb("w0_qk", [P, 2, 2, D])
        self.w0_v = sb("w0_v", [P, D])
        self.w0_out = sb("w0_out", [P, D])
        self.b0_out = sb("b0_out", [P, D])
        self.rope = sb("rope", [P, 2, TOK])
        self.w0_fc = sb("w0_fc", [P, 4, D])
        self.w0_proj = sb("w0_proj", [P, 4, D])
        self.cols = sb("cols", [P, 10])
        self.w1_kv = sb("w1_kv", [P, 2, D])
        self.w1_qk = sb("w1_qk", [P, D])
        self.w1_out = sb("w1_out", [P, D])
        self.mix = sb("mix", [P, HEADS, D])
        self.w1_gate = sb("w1_gate", [P, 3, D])
        self.w1_up = sb("w1_up", [P, 3, D])
        self.w1_down = sb("w1_down", [P, 3, D])
        self.zeros = sb("zeros", [P, TOK])
        self.ln_scale = sb("ln_scale", [P, 2, TILES])
        self.ln_shift = sb("ln_shift", [P, 2, TILES])
        self.minus_half = sb("minus_half", [P, 2, TILES])
        self.k_stack = [sb(f"k_stack{k}", [P, PAIRS, TOK], BF16) for k in range(2)]
        self.q_stack = [sb(f"q_stack{k}", [P, 2, PAIRS, TOK], BF16) for k in range(2)]

    def sb(self, name, shape, dt=FP32):
        return self.ctx.enter_context(self.nc.sbuf_tensor(name, shape, dt))

    def sem(self, name):
        return self.ctx.enter_context(self.nc.semaphore(name))


def prepare(nc, core, w):
    bank = core.bank
    with ExitStack() as ctx:
        def sb(name, shape, dt=FP32):
            return ctx.enter_context(nc.sbuf_tensor(name, shape, dt))

        def sem(name):
            return core.sem(name)

        raw_qkv = sb("raw_qkv", [P, 3, D])
        raw_out = sb("raw_out", [P, D])
        raw_rows = sb("raw_rows", [10, D])
        raw_mix = sb("raw_mix", [1, HEADS * HEADS])
        raw_bias = sb("raw_bias", [1, D])
        raw_fc = sb("raw_fc", [P, 4, D])
        raw_proj = sb("raw_proj", [P, 4, D])
        raw_int = sb("raw_int", [P, 3, 3, D], INT32)
        scaled = sb("scaled", [P, 3, 3, D])
        ternary = sb("ternary", [P, 2, 4, D])
        below = sb("below", [P, 2, 4, D])
        ones = sb("ones", [P, P])
        totals = sb("totals", [P, 2])
        gamma = sb("gamma", [P, 2])
        bounds = sb("bounds", [P, 2, 2])

        load_attn = sem("load_attn")
        load_ffn0 = sem("load_ffn0")
        load_ffn1 = sem("load_ffn1")
        load_rest = sem("load_rest")
        ident_step = sem("ident_step")
        ident_bf_ready = sem("ident_bf_ready")
        stacks_zero = sem("stacks_zero")
        consts_ready = sem("consts_ready")
        sums_ready = sem("sums_ready")
        gamma_total = sem("gamma_total")
        gamma_step = sem("gamma_step")
        below_ready = sem("below_ready")
        ternary_ready = sem("ternary_ready")
        scaled_ready = sem("scaled_ready")
        attn_turned = sem("attn_turned")
        small_turned = sem("small_turned")
        ffn0_turned = sem("ffn0_turned")
        ffn1_turned = sem("ffn1_turned")

        with nc.Block() as block:
            @block.sync
            def _(sp):
                sp.dma_start(raw_qkv[:, :, :], w["w_qkv"].rearrange("(t e) d -> e t d", e=D)).then_inc(load_attn, 16)
                sp.dma_start(raw_out[:, :], w["w_out0"]).then_inc(load_attn, 16)
                sp.dma_start(raw_fc[:, :, :], w["w_fc"].rearrange("(c p) d -> p c d", p=P)).then_inc(load_ffn0, 16)
                sp.dma_start(raw_proj[:, :, :], w["w_proj"].rearrange("p (c d) -> p c d", c=4)).then_inc(load_ffn0, 16)
                sp.dma_start(core.rope[:, :, :], w["rope"]).then_inc(load_rest, 16)
                sp.dma_start(core.w1_kv[:, :, :], w["w_kv"].rearrange("p (t e) -> p t e", t=2)).then_inc(load_rest, 16)
                sp.dma_start(core.w1_out[:, :], w["w_out1"]).then_inc(load_rest, 16)
                x = w["x"].rearrange("b (t p) d -> p (b t) d", p=P)
                to = core.x_all[:, :, :, :].rearrange("p b t d -> p (b t) d")
                tiles = core.n * TILES // core.x_all_loads
                for k in range(core.x_all_loads):
                    sp.dma_start(to[:, k * tiles:(k + 1) * tiles, :], x[:, k * tiles:(k + 1) * tiles, :]).then_inc(core.x_all_loaded, 16)

            @block.scalar
            def _(act):
                act.dma_start(raw_rows[0:4, :], w["ln_w"].rearrange("(c p) -> c p", p=P)).then_inc(load_rest, 16)
                act.dma_start(raw_rows[4:8, :], w["ln_b"].rearrange("(c p) -> c p", p=P)).then_inc(load_rest, 16)
                act.dma_start(raw_rows[8:9, :], w["ln_g1"].rearrange("(a p) -> a p", a=1)).then_inc(load_rest, 16)
                act.dma_start(raw_rows[9:10, :], w["ln_b1"].rearrange("(a p) -> a p", a=1)).then_inc(load_rest, 16)
                act.dma_start(raw_mix[:, :], w["w_x"].rearrange("(a g) h -> a (g h)", a=1)).then_inc(load_rest, 16)
                act.dma_start(raw_bias[:, :], w["b_out"].rearrange("(a p) -> a p", a=1)).then_inc(load_rest, 16)
                act.dma_start(raw_int[:, 0, :, :], w["w_gate"].rearrange("(c p) d -> p c d", p=P)).then_inc(load_ffn1, 16)
                act.dma_start(raw_int[:, 1, :, :], w["w_up"].rearrange("(c p) d -> p c d", p=P)).then_inc(load_ffn1, 16)
                act.dma_start(raw_int[:, 2, :, :], w["w_down"].rearrange("p (c d) -> p c d", c=3)).then_inc(load_ffn1, 16)

            @block.gpsimd
            def _(pool):
                pool.memset(core.ident[:, :], 0.0).then_inc(ident_step, 1)
                pool.wait_ge(ident_step, 1)
                pool.affine_select(out=core.ident[:, :], in_=core.ident[:, :], compare_op=ALU.not_equal, fill=1.0,
                                   base=0, pattern=[[-1, P]], channel_multiplier=1).then_inc(ident_step, 1)

            @block.vector
            def _(dve):
                dve.memset(ones[:, :], 1.0).then_inc(consts_ready, 1)
                dve.memset(core.zeros[:, :], 0.0)
                dve.memset(core.ln_scale[:, 0, :], 1.0)
                dve.memset(core.ln_scale[:, 1, :], 1.0 + LN_EPS)
                dve.memset(core.ln_shift[:, 0, :], LN_EPS)
                dve.memset(core.ln_shift[:, 1, :], LN_EPS * LN_EPS)
                dve.memset(core.minus_half[:, :, :], -0.5)
                for stack in core.q_stack:
                    dve.memset(stack[:, :, :, :], 0.0).then_inc(stacks_zero, 1)
                for k, stack in enumerate(core.k_stack):
                    dve.memset(stack[:, :, :], 0.0).then_inc(stacks_zero, 1)
                    dve.wait_ge(stacks_zero, 3 + k)
                    dve.memset(stack[SHIFT_ROW:SHIFT_ROW + 1, :, :], 1.0)
                dve.wait_ge(ident_step, 2)
                dve.tensor_copy(core.ident_bf[:, :], core.ident[:, :])
                dve.wait_ge(load_ffn0, 32)
                for k, raw in enumerate((raw_fc, raw_proj)):
                    dve.tensor_reduce(totals[:, k:k + 1], raw[:, :, :], op=ALU.add, axis=AX.XY,
                                      apply_absolute_value=True).then_inc(sums_ready, 1)
                dve.wait_ge(gamma_total, 1)
                dve.tensor_scalar(gamma[:, :], bank[7][:, 0:2], 1.0 / (4 * P * D), 1e-6,
                                  ALU.mult, ALU.add).then_inc(gamma_step, 1)
                dve.wait_ge(gamma_step, 1)
                dve.tensor_scalar(bounds[:, 0, :], gamma[:, :], 0.5, None, ALU.mult).then_inc(gamma_step, 1)
                dve.tensor_scalar(bounds[:, 1, :], gamma[:, :], -0.5, None, ALU.mult).then_inc(gamma_step, 1)
                dve.wait_ge(gamma_step, 3)
                for k, raw in enumerate((raw_fc, raw_proj)):
                    dve.tensor_scalar(below[:, k, :, :], raw[:, :, :], bounds[:, 1, k:k + 1], None,
                                      ALU.is_lt).then_inc(below_ready, 1)
                for k, raw in enumerate((raw_fc, raw_proj)):
                    dve.wait_ge(below_ready, k + 1)
                    dve.scalar_tensor_tensor(ternary[:, k, :, :].rearrange("p c d -> p (c d)"),
                                             raw[:, :, :].rearrange("p c d -> p (c d)"), bounds[:, 0, k:k + 1],
                                             below[:, k, :, :].rearrange("p c d -> p (c d)"),
                                             op0=ALU.is_gt, op1=ALU.subtract).then_inc(ternary_ready, 1)
                dve.wait_ge(load_ffn1, 48)
                dve.tensor_scalar(scaled[:, :, :, :].rearrange("p a c d -> p (a c d)"),
                                  raw_int[:, :, :, :].rearrange("p a c d -> p (a c d)"), float(np.float32(1.0 / 127.0)), None,
                                  ALU.mult).then_inc(scaled_ready, 1)
                dve.wait_ge(attn_turned, 1)
                for side in range(2):
                    turned = bank[0][:, side * D:(side + 1) * D].rearrange("p (r a d) -> p a d r", a=2, d=HD)
                    dve.tensor_copy(core.w0_qk[:, side, 0, :].rearrange("p (a d r) -> p a d r", a=2, d=HD), turned)
                    swapped = core.w0_qk[:, side, 1, :].rearrange("p (a c t r) -> p a c t r", a=2, c=HD // 2, t=2)
                    source = bank[0][:, side * D:(side + 1) * D].rearrange("p (r a c t) -> p a c t r", a=2, c=HD // 2, t=2)
                    for t in range(2):
                        dve.tensor_copy(swapped[:, :, :, t, :], source[:, :, :, 1 - t, :])
                dve.tensor_copy(core.w0_v[:, :], bank[0][:, 2 * D:3 * D])
                dve.tensor_copy(core.w0_out[:, :], bank[0][:, 3 * D:4 * D])
                dve.wait_ge(small_turned, 1)
                dve.tensor_copy(core.cols[:, :], bank[1][:, 0:10])
                dve.tensor_copy(core.b0_out[:, :], bank[1][:, 384:512])
                mixed = bank[1][:, 128:384].rearrange("p (g h) -> p h g", h=HEADS)
                for d in range(HD):
                    dve.tensor_copy(core.mix[:, :, :].rearrange("p h (g d) -> p h g d", d=HD)[:, :, :, d], mixed)
                dve.wait_ge(load_rest, 16 * 9)
                dve.tensor_copy(core.w1_qk[:, :].rearrange("p (a d r) -> p a d r", a=2, d=HD),
                                core.w1_kv[:, 0, :].rearrange("p (r a d) -> p a d r", a=2, d=HD))
                dve.wait_ge(ffn0_turned, 2)
                dve.tensor_copy(core.w0_fc[:, :, :].rearrange("p c d -> p (c d)"), bank[2][:, :])
                dve.tensor_copy(core.w0_proj[:, :, :].rearrange("p c d -> p (c d)"), bank[3][:, :])
                dve.wait_ge(ffn1_turned, 1)
                for k, to in enumerate((core.w1_gate, core.w1_up, core.w1_down)):
                    dve.tensor_copy(to[:, :, :].rearrange("p c d -> p (c d)"), bank[4 + k][:, 0:3 * D])

            @block.tensor
            def _(pe):
                pe.wait_ge(ident_step, 2)
                pe.wait_ge(load_attn, 32)
                for t in range(3):
                    pe.transpose(bank[0][:, t * D:(t + 1) * D], raw_qkv[:, t, :], core.ident[:, :])
                pe.transpose(bank[0][:, 3 * D:4 * D], raw_out[:, :], core.ident[:, :]).then_inc(attn_turned, 1)
                pe.wait_ge(consts_ready, 1)
                pe.wait_ge(load_rest, 16 * 9)
                pe.transpose(bank[1][:, 0:10], raw_rows[:, :], core.ident[0:10, 0:10])
                pe.matmul(bank[1][:, 128:384], ones[0:1, :], raw_mix[:, :], start=True, stop=True)
                pe.matmul(bank[1][:, 384:512], ones[0:1, :], raw_bias[:, :], start=True, stop=True).then_inc(small_turned, 1)
                pe.wait_ge(sums_ready, 2)
                pe.matmul(bank[7][:, 0:2], ones[:, :], totals[:, :], start=True, stop=True).then_inc(gamma_total, 1)
                for k in range(2):
                    pe.wait_ge(ternary_ready, k + 1)
                    for c in range(4):
                        last = pe.transpose(bank[2 + k][:, c * D:(c + 1) * D], ternary[:, k, c, :], core.ident[:, :])
                    last.then_inc(ffn0_turned, 1)
                pe.wait_ge(scaled_ready, 1)
                for k in range(3):
                    for c in range(3):
                        last = pe.transpose(bank[4 + k][:, c * D:(c + 1) * D], scaled[:, k, c, :], core.ident[:, :])
                last.then_inc(ffn1_turned, 1)


def attention(nc, core, layer, x_dram, scratch):
    n = core.n
    first = layer == 0
    sides = 2 if first else 1
    scale = float(1.0 / np.sqrt(np.float32(HD))) if first else 1.0
    half_heads = HEADS // 2
    s1 = core.bank[0:2]
    s2 = core.bank[2:4]
    pv = core.bank[4:6]
    m0, m1 = core.bank[6], core.bank[7]
    groups = HEADS // 4

    with ExitStack() as ctx:
        def sb(name, shape, dt=FP32):
            return ctx.enter_context(nc.sbuf_tensor(f"{name}_{layer}", shape, dt))

        def sem(name):
            return core.sem(f"{name}_{layer}")

        x_in = [sb(f"x_in{k}", [P, TILES, D]) for k in range(2)]
        x_t = [sb(f"x_t{k}", [P, TOK]) for k in range(2)]
        turned = sb("turned", [P, sides, 2, TOK])
        exact = sb("exact", [P, sides, TOK])
        rest = sb("rest", [P, sides, TOK])
        parts = sb("parts", [P, 3, sides, TOK], BF16)
        shifts = sb("shifts", [P, TILES, 2, half_heads], BF16)
        shift_rows = [sb(f"shift_rows{k}", [half_heads, TOK], BF16) for k in range(2)]
        probs = sb("probs", [P, RING, TILES, TOK])
        added = sb("added", [P, TILES, D]) if first else None
        y = sb("y", [P, TILES, D])
        stats = sb("stats", [P, TILES, 6])
        moments = sb("moments", [P, TILES, 2])
        shifted_var = sb("shifted_var", [P, TILES])
        rstd = sb("rstd", [P, TILES])
        o_t = sb("o_t", [P, TOK])
        if first:
            values = [sb(f"values{k}", [P, TILES, HEADS, VW]) for k in range(2)]
            heads_t = [sb(f"heads_t{k}", [P, groups, TOK]) for k in range(2)]
            recips = sb("recips", [P, 2, TILES, half_heads])
            o = sb("o", [P, TILES, D])
        else:
            v_in = sb("v_in", [P, TILES, D])
            values = [sb(f"values{k}", [P, TILES, HEADS, D + 1]) for k in range(2)]
            recips = sb("recips", [P, 2, TILES])
            o_sum = [sb(f"o_sum{k}", [P, TILES, D]) for k in range(2)]

        ones_ready = sem("ones_ready")
        x_loaded = [sem(f"x_loaded{k}") for k in range(2)]
        xt_in_psum = sem("xt_in_psum")
        xt_ready = sem("xt_ready")
        qk_in_psum = sem("qk_in_psum")
        qk_taken = sem("qk_taken")
        exact_ready = sem("exact_ready")
        part0_ready = sem("part0_ready")
        rest_ready = sem("rest_ready")
        part1_ready = sem("part1_ready")
        var_ready = sem("var_ready")
        parts_ready = sem("parts_ready")
        parts_written = sem("parts_written")
        stacked = [sem(f"stacked{k}") for k in range(2)]
        v_in_psum = sem("v_in_psum")
        v_taken = sem("v_taken")
        values_ready = sem("values_ready")
        max_in_psum = sem("max_in_psum")
        max_done = sem("max_done")
        shifts_in_psum = sem("shifts_in_psum")
        shift_rows_ready = sem("shift_rows_ready")
        shifted = [sem(f"shifted{k}") for k in range(2)]
        s_in_psum = sem("s_in_psum")
        exp_done = sem("exp_done")
        pv_done = sem("pv_done")
        pv_taken = sem("pv_taken")
        heads_in_psum = sem("heads_in_psum")
        recips_ready = sem("recips_ready")
        o_ready = sem("o_ready")
        ot_in_psum = sem("ot_in_psum")
        ot_ready = sem("ot_ready")
        out_in_psum = sem("out_in_psum")
        added_ready = sem("added_ready")
        y_ready = sem("y_ready")
        stats_ready = sem("stats_ready")
        moments_ready = sem("moments_ready")
        rstd_ready = sem("rstd_ready")
        x_ready = sem("x_ready")

        def stack_rows(parity):
            return slice(parity * HEAD_ROWS, (parity + 1) * HEAD_ROWS)

        with nc.Block() as block:
            @block.sync
            def _(sp):
                source = x_dram.rearrange("b (t p) d -> b p t d", p=P) if first else None

                def shift_rows_in(b, hf):
                    wait_apart(sp, shift_rows_ready, b.number() * 2 + (hf + 1))
                    for parity in range(2):
                        sp.dma_start(core.q_stack[b.odd][SHIFT_ROW:SHIFT_ROW + 1, parity, 4 * hf:4 * hf + 4, :].rearrange("q r n -> q (r n)"),
                                     shift_rows[hf][4 * parity:4 * parity + 4, :]).then_inc(shifted[hf], 16)

                def stack_in(b, i, on, hf):
                    if on(0):
                        wait_apart(sp, s_in_psum, i.number() * HEADS + half_heads * (hf + 1))
                    prs = slice(4 * hf, 4 * hf + 4)
                    for parity in range(2):
                        for side, to in ((0, core.k_stack[b.odd][stack_rows(parity), prs, :]),
                                         (1, core.q_stack[b.odd][stack_rows(parity), parity, prs, :])):
                            src = scratch[side, :, parity * 64:(parity + 1) * 64, :].rearrange(
                                "s (d r) n -> s d r n", r=PAIRS)[:, :, prs, :].rearrange("s d r n -> s d (r n)")
                            sp.dma_start(to.rearrange("q r n -> q (r n)"), src).then_inc(stacked[hf], 16)

                def step(i, on):
                    if on(4):
                        b = i.plus(4)
                        wait_apart(sp, xt_in_psum, times(i, 2, n))
                        src = source[b.number(), :, :, :] if first else core.xh_all[:, b.number(), :, :]
                        sp.dma_start(x_in[b.odd][:, :, :], src).then_inc(x_loaded[b.odd], 16)
                    if on(0):
                        shift_rows_in(i, 1)
                    if on(2):
                        b = i.plus(2)
                        wait_apart(sp, parts_ready, times(i, 2, n))
                        wait_apart(sp, stacked[0], times(i, 1, n) * 64)
                        wait_apart(sp, stacked[1], times(i, 1, n) * 64)
                        for s, m in RUNS:
                            k = K_PART[s]
                            src = parts[:, k:k + 1, sides - 1, :]
                            if m > 1:
                                src = src.broadcast_to([P, m, TOK])
                            sp.dma_start(scratch[0, s:s + m, :, :].rearrange("s r n -> r s n"), src).then_inc(parts_written, 16)
                            sp.dma_start(scratch[1, s:s + m, :, :].rearrange("s r n -> r s n"),
                                         parts[:, Q_PART[s]:Q_PART[s] + m, 0, :]).then_inc(parts_written, 16)
                        wait_apart(sp, parts_written, times(i, 2, n) * (32 * len(RUNS)))
                        stack_in(b, i, on, 0)
                    if on(1):
                        shift_rows_in(i.plus(1), 0)
                    if on(2):
                        stack_in(i.plus(2), i, on, 1)

                steps(sp, n, 4, 0, step)

            @block.gpsimd
            def _(pool):
                def step(i, on):
                    if on(2):
                        split(i)
                    if first and on(-1):
                        b = i.plus(-1)
                        pool.wait_ge(core.x_all_loaded, 16 * core.x_all_loads)
                        wait(pool, y_ready, times(i, -2, n))
                        pool.tensor_tensor(added[:, :, :], core.x_all[:, b.number(), :, :],
                                           core.b0_out[:, :].unsqueeze(1).broadcast_to([P, TILES, D]),
                                           op=ALU.add).then_inc(added_ready, 1)
                    if not first and on(1):
                        b = i.plus(1)
                        pool.wait_ge(v_taken, times(i, 1, n))
                        wait(pool, pv_done, times(i, -1, n) * HEADS)
                        for t in range(TILES):
                            pool.tensor_tensor(values[b.odd][:, t, :, 0:D], core.mix[:, :, :],
                                               v_in[:, t, :].unsqueeze(1).broadcast_to([P, HEADS, D]),
                                               op=ALU.mult).then_inc(values_ready, 1)
                    if on(-1):
                        pool.wait_ge(moments_ready, times(i, -1, n) * TILES)
                        pool.tensor_tensor(shifted_var[:, :], moments[:, :, 1], core.ln_shift[:, 0, :], op=ALU.add).then_inc(var_ready, 1)
                        pool.wait_ge(var_ready, times(i, -1, n))
                        pool.tensor_tensor(rstd[:, :], shifted_var[:, :], core.minus_half[:, 0, :], op=ALU.pow).then_inc(rstd_ready, 1)

                def split(i):
                    zeros = core.zeros[:, :].unsqueeze(1).broadcast_to([P, sides, TOK])
                    pool.wait_ge(qk_taken, times(i, 2, n) * sides)
                    if first:
                        pool.tensor_tensor(exact[:, :, :], turned[:, :, 0, :], turned[:, :, 1, :], op=ALU.add).then_inc(exact_ready, 1)
                        pool.wait_ge(exact_ready, times(i, 2, n))
                    wait(pool, parts_written, times(i, 1, n) * (32 * len(RUNS)))
                    pool.tensor_tensor(parts[:, 0, :, :], exact[:, :, :], zeros, op=ALU.add).then_inc(part0_ready, 1)
                    pool.wait_ge(part0_ready, times(i, 2, n))
                    pool.tensor_tensor(rest[:, :, :], exact[:, :, :], parts[:, 0, :, :], op=ALU.subtract).then_inc(rest_ready, 1)
                    pool.wait_ge(rest_ready, times(i, 2, n))
                    pool.tensor_tensor(parts[:, 1, :, :], rest[:, :, :], zeros, op=ALU.add).then_inc(part1_ready, 1)
                    pool.wait_ge(part1_ready, times(i, 2, n))
                    pool.tensor_tensor(parts[:, 2, :, :], rest[:, :, :], parts[:, 1, :, :], op=ALU.subtract).then_inc(parts_ready, 1)

                steps(pool, n, 2, 1, step)

            @block.scalar
            def _(act):
                def shift_rows_out(b, hf):
                    act.wait_ge(shifts_in_psum, b.number() * 2 + (hf + 1))
                    wait(act, shifted[hf], b.number() * 32)
                    act.activation(shift_rows[hf][:, :], m0[:, :].bitcast(BF16)[0:half_heads, 0:TOK], ACT.Copy).then_inc(shift_rows_ready, 1)

                def take_heads(b, g):
                    act.wait_ge(pv_done, b.number() * groups + (g + 1))
                    act.activation(heads_t[b.odd][:, g, :], pv[g % 2][:, 0:TOK], ACT.Copy).then_inc(pv_taken, 1)

                def step(i, on):
                    for s in range(HEADS):
                        if s == SHIFTS1 and on(0):
                            shift_rows_out(i, 1)
                        if s == 2 and first and on(-1):
                            take_heads(i.plus(-1), 3)
                        if s == V_SLOT + 1 and on(1):
                            b = i.plus(1)
                            act.wait_ge(v_in_psum, times(i, 1, n))
                            if first:
                                wait(act, pv_done, times(i, -1, n) * groups)
                                act.activation(values[b.odd][:, :, :, 0:HD],
                                               m1[:, 0:TOK].rearrange("p (t h d) -> p t h d", t=TILES, d=HD),
                                               ACT.Copy).then_inc(v_taken, 1)
                            else:
                                wait(act, values_ready, times(i, 0, n) * TILES)
                                act.activation(v_in[:, :, :].rearrange("p t d -> p (t d)"), m1[:, 0:TOK], ACT.Copy).then_inc(v_taken, 1)
                        if s in (6, 10, 14) and first and on(0):
                            take_heads(i, (s - 6) // 4)
                        if s == OT_SLOT and on(-1):
                            act.wait_ge(ot_in_psum, times(i, -1, n))
                            act.activation(o_t[:, :], m1[:, 0:TOK], ACT.Copy).then_inc(ot_ready, 1)
                        if s == SHIFTS0 and on(1):
                            shift_rows_out(i.plus(1), 0)
                        if s == XT_SLOT and on(3):
                            b = i.plus(3)
                            act.wait_ge(xt_in_psum, times(i, 3, n))
                            if first:
                                act.activation(x_t[b.odd][:, :], m1[:, 0:TOK], ACT.Copy).then_inc(xt_ready, 1)
                            else:
                                act.activation(x_t[b.odd][:, :], m1[:, 0:TOK], ACT.Identity, scale=core.cols[:, 8:9],
                                               bias=core.cols[:, 9:10]).then_inc(xt_ready, 1)
                        if on(0):
                            act.wait_ge(s_in_psum, i.number() * HEADS + (s + 1))
                            if first and s % 4 == 0:
                                wait(act, pv_done, i.number() * groups + (s // 4 - 1))
                            if not first:
                                wait(act, pv_done, i.number() * HEADS + (s + 1 - RING))
                            act.activation(probs[:, s % RING, :, :].rearrange("p t n -> p (t n)"), s2[s % 2][:, :], ACT.Exp,
                                           scale=scale).then_inc(exp_done, 1)

                steps(act, n, 3, 1, step)

            @block.vector
            def _(dve):
                def sum_head(b, h):
                    dve.wait_ge(recips_ready, b.number() * HEADS + (h + 1))
                    wait(dve, pv_taken, (b.number() * HEADS + h) * TILES)
                    for t in range(TILES):
                        part = pv[h % 2][:, t * (D + 1):t * (D + 1) + D]
                        if h == 0:
                            dve.tensor_scalar(o_sum[b.odd][:, t, :], part, recips[:, h % 2, t:t + 1], None,
                                              ALU.mult).then_inc(pv_taken, 1)
                        else:
                            dve.scalar_tensor_tensor(o_sum[b.odd][:, t, :], part, recips[:, h % 2, t:t + 1],
                                                     o_sum[b.odd][:, t, :], op0=ALU.mult, op1=ALU.add).then_inc(pv_taken, 1)

                def recip_head(b, h):
                    dve.wait_ge(pv_done, b.number() * HEADS + (h + 1))
                    sums = pv[h % 2][:, 0:TILES * (D + 1)].rearrange("p (t c) -> p t c", t=TILES)[:, :, D]
                    dve.reciprocal(recips[:, h % 2, :], sums).then_inc(recips_ready, 1)

                def step(i, on):
                    for s in range(HEADS):
                        lagged, h = (i, s - 3) if s >= 3 else (i.plus(-1), s + HEADS - 3)
                        summing = not first and (on(0) if s >= 3 else on(-1))
                        if summing:
                            recip_head(lagged, h)
                        if on(1):
                            b = i.plus(1)
                            hf, col = s // half_heads, s % 2 * 4 + s // 2 % 4
                            dve.wait_ge(max_in_psum, b.number() * HEADS + (s + 1))
                            dve.tensor_reduce(shifts[:, :, hf, col], s1[s % 2][:, :].rearrange("p (t n) -> p t n", t=TILES),
                                              op=ALU.max, axis=AX.X, negate=True).then_inc(max_done, 1)
                        if summing:
                            sum_head(lagged, h)
                        if first and s in (Q_SLOT, K_SLOT) and on(3):
                            side = int(s == K_SLOT)
                            dve.wait_ge(qk_in_psum, times(i, 2, n) * 2 + (side + 1))
                            wait(dve, exact_ready, times(i, 2, n))
                            dve.tensor_tensor(turned[:, side, :, :], (m1, m0)[side][:, :].rearrange("p (v n) -> p v n", v=2),
                                              core.rope[:, :, :], op=ALU.mult).then_inc(qk_taken, 1)
                        if not first and s == Q_SLOT and on(3):
                            dve.wait_ge(qk_in_psum, times(i, 3, n))
                            wait(dve, rest_ready, times(i, 2, n))
                            dve.tensor_copy(exact[:, 0, :], m1[:, 0:TOK]).then_inc(qk_taken, 1)
                        for k, slot in enumerate((HEADS0, HEADS1)):
                            heads = (m0, m1)[k][:, :].rearrange("p (t h c) -> p t h c", t=TILES, c=VW)
                            if first and s == slot and on(-1):
                                dve.wait_ge(heads_in_psum, times(i, -2, n) * 2 + (k + 1))
                                dve.reciprocal(recips[:, k, :, :], heads[:, :, :, HD]).then_inc(recips_ready, 1)
                            if first and s == slot + 1 and on(-1):
                                dve.wait_ge(recips_ready, times(i, -2, n) * 2 + (k + 1))
                                dve.tensor_tensor(o[:, :, k * 64:(k + 1) * 64].rearrange("p t (h d) -> p t h d", d=HD),
                                                  heads[:, :, :, 0:HD],
                                                  recips[:, k, :, :].unsqueeze(3).broadcast_to([P, TILES, half_heads, HD]),
                                                  op=ALU.mult).then_inc(o_ready, 1)
                        if s == Y_SLOT and on(-1):
                            b = i.plus(-1)
                            wait(dve, x_ready, times(i, -2, n) * TILES)
                            if first:
                                dve.wait_ge(added_ready, times(i, -1, n))
                            dve.wait_ge(out_in_psum, times(i, -1, n))
                            dve.tensor_tensor(y[:, :, :], m1[:, 0:TOK].rearrange("p (t d) -> p t d", t=TILES),
                                              added[:, :, :] if first else core.x_all[:, b.number(), :, :],
                                              op=ALU.add).then_inc(y_ready, 1)
                        if s == Y_SLOT + 1 and on(-1):
                            wait_apart(dve, y_ready, times(i, -1, n))
                            for t in range(TILES):
                                dve.bn_stats(stats[:, t, :], y[:, t, :]).then_inc(stats_ready, 1)
                        if s == Y_SLOT + 2 and on(-1):
                            wait_apart(dve, var_ready, times(i, -2, n))
                            wait_apart(dve, stats_ready, times(i, -1, n) * TILES)
                            for t in range(TILES):
                                dve.bn_aggr(moments[:, t, :], stats[:, t, :]).then_inc(moments_ready, 1)
                    if on(-1):
                        b = i.plus(-1)
                        dve.wait_ge(rstd_ready, times(i, -1, n))
                        dve.wait_ge(moments_ready, times(i, -1, n) * TILES)
                        for t in range(TILES):
                            dve.tensor_scalar(core.x_all[:, b.number(), t, :], y[:, t, :], moments[:, t, 0:1], rstd[:, t:t + 1],
                                              ALU.subtract, ALU.mult).then_inc(x_ready, 1)

                for v in values:
                    if first:
                        dve.memset(v[:, :, :, HD:VW], 0.0).then_inc(ones_ready, 1)
                    else:
                        dve.memset(v[:, :, :, D:D + 1], 1.0).then_inc(ones_ready, 1)
                if first:
                    for k, v in enumerate(values):
                        dve.wait_ge(ones_ready, k + 1)
                        dve.memset(v[:, :, :, HD:HD + 1], 1.0).then_inc(ones_ready, 1)
                steps(dve, n, 3, 1, step)

            @block.tensor
            def _(pe):
                def shifts_turned(b, hf):
                    pe.wait_ge(max_done, b.number() * HEADS + half_heads * (hf + 1))
                    for t in range(TILES):
                        last = pe.transpose(m0[:, :].bitcast(BF16)[0:half_heads, t * P:(t + 1) * P], shifts[:, t, hf, :],
                                            core.ident_bf[:, :])
                    last.then_inc(shifts_in_psum, 1)

                def products_by_group(b, g):
                    if g == 0:
                        pe.wait_ge(v_taken, b.number() + 1)
                    pe.wait_ge(exp_done, b.number() * HEADS + 4 * (g + 1))
                    wait(pe, pv_taken, b.number() * groups + (g - 1))
                    for t in range(TILES):
                        for a in range(4):
                            h = 4 * g + a
                            last = pe.matmul(pv[g % 2][VW * a:VW * (a + 1), 0:TOK], values[b.odd][:, t, h, :],
                                             probs[:, h % RING, t, :], start=(t == 0), stop=(t == TILES - 1),
                                             skip_group_check=True)
                    last.then_inc(pv_done, 1)

                def products_of_head(b, h):
                    if h == 0:
                        pe.wait_ge(values_ready, b.number() * TILES + TILES)
                    pe.wait_ge(exp_done, b.number() * HEADS + (h + 1))
                    wait(pe, pv_taken, (b.number() * HEADS + (h - 1)) * TILES)
                    for q in range(TILES):
                        for t in range(TILES):
                            last = pe.matmul(pv[h % 2][:, q * (D + 1):(q + 1) * (D + 1)], probs[:, h % RING, t, q * P:(q + 1) * P],
                                             values[b.odd][:, t, h, :], start=(t == 0), stop=(t == TILES - 1))
                    last.then_inc(pv_done, 1)

                def step(i, on):
                    for s in range(HEADS):
                        if s == SHIFTS1 and on(0):
                            pe.wait_ge(shift_rows_ready, i.number() * 2 + 1)
                            if first:
                                wait(pe, qk_taken, times(i, 2, n) * 2)
                            shifts_turned(i, 1)
                        if s == V_SLOT and on(1):
                            b = i.plus(1)
                            wait(pe, qk_taken, times(i, 2, n) * sides - (sides - 1))
                            wait(pe, y_ready, times(i, -2, n))
                            w_v = core.w0_v[:, :] if first else core.w1_kv[:, 1, :]
                            for t in range(TILES):
                                last = pe.matmul(m1[:, t * P:(t + 1) * P], x_t[b.odd][:, t * P:(t + 1) * P], w_v,
                                                 start=True, stop=True)
                            last.then_inc(v_in_psum, 1)
                        if first and s in (HEADS0, HEADS1) and on(-1):
                            b = i.plus(-1)
                            k = int(s == HEADS1)
                            pe.wait_ge(pv_taken, times(i, -1, n) * groups)
                            if k == 0:
                                wait(pe, shift_rows_ready, times(i, 0, n) * 2)
                            else:
                                wait(pe, v_taken, times(i, 1, n))
                                wait(pe, y_ready, times(i, -2, n))
                            for t in range(TILES):
                                for g in range(2):
                                    last = pe.transpose((m0, m1)[k][:, (2 * t + g) * P:(2 * t + g + 1) * P],
                                                        heads_t[b.odd][:, 2 * k + g, t * P:(t + 1) * P], core.ident[:, :])
                            last.then_inc(heads_in_psum, 1)
                        if s == OT_SLOT and on(-1):
                            b = i.plus(-1)
                            if first:
                                pe.wait_ge(o_ready, times(i, -1, n) * 2)
                            else:
                                pe.wait_ge(pv_taken, times(i, -1, n) * (HEADS * TILES))
                                wait(pe, v_taken, times(i, 1, n))
                                wait(pe, y_ready, times(i, -2, n))
                            for t in range(TILES):
                                src = o[:, t, :] if first else o_sum[b.odd][:, t, :]
                                last = pe.transpose(m1[:, t * P:(t + 1) * P], src, core.ident[:, :])
                            last.then_inc(ot_in_psum, 1)
                        if s == SHIFTS0 and on(1):
                            if first:
                                wait(pe, o_ready, times(i, -1, n) * 2 - 1)
                                wait(pe, qk_taken, times(i, 2, n) * 2)
                            wait(pe, shift_rows_ready, times(i, 0, n) * 2)
                            shifts_turned(i.plus(1), 0)
                        if s == OUT_SLOT and on(-1):
                            pe.wait_ge(ot_ready, times(i, -1, n))
                            w_out = core.w0_out if first else core.w1_out
                            for t in range(TILES):
                                last = pe.matmul(m1[:, t * P:(t + 1) * P], o_t[:, t * P:(t + 1) * P], w_out[:, :],
                                                 start=True, stop=True)
                            last.then_inc(out_in_psum, 1)
                        if s == XT_SLOT and on(3):
                            b = i.plus(3)
                            pe.wait_ge(x_loaded[b.odd], (b.half + 1) * 16)
                            wait(pe, y_ready, times(i, -1, n))
                            wait(pe, qk_taken, times(i, 2, n) * sides)
                            wait(pe, v_taken, times(i, 1, n))
                            for t in range(TILES):
                                last = pe.transpose(m1[:, t * P:(t + 1) * P], x_in[b.odd][:, t, :], core.ident[:, :])
                            last.then_inc(xt_in_psum, 1)
                        if s in (Q_SLOT, K_SLOT)[:sides] and on(3):
                            b = i.plus(3)
                            side = int(s == K_SLOT)
                            if side == 0:
                                pe.wait_ge(xt_ready, times(i, 3, n))
                            else:
                                if on(1):
                                    pe.wait_ge(shift_rows_ready, i.plus(1).number() * 2 + 1)
                                wait(pe, qk_taken, times(i, 2, n) * 2)
                            if first:
                                for v in range(2):
                                    last = pe.matmul((m1, m0)[side][:, v * TOK:(v + 1) * TOK], core.w0_qk[:, side, v, :],
                                                     x_t[b.odd][:, :], start=True, stop=True)
                            else:
                                last = pe.matmul(m1[:, 0:TOK], core.w1_qk[:, :], x_t[b.odd][:, :], start=True, stop=True)
                            last.then_inc(qk_in_psum, 1)
                        if on(0):
                            b = i
                            if s % half_heads == 0:
                                pe.wait_ge(shifted[s // half_heads], b.number() * 32 + 32)
                            wait(pe, exp_done, b.number() * HEADS + (s - 1))
                            for t in range(TILES):
                                last = pe.matmul(s2[s % 2][:, t * TOK:(t + 1) * TOK],
                                                 core.k_stack[b.odd][0:SHIFT_ROW + 1, s // 2, t * P:(t + 1) * P],
                                                 core.q_stack[b.odd][0:SHIFT_ROW + 1, s % 2, s // 2, :], start=True, stop=True)
                            last.then_inc(s_in_psum, 1)
                        if on(1):
                            b = i.plus(1)
                            if s % half_heads == 0:
                                pe.wait_ge(stacked[s // half_heads], b.number() * 64 + 64)
                            wait(pe, max_done, b.number() * HEADS + (s - 1))
                            for t in range(TILES):
                                last = pe.matmul(s1[s % 2][:, t * TOK:(t + 1) * TOK],
                                                 core.q_stack[b.odd][0:PAIR_ROWS, s % 2, s // 2, t * P:(t + 1) * P],
                                                 core.k_stack[b.odd][0:PAIR_ROWS, s // 2, :], start=True, stop=True)
                            last.then_inc(max_in_psum, 1)
                        if first:
                            if s == 1 and on(-1):
                                products_by_group(i.plus(-1), 3)
                            if s in (5, 9, 13) and on(0):
                                products_by_group(i, (s - 5) // 4)
                        elif s >= 2:
                            if on(0):
                                products_of_head(i, s - 2)
                        elif on(-1):
                            products_of_head(i.plus(-1), s + HEADS - 2)

                pe.wait_ge(ones_ready, 4 if first else 2)
                steps(pe, n, 3, 1, step)


def ffn0(nc, core):
    n = core.n
    chunks = 4
    xt_bank, out_bank = core.bank[0], core.bank[5]
    up_banks = (core.bank[1:3], core.bank[6:8])
    turn_banks = core.bank[3:5]

    with ExitStack() as ctx:
        def sb(name, shape, dt=FP32):
            return ctx.enter_context(nc.sbuf_tensor(f"{name}_f0", shape, dt))

        def sem(name):
            return core.sem(f"{name}_f0")

        x_in = [sb(f"x_in{k}", [P, TILES, D]) for k in range(2)]
        x_t = [sb(f"x_t{k}", [P, TOK]) for k in range(2)]
        h = [sb(f"h{k}", [P, TILES, chunks * D]) for k in range(2)]
        h_norm = [sb(f"h_norm{k}", [P, TILES, chunks * D]) for k in range(2)]
        h_t = sb("h_t", [P, chunks, TOK])
        y = sb("y", [P, TILES, D])
        h_stats, y_stats = (sb(f"{v}_stats", [P, TILES, 6]) for v in "hy")
        h_moments, y_moments = (sb(f"{v}_moments", [P, TILES, 2]) for v in "hy")
        h_var, h_rstd = sb("h_var", [P, TILES]), sb("h_rstd", [P, TILES])
        y_scaled, y_var, y_rstd = (sb(v, [P, 2, TILES]) for v in ("y_scaled", "y_var", "y_rstd"))

        x_loaded = [sem(f"x_loaded{k}") for k in range(2)]
        xt_in_psum = sem("xt_in_psum")
        xt_ready = sem("xt_ready")
        up_in_psum = sem("up_in_psum")
        h_ready = sem("h_ready")
        h_norm_ready = sem("h_norm_ready")
        turned_in_psum = sem("turned_in_psum")
        h_t_ready = sem("h_t_ready")
        out_in_psum = sem("out_in_psum")
        y_ready = sem("y_ready")
        y_scaled_ready = sem("y_scaled_ready")
        x_ready = sem("x_ready")
        h_sems, y_sems = ({k: sem(f"{v}_{k}") for k in ("stats", "moments", "var", "rstd")} for v in "hy")

        def measure(dve, before, used, sems, source, stats, moments):
            for t in range(TILES):
                dve.bn_stats(stats[:, t, :], source(t)).then_inc(sems["stats"], 1)
            wait_apart(dve, sems["var"], before)
            wait_apart(dve, *used)
            wait_apart(dve, sems["stats"], before * TILES + TILES)
            for t in range(TILES):
                dve.bn_aggr(moments[:, t, :], stats[:, t, :]).then_inc(sems["moments"], 1)

        with nc.Block() as block:
            @block.sync
            def _(sp):
                def step(i, on):
                    if on(4):
                        b = i.plus(4)
                        wait_apart(sp, xt_in_psum, times(i, 2, n))
                        sp.dma_start(x_in[b.odd][:, :, :], core.x_all[:, b.number(), :, :]).then_inc(x_loaded[b.odd], 16)

                steps(sp, n, 4, 0, step)

            @block.gpsimd
            def _(pool):
                def step(i, on):
                    if on(2):
                        pool.wait_ge(h_sems["moments"], times(i, 2, n) * TILES)
                        pool.tensor_tensor(h_var[:, :], h_moments[:, :, 1], core.ln_shift[:, 0, :], op=ALU.add).then_inc(h_sems["var"], 1)
                        pool.wait_ge(h_sems["var"], times(i, 2, n))
                        pool.tensor_tensor(h_rstd[:, :], h_var[:, :], core.minus_half[:, 0, :], op=ALU.pow).then_inc(h_sems["rstd"], 1)
                    if on(0):
                        pool.wait_ge(y_sems["moments"], times(i, 0, n) * TILES)
                        pool.tensor_tensor(y_scaled[:, :, :], y_moments[:, :, 1].unsqueeze(1).broadcast_to([P, 2, TILES]),
                                           core.ln_scale[:, :, :], op=ALU.mult).then_inc(y_scaled_ready, 1)
                        pool.wait_ge(y_scaled_ready, times(i, 0, n))
                        pool.tensor_tensor(y_var[:, :, :], y_scaled[:, :, :], core.ln_shift[:, :, :], op=ALU.add).then_inc(y_sems["var"], 1)
                        pool.wait_ge(y_sems["var"], times(i, 0, n))
                        pool.tensor_tensor(y_rstd[:, :, :], y_var[:, :, :], core.minus_half[:, :, :], op=ALU.pow).then_inc(y_sems["rstd"], 1)

                steps(pool, n, 2, 0, step)

            @block.scalar
            def _(act):
                def step(i, on):
                    if on(3):
                        b = i.plus(3)
                        act.wait_ge(xt_in_psum, times(i, 3, n))
                        wait(act, up_in_psum, times(i, 1, n) * TILES)
                        act.activation(x_t[b.odd][:, :], xt_bank[:, 0:TOK], ACT.Copy).then_inc(xt_ready, 1)
                    if on(0):
                        for c in range(chunks):
                            if c % 2 == 0:
                                act.wait_ge(turned_in_psum, times(i, -1, n) * 2 + (c // 2 + 1))
                            act.activation(h_t[:, c, :], turn_banks[c // 2][:, c % 2 * TOK:(c % 2 + 1) * TOK], ACT.Identity,
                                           scale=core.cols[:, c:c + 1], bias=core.cols[:, 4 + c:5 + c]).then_inc(h_t_ready, 1)
                    if on(2):
                        b = i.plus(2)
                        wait(act, h_norm_ready, times(i, 0, n) * TILES)
                        for t in range(TILES):
                            act.wait_ge(up_in_psum, times(i, 1, n) * TILES + (t + 1))
                            act.activation(h[b.odd][:, t, :], up_banks[b.odd][t][:, :], ACT.Gelu).then_inc(h_ready, 1)

                steps(act, n, 3, 0, step)

            @block.vector
            def _(dve):
                def step(i, on):
                    if on(1):
                        b = i.plus(1)
                        dve.wait_ge(h_sems["rstd"], times(i, 1, n))
                        dve.wait_ge(h_sems["moments"], times(i, 1, n) * TILES)
                        for t in range(TILES):
                            dve.tensor_scalar(h_norm[b.odd][:, t, :], h[b.odd][:, t, :], h_moments[:, t, 0:1], h_rstd[:, t:t + 1],
                                              ALU.subtract, ALU.mult).then_inc(h_norm_ready, 1)
                    if on(-1):
                        b = i.plus(-1)
                        dve.wait_ge(y_sems["rstd"], times(i, -1, n))
                        dve.wait_ge(y_sems["moments"], times(i, -1, n) * TILES)
                        for k, to in enumerate((core.x_all, core.xh_all)):
                            for t in range(TILES):
                                dve.tensor_scalar(to[:, b.number(), t, :], y[:, t, :], y_moments[:, t, 0:1],
                                                  y_rstd[:, k, t:t + 1], ALU.subtract, ALU.mult).then_inc(x_ready, 1)
                    if on(2):
                        b = i.plus(2)
                        wait_apart(dve, h_ready, times(i, 2, n) * TILES)
                        measure(dve, times(i, 1, n), (h_norm_ready, times(i, 1, n) * TILES), h_sems,
                                lambda t: h[b.odd][:, t, :], h_stats, h_moments)
                    if on(0):
                        wait(dve, x_ready, times(i, -1, n) * (2 * TILES))
                        dve.wait_ge(out_in_psum, times(i, 0, n))
                        dve.tensor_tensor(y[:, :, :], out_bank[:, 0:TOK].rearrange("p (t d) -> p t d", t=TILES),
                                          core.x_all[:, i.number(), :, :], op=ALU.add).then_inc(y_ready, 1)
                        wait_apart(dve, y_ready, times(i, 0, n))
                        measure(dve, times(i, -1, n), (x_ready, times(i, -1, n) * (2 * TILES)), y_sems,
                                lambda t: y[:, t, :], y_stats, y_moments)

                steps(dve, n, 2, 1, step)

            @block.tensor
            def _(pe):
                def step(i, on):
                    if on(3):
                        b = i.plus(3)
                        pe.wait_ge(x_loaded[b.odd], (b.half + 1) * 16)
                        wait(pe, xt_ready, times(i, 2, n))
                        for t in range(TILES):
                            last = pe.transpose(xt_bank[:, t * P:(t + 1) * P], x_in[b.odd][:, t, :], core.ident[:, :])
                        last.then_inc(xt_in_psum, 1)
                    if on(0):
                        pe.wait_ge(h_norm_ready, times(i, 0, n) * TILES)
                        wait(pe, h_t_ready, times(i, -1, n) * chunks)
                        for k in range(2):
                            for c in range(2):
                                for t in range(TILES):
                                    last = pe.transpose(turn_banks[k][:, (2 * c + t) * P:(2 * c + t + 1) * P],
                                                        h_norm[i.odd][:, t, (2 * k + c) * D:(2 * k + c + 1) * D],
                                                        core.ident[:, :])
                            last.then_inc(turned_in_psum, 1)
                    if on(2):
                        b = i.plus(2)
                        pe.wait_ge(xt_ready, times(i, 2, n))
                        wait(pe, h_ready, times(i, 0, n) * TILES)
                        for t in range(TILES):
                            pe.matmul(up_banks[b.odd][t][:, :], x_t[b.odd][:, t * P:(t + 1) * P],
                                      core.w0_fc[:, :, :].rearrange("p c d -> p (c d)"), start=True, stop=True).then_inc(up_in_psum, 1)
                    if on(0):
                        pe.wait_ge(h_t_ready, times(i, 0, n) * chunks)
                        wait(pe, y_ready, times(i, -1, n))
                        for t in range(TILES):
                            for c in range(chunks):
                                last = pe.matmul(out_bank[:, t * P:(t + 1) * P], h_t[:, c, t * P:(t + 1) * P],
                                                 core.w0_proj[:, c, :], start=(c == 0), stop=(c == chunks - 1))
                        last.then_inc(out_in_psum, 1)

                steps(pe, n, 3, 0, step)


def ffn1(nc, core, out):
    n = core.n
    chunks = 3
    xt_bank, out_bank = core.bank[0], core.bank[4]
    up_banks = (core.bank[1:4], core.bank[5:8])
    out_v = out.rearrange("b (t p) d -> b p t d", p=P)

    with ExitStack() as ctx:
        def sb(name, shape, dt=FP32):
            return ctx.enter_context(nc.sbuf_tensor(f"{name}_f1", shape, dt))

        def sem(name):
            return core.sem(f"{name}_f1")

        x_in = [sb(f"x_in{k}", [P, TILES, D]) for k in range(2)]
        x_t = [sb(f"x_t{k}", [P, TOK]) for k in range(2)]
        gate = sb("gate", [P, chunks, TOK])
        h_t = [sb(f"h_t{k}", [P, chunks, TOK]) for k in range(2)]
        y = sb("y", [P, TILES, D])
        stats = sb("stats", [P, TILES, 6])
        moments = sb("moments", [P, TILES, 2])
        var = sb("var", [P, TILES])
        rstd = sb("rstd", [P, TILES])
        x_out = [sb(f"x_out{k}", [P, TILES, D]) for k in range(2)]

        x_loaded = [sem(f"x_loaded{k}") for k in range(2)]
        xt_in_psum = sem("xt_in_psum")
        xt_ready = sem("xt_ready")
        up_in_psum = sem("up_in_psum")
        gate_ready = sem("gate_ready")
        h_ready = sem("h_ready")
        out_in_psum = sem("out_in_psum")
        y_ready = sem("y_ready")
        stats_ready = sem("stats_ready")
        moments_ready = sem("moments_ready")
        var_ready = sem("var_ready")
        rstd_ready = sem("rstd_ready")
        x_out_ready = sem("x_out_ready")
        stored = [sem(f"stored{k}") for k in range(2)]

        with nc.Block() as block:
            @block.sync
            def _(sp):
                def step(i, on):
                    if on(3):
                        b = i.plus(3)
                        wait_apart(sp, xt_in_psum, times(i, 1, n))
                        sp.dma_start(x_in[b.odd][:, :, :], core.x_all[:, b.number(), :, :]).then_inc(x_loaded[b.odd], 16)
                    if on(-1):
                        b = i.plus(-1)
                        wait_apart(sp, x_out_ready, times(i, -1, n) * TILES)
                        sp.dma_start(out_v[b.number(), :, :, :], x_out[b.odd][:, :, :]).then_inc(stored[b.odd], 16)

                steps(sp, n, 3, 1, step)
                for k in range(2):
                    sp.wait_ge(stored[k], (n - k + 1) // 2 * 16)

            @block.gpsimd
            def _(pool):
                def step(i, on):
                    if on(0):
                        pool.wait_ge(moments_ready, times(i, 0, n) * TILES)
                        pool.tensor_tensor(var[:, :], moments[:, :, 1], core.ln_shift[:, 0, :], op=ALU.add).then_inc(var_ready, 1)
                        pool.wait_ge(var_ready, times(i, 0, n))
                        pool.tensor_tensor(rstd[:, :], var[:, :], core.minus_half[:, 0, :], op=ALU.pow).then_inc(rstd_ready, 1)

                steps(pool, n, 0, 0, step)

            @block.scalar
            def _(act):
                def step(i, on):
                    if on(2):
                        b = i.plus(2)
                        act.wait_ge(xt_in_psum, times(i, 2, n))
                        wait(act, up_in_psum, times(i, 0, n) * chunks)
                        act.activation(x_t[b.odd][:, :], xt_bank[:, 0:TOK], ACT.Copy).then_inc(xt_ready, 1)
                    if on(1):
                        b = i.plus(1)
                        wait(act, h_ready, times(i, 0, n) * chunks)
                        for c in range(chunks):
                            act.wait_ge(up_in_psum, times(i, 0, n) * chunks + (c + 1))
                            act.activation(gate[:, c, :], up_banks[b.odd][c][:, 0:TOK], ACT.Silu).then_inc(gate_ready, 1)

                steps(act, n, 2, 0, step)

            @block.vector
            def _(dve):
                def step(i, on):
                    if on(-1):
                        b = i.plus(-1)
                        dve.wait_ge(rstd_ready, times(i, -1, n))
                        dve.wait_ge(moments_ready, times(i, -1, n) * TILES)
                        wait(dve, stored[b.odd], b.half * 16)
                        for t in range(TILES):
                            dve.tensor_scalar(x_out[b.odd][:, t, :], y[:, t, :], moments[:, t, 0:1], rstd[:, t:t + 1],
                                              ALU.subtract, ALU.mult).then_inc(x_out_ready, 1)
                    if on(1):
                        b = i.plus(1)
                        for c in range(chunks):
                            dve.wait_ge(gate_ready, times(i, 0, n) * chunks + (c + 1))
                            dve.tensor_tensor(h_t[b.odd][:, c, :], up_banks[b.odd][c][:, TOK:2 * TOK], gate[:, c, :],
                                              op=ALU.mult).then_inc(h_ready, 1)
                    if on(0):
                        wait(dve, x_out_ready, times(i, -1, n) * TILES)
                        dve.wait_ge(out_in_psum, times(i, 0, n))
                        dve.tensor_tensor(y[:, :, :], out_bank[:, 0:TOK].rearrange("p (t d) -> p t d", t=TILES),
                                          core.x_all[:, i.number(), :, :], op=ALU.add).then_inc(y_ready, 1)
                        wait_apart(dve, y_ready, times(i, 0, n))
                        for t in range(TILES):
                            dve.bn_stats(stats[:, t, :], y[:, t, :]).then_inc(stats_ready, 1)
                        wait_apart(dve, var_ready, times(i, -1, n))
                        wait_apart(dve, stats_ready, times(i, 0, n) * TILES)
                        for t in range(TILES):
                            dve.bn_aggr(moments[:, t, :], stats[:, t, :]).then_inc(moments_ready, 1)

                steps(dve, n, 1, 1, step)

            @block.tensor
            def _(pe):
                def step(i, on):
                    if on(2):
                        b = i.plus(2)
                        pe.wait_ge(x_loaded[b.odd], (b.half + 1) * 16)
                        wait(pe, xt_ready, times(i, 1, n))
                        for t in range(TILES):
                            last = pe.transpose(xt_bank[:, t * P:(t + 1) * P], x_in[b.odd][:, t, :], core.ident[:, :])
                        last.then_inc(xt_in_psum, 1)
                    if on(1):
                        b = i.plus(1)
                        pe.wait_ge(xt_ready, times(i, 1, n))
                        wait(pe, h_ready, times(i, -1, n) * chunks)
                        for c in range(chunks):
                            pe.matmul(up_banks[b.odd][c][:, 0:TOK], core.w1_gate[:, c, :], x_t[b.odd][:, :], start=True, stop=True)
                            pe.matmul(up_banks[b.odd][c][:, TOK:2 * TOK], core.w1_up[:, c, :], x_t[b.odd][:, :],
                                      start=True, stop=True).then_inc(up_in_psum, 1)
                    if on(0):
                        pe.wait_ge(h_ready, times(i, 0, n) * chunks)
                        wait(pe, y_ready, times(i, -1, n))
                        for t in range(TILES):
                            for c in range(chunks):
                                last = pe.matmul(out_bank[:, t * P:(t + 1) * P], h_t[i.odd][:, c, t * P:(t + 1) * P],
                                                 core.w1_down[:, c, :], start=(c == 0), stop=(c == chunks - 1))
                        last.then_inc(out_in_psum, 1)

                steps(pe, n, 2, 0, step)


_WEIGHTS = {"w_qkv": "L0_attn_w_qkv", "w_out0": "L0_attn_w_out", "b_out": "L0_attn_b_out", "w_fc": "L0_ffn_W_fc",
            "ln_w": "L0_ffn_ln_w", "ln_b": "L0_ffn_ln_b", "w_proj": "L0_ffn_W_proj", "ln_g1": "L1_attn_ln_g",
            "ln_b1": "L1_attn_ln_b", "w_kv": "L1_attn_W_kv", "w_x": "L1_attn_W_x", "w_out1": "L1_attn_W_out",
            "w_gate": "L1_ffn_w_gate", "w_up": "L1_ffn_w_up", "w_down": "L1_ffn_w_down"}


def build(nc, x, weights, out):
    n = x.shape[0]
    scratch = nc.dram_tensor("score_parts", (2, SLOTS, P, TOK), BF16, kind="Internal").ap()
    w = dict(weights, x=x)
    w["rope"] = nc.inline_tensor(rope_tables(), name="rope_tables").ap()
    with ExitStack() as ctx:
        core = Core(nc, ctx, n)
        prepare(nc, core, w)
        attention(nc, core, 0, x, scratch)
        ffn0(nc, core)
        attention(nc, core, 1, None, scratch)
        ffn1(nc, core, out)


def kernel(**inputs):
    import numpy as _np
    import concourse.bacc as _bacc
    from concourse import mybir as _mybir
    from concourse.bass_utils import run_bass_kernel_spmd as _run

    nc = _bacc.Bacc("TRN2", target_bir_lowering=False, num_devices=1)
    arrays, aps = {}, {}
    for name in ["L0_attn_x", *_WEIGHTS.values()]:
        a = _np.ascontiguousarray(inputs[name])
        arrays[f"in_{name}"] = a
        aps[name] = nc.dram_tensor(f"in_{name}", a.shape, _mybir.dt.from_np(a.dtype), kind="ExternalInput").ap()
    shape = arrays["in_L0_attn_x"].shape
    out = nc.dram_tensor("out_x", shape, _mybir.dt.float32, kind="ExternalOutput").ap()
    build(nc, aps["L0_attn_x"], {k: aps[v] for k, v in _WEIGHTS.items()}, out)
    r = _run(nc, [arrays], core_ids=[0])
    return r.results[0]["out_x"]
```

```python
import numpy as np
import concourse.bass as bass
from concourse import mybir
from contextlib import ExitStack

FP32 = mybir.dt.float32
BF16 = mybir.dt.bfloat16
INT32 = mybir.dt.int32
ALU = mybir.AluOpType
ACT = mybir.ActivationFunctionType
AX = mybir.AxisListType

P = 128
D = 128
TOK = 256
TILES = TOK // P
HEADS = 16
HD = D // HEADS
PAIRS = HEADS // 2
BANK = 512
LN_EPS = 1e-5

K_PART = (0, 0, 0, 1, 1, 2)
Q_PART = (0, 1, 2, 0, 1, 0)
SLOTS = len(K_PART)
RUNS = ((0, 3), (3, 2), (5, 1))
HEAD_ROWS = SLOTS * HD
PAIR_ROWS = 2 * HEAD_ROWS
SHIFT_ROW = PAIR_ROWS
RING = 8
VW = 32



class Slots:

    def __init__(self, first):
        self.shifts1 = 2 if first else 1
        self.shifts0 = 11 if first else 9
        self.v = 14 if first else 4
        self.xt = 0 if first else 13
        self.q = 3 if first else 15
        self.k = 5 if first else None
        self.heads = (8, 6) if first else ()
        self.ot = 11 if first else 7
        self.out = 13 if first else 10
        self.norm, self.norm_lag = (2, 2) if first else (15, 1)
        self.split = 3 if first else 2


class Batch:

    def __init__(self, half, odd):
        self.half, self.odd = half, odd

    def plus(self, k):
        n = self.odd + k
        return Batch(self.half + n // 2 if n // 2 else self.half, n % 2)

    def number(self):
        return self.half * 2 + self.odd if self.odd else self.half * 2


def wait(eng, sem, count):
    if isinstance(count, int) and count <= 0:
        return
    eng.wait_ge(sem, count)


def wait_apart(eng, sem, count):
    if not isinstance(count, int):
        count = eng.to_reg(count)
        eng.wait_ge(sem, 1)
    wait(eng, sem, count)


FIRST = 2


def wait_for_x(sp, before, writes, b):
    if isinstance(b.half, int):
        sp.wait_ge(before.sems["x_ready"], (b.number() + 1) * writes)


class Phase:

    def __init__(self, core, name):
        self.n, self.core, self.name = core.n, core, name
        self.functions, self.sems = {}, {}

    def sem(self, name):
        self.sems[name] = self.core.sem(f"{name}_{self.name}")
        return self.sems[name]

    def engine(self, kind):
        def keep(function):
            self.functions[kind] = function
            return function
        return keep

    def begin(self, kind, eng):
        self.eng = eng
        self.step = self.functions[kind](eng)

    def at(self, *indices):
        for i in indices:
            self.step(Batch(i // 2, i % 2), lambda k, i=i: 0 <= i + k < self.n)

    def loop(self):
        with self.eng.Fori(FIRST // 2, (self.n - 4) // 2) as half:
            self.step(Batch(half, 0), lambda k: True)
            self.step(Batch(half, 1), lambda k: True)


def times(i, k, n):
    if isinstance(i.half, int):
        return max(0, min(n, 2 * i.half + i.odd + k + 1))
    assert i.odd + k + 1 > -2, "a loop's first step is 2 or later, and no wait is for less than one"
    return i.half * 2 + (i.odd + k + 1)


def rope_tables():
    inv = (1.0 / 10000.0 ** (np.arange(0, HD, 2, dtype=np.float32) / HD)).astype(np.float32)
    angle = np.outer(np.arange(TOK, dtype=np.float32), inv).astype(np.float32)
    table = np.zeros((2, HD, PAIRS, 2, TOK), np.float32)
    for d in range(HD):
        table[:, d, :, 0, :] = np.cos(angle[:, d // 2])
        table[:, d, :, 1, :] = np.sin(angle[:, d // 2]) * (1 if d % 2 else -1)
    return table.reshape(P, 2, TOK)


class Core:

    def __init__(self, nc, ctx, n):
        self.nc, self.ctx, self.n = nc, ctx, n
        sb = self.sb
        self.bank = [ctx.enter_context(nc.psum_tensor(f"bank{k}", [P, BANK], FP32)) for k in range(8)]
        self.x_all = sb("x_all", [P, n, TILES, D])
        self.x_all_loads = 4
        self.x_all_loaded = self.sem("x_all_loaded")
        self.xh_all = sb("xh_all", [P, n, TILES, D])
        self.ident = sb("ident", [P, P])
        self.ident_bf = sb("ident_bf", [P, P], BF16)
        self.w0_qk = sb("w0_qk", [P, 2, 2, D])
        self.w0_v = sb("w0_v", [P, D])
        self.w0_out = sb("w0_out", [P, D])
        self.b0_out = sb("b0_out", [P, D])
        self.rope = sb("rope", [P, 2, TOK])
        self.w0_fc = sb("w0_fc", [P, 4, D])
        self.w0_proj = sb("w0_proj", [P, 4, D])
        self.cols = sb("cols", [P, 10])
        self.w1_kv = sb("w1_kv", [P, 2, D])
        self.w1_qk = sb("w1_qk", [P, D])
        self.w1_out = sb("w1_out", [P, D])
        self.mix = sb("mix", [P, HEADS, D])
        self.w1_gate = sb("w1_gate", [P, 3, D])
        self.w1_up = sb("w1_up", [P, 3, D])
        self.w1_down = sb("w1_down", [P, 3, D])
        self.zeros = sb("zeros", [P, TOK])
        self.ln_scale = sb("ln_scale", [P, 2, TILES])
        self.ln_shift = sb("ln_shift", [P, 2, TILES])
        self.minus_half = sb("minus_half", [P, 2, TILES])
        self.k_stack = [sb(f"k_stack{k}", [P, PAIRS, TOK], BF16) for k in range(2)]
        self.q_stack = [sb(f"q_stack{k}", [P, 2, PAIRS, TOK], BF16) for k in range(2)]

    def sb(self, name, shape, dt=FP32):
        return self.ctx.enter_context(self.nc.sbuf_tensor(name, shape, dt))

    def sem(self, name):
        return self.ctx.enter_context(self.nc.semaphore(name))


def prepare(nc, core, w, ctx):
    bank = core.bank
    early, late = Phase(core, "early"), Phase(core, "late")

    def sb(name, shape, dt=FP32):
        return ctx.enter_context(nc.sbuf_tensor(name, shape, dt, side="right"))

    raw_qkv = sb("raw_qkv", [P, 3, D])
    raw_out = sb("raw_out", [P, D])
    raw_rows = sb("raw_rows", [10, D])
    raw_mix = sb("raw_mix", [1, HEADS * HEADS])
    raw_bias = sb("raw_bias", [1, D])
    raw_fc = sb("raw_fc", [P, 4, D])
    raw_proj = sb("raw_proj", [P, 4, D])
    raw_int = sb("raw_int", [P, 3, 3, D], INT32)
    scaled = sb("scaled", [P, 3, 3, D])
    below = sb("below", [P, 2, 4, D])
    ones = sb("ones", [P, P])
    totals = sb("totals", [P, 2])
    gamma = sb("gamma", [P, 2])
    bounds = sb("bounds", [P, 2, 2])

    load_attn = early.sem("load_attn")
    load_rope = early.sem("load_rope")
    ident_step = early.sem("ident_step")
    stacks_set = early.sem("stacks_set")
    ones_set = early.sem("ones_set")
    consts_ready = early.sem("consts_ready")
    attn_turned = early.sem("attn_turned")
    attn_taken = early.sem("attn_taken")
    load_ffn0 = late.sem("load_ffn0")
    load_ffn1 = late.sem("load_ffn1")
    load_rest = late.sem("load_rest")
    sums_ready = late.sem("sums_ready")
    gamma_total = late.sem("gamma_total")
    gamma_step = late.sem("gamma_step")
    below_ready = late.sem("below_ready")
    ternary_ready = late.sem("ternary_ready")
    scaled_ready = late.sem("scaled_ready")
    small_turned = late.sem("small_turned")
    ffn0_turned = late.sem("ffn0_turned")
    ffn1_turned = late.sem("ffn1_turned")
    late_taken = late.sem("late_taken")
    q_stacks_set = late.sem("q_stacks_set")

    @early.engine("sync")
    def _(sp):
        sp.dma_start(raw_qkv[:, :, :], w["w_qkv"].rearrange("(t e) d -> e t d", e=D)).then_inc(load_attn, 16)
        sp.dma_start(raw_out[:, :], w["w_out0"]).then_inc(load_attn, 16)
        sp.dma_start(core.rope[:, :, :], w["rope"]).then_inc(load_rope, 16)

    @late.engine("sync")
    def _(sp):
        sp.dma_start(raw_fc[:, :, :], w["w_fc"].rearrange("(c p) d -> p c d", p=P)).then_inc(load_ffn0, 16)
        sp.dma_start(raw_proj[:, :, :], w["w_proj"].rearrange("p (c d) -> p c d", c=4)).then_inc(load_ffn0, 16)
        sp.dma_start(core.w1_kv[:, :, :], w["w_kv"].rearrange("p (t e) -> p t e", t=2)).then_inc(load_rest, 16)
        sp.dma_start(core.w1_out[:, :], w["w_out1"]).then_inc(load_rest, 16)
        x = w["x"].rearrange("b (t p) d -> p (b t) d", p=P)
        to = core.x_all[:, :, :, :].rearrange("p b t d -> p (b t) d")
        tiles = core.n * TILES // core.x_all_loads
        for k in range(core.x_all_loads):
            sp.dma_start(to[:, k * tiles:(k + 1) * tiles, :], x[:, k * tiles:(k + 1) * tiles, :]).then_inc(core.x_all_loaded, 16)

    @early.engine("scalar")
    def _(act):
        pass

    @late.engine("scalar")
    def _(act):
        act.dma_start(raw_rows[0:4, :], w["ln_w"].rearrange("(c p) -> c p", p=P)).then_inc(load_rest, 16)
        act.dma_start(raw_rows[4:8, :], w["ln_b"].rearrange("(c p) -> c p", p=P)).then_inc(load_rest, 16)
        act.dma_start(raw_rows[8:9, :], w["ln_g1"].rearrange("(a p) -> a p", a=1)).then_inc(load_rest, 16)
        act.dma_start(raw_rows[9:10, :], w["ln_b1"].rearrange("(a p) -> a p", a=1)).then_inc(load_rest, 16)
        act.dma_start(raw_mix[:, :], w["w_x"].rearrange("(a g) h -> a (g h)", a=1)).then_inc(load_rest, 16)
        act.dma_start(raw_bias[:, :], w["b_out"].rearrange("(a p) -> a p", a=1)).then_inc(load_rest, 16)
        act.dma_start(raw_int[:, 0, :, :], w["w_gate"].rearrange("(c p) d -> p c d", p=P)).then_inc(load_ffn1, 16)
        act.dma_start(raw_int[:, 1, :, :], w["w_up"].rearrange("(c p) d -> p c d", p=P)).then_inc(load_ffn1, 16)
        act.dma_start(raw_int[:, 2, :, :], w["w_down"].rearrange("p (c d) -> p c d", c=3)).then_inc(load_ffn1, 16)

    @early.engine("gpsimd")
    def _(pool):
        pool.memset(core.ident[:, :], 0.0).then_inc(ident_step, 1)
        pool.wait_ge(ident_step, 1)
        pool.affine_select(out=core.ident[:, :], in_=core.ident[:, :], compare_op=ALU.not_equal, fill=1.0,
                           base=0, pattern=[[-1, P]], channel_multiplier=1).then_inc(ident_step, 1)
        pool.memset(core.zeros[:, :], 0.0).then_inc(stacks_set, 1)
        pieces = [(core.k_stack[k][:, :, :], 0.0) for k in range(2)]
        pieces += [(core.k_stack[k][SHIFT_ROW:SHIFT_ROW + 1, :, :], 1.0) for k in range(2)]
        for k, (piece, value) in enumerate(pieces):
            pool.wait_ge(stacks_set, k + 1)
            pool.memset(piece, value).then_inc(stacks_set, 1)
        pool.wait_ge(stacks_set, len(pieces) + 1)

    @late.engine("gpsimd")
    def _(pool):
        pass

    @early.engine("vector")
    def _(dve):
        dve.memset(ones[:, :], 1.0).then_inc(ones_set, 1)
        dve.memset(core.ln_scale[:, 0, :], 1.0)
        dve.memset(core.ln_scale[:, 1, :], 1.0 + LN_EPS)
        dve.memset(core.ln_shift[:, 0, :], LN_EPS)
        dve.memset(core.ln_shift[:, 1, :], LN_EPS * LN_EPS)
        dve.memset(core.minus_half[:, :, :], -0.5)
        dve.wait_ge(ident_step, 2)
        dve.tensor_copy(core.ident_bf[:, :], core.ident[:, :]).then_inc(consts_ready, 1)
        dve.wait_ge(attn_turned, 1)
        for side in range(2):
            turned = bank[0][:, side * D:(side + 1) * D].rearrange("p (r a d) -> p a d r", a=2, d=HD)
            dve.tensor_copy(core.w0_qk[:, side, 0, :].rearrange("p (a d r) -> p a d r", a=2, d=HD), turned)
            swapped = core.w0_qk[:, side, 1, :].rearrange("p (a c t r) -> p a c t r", a=2, c=HD // 2, t=2)
            source = bank[0][:, side * D:(side + 1) * D].rearrange("p (r a c t) -> p a c t r", a=2, c=HD // 2, t=2)
            for t in range(2):
                dve.tensor_copy(swapped[:, :, :, t, :], source[:, :, :, 1 - t, :])
        dve.tensor_copy(core.w0_v[:, :], bank[0][:, 2 * D:3 * D])
        dve.tensor_copy(core.w0_out[:, :], bank[0][:, 3 * D:4 * D]).then_inc(attn_taken, 1)
        dve.wait_ge(load_rope, 16)

    @late.engine("vector")
    def _(dve):
        for stack in core.q_stack:
            dve.memset(stack[:, :, :, :], 0.0).then_inc(q_stacks_set, 1)
        dve.wait_ge(small_turned, 1)
        dve.wait_ge(load_rest, 16 * 8)
        dve.tensor_copy(core.cols[:, :], bank[1][:, 0:10])
        dve.tensor_copy(core.b0_out[:, :], bank[1][:, 384:512])
        mixed = bank[1][:, 128:384].rearrange("p (g h) -> p h g", h=HEADS)
        for d in range(HD):
            dve.tensor_copy(core.mix[:, :, :].rearrange("p h (g d) -> p h g d", d=HD)[:, :, :, d], mixed)
        dve.tensor_copy(core.w1_qk[:, :].rearrange("p (a d r) -> p a d r", a=2, d=HD),
                        core.w1_kv[:, 0, :].rearrange("p (r a d) -> p a d r", a=2, d=HD))
        dve.wait_ge(load_ffn0, 32)
        for k, raw in enumerate((raw_fc, raw_proj)):
            dve.tensor_reduce(totals[:, k:k + 1], raw[:, :, :], op=ALU.add, axis=AX.XY,
                              apply_absolute_value=True).then_inc(sums_ready, 1)
        dve.wait_ge(load_ffn1, 48)
        dve.tensor_scalar(scaled[:, :, :, :].rearrange("p a c d -> p (a c d)"),
                          raw_int[:, :, :, :].rearrange("p a c d -> p (a c d)"), float(np.float32(1.0 / 127.0)), None,
                          ALU.mult).then_inc(scaled_ready, 1)
        dve.wait_ge(gamma_total, 1)
        dve.tensor_scalar(gamma[:, :], bank[0][:, 0:2], 1.0 / (4 * P * D), 1e-6,
                          ALU.mult, ALU.add).then_inc(gamma_step, 1)
        dve.wait_ge(gamma_step, 1)
        dve.tensor_scalar(bounds[:, 0, :], gamma[:, :], 0.5, None, ALU.mult).then_inc(gamma_step, 1)
        dve.tensor_scalar(bounds[:, 1, :], gamma[:, :], -0.5, None, ALU.mult).then_inc(gamma_step, 1)
        dve.wait_ge(gamma_step, 3)
        for k, raw in enumerate((raw_fc, raw_proj)):
            dve.tensor_scalar(below[:, k, :, :], raw[:, :, :], bounds[:, 1, k:k + 1], None,
                              ALU.is_lt).then_inc(below_ready, 1)
        for k, raw in enumerate((raw_fc, raw_proj)):
            dve.wait_ge(below_ready, k + 1)
            flat = raw[:, :, :].rearrange("p c d -> p (c d)")
            dve.scalar_tensor_tensor(flat, flat, bounds[:, 0, k:k + 1], below[:, k, :, :].rearrange("p c d -> p (c d)"),
                                     op0=ALU.is_gt, op1=ALU.subtract).then_inc(ternary_ready, 1)
        dve.wait_ge(ffn1_turned, 1)
        for k, to in enumerate((core.w1_gate, core.w1_up, core.w1_down)):
            dve.tensor_copy(to[:, :, :].rearrange("p c d -> p (c d)"), bank[(4, 5, 0)[k]][:, 0:3 * D])
        dve.wait_ge(ffn0_turned, 2)
        dve.tensor_copy(core.w0_fc[:, :, :].rearrange("p c d -> p (c d)"), bank[2][:, :])
        dve.tensor_copy(core.w0_proj[:, :, :].rearrange("p c d -> p (c d)"), bank[3][:, :]).then_inc(late_taken, 1)

    @early.engine("tensor")
    def _(pe):
        pe.wait_ge(ident_step, 2)
        pe.wait_ge(load_attn, 32)
        for t in range(3):
            pe.transpose(bank[0][:, t * D:(t + 1) * D], raw_qkv[:, t, :], core.ident[:, :])
        pe.transpose(bank[0][:, 3 * D:4 * D], raw_out[:, :], core.ident[:, :]).then_inc(attn_turned, 1)
        pe.wait_ge(consts_ready, 1)
        pe.wait_ge(attn_taken, 1)

    @late.engine("tensor")
    def _(pe):
        pe.wait_ge(ones_set, 1)
        pe.wait_ge(load_rest, 16 * 8)
        pe.transpose(bank[1][:, 0:10], raw_rows[:, :], core.ident[0:10, 0:10])
        pe.matmul(bank[1][:, 128:384], ones[0:1, :], raw_mix[:, :], start=True, stop=True)
        pe.matmul(bank[1][:, 384:512], ones[0:1, :], raw_bias[:, :], start=True, stop=True).then_inc(small_turned, 1)
        pe.wait_ge(sums_ready, 2)
        pe.matmul(bank[0][:, 0:2], ones[:, :], totals[:, :], start=True, stop=True).then_inc(gamma_total, 1)
        pe.wait_ge(scaled_ready, 1)
        pe.wait_ge(gamma_step, 1)
        for k in range(3):
            for c in range(3):
                last = pe.transpose(bank[(4, 5, 0)[k]][:, c * D:(c + 1) * D], scaled[:, k, c, :], core.ident[:, :])
        last.then_inc(ffn1_turned, 1)
        for k, raw in enumerate((raw_fc, raw_proj)):
            pe.wait_ge(ternary_ready, k + 1)
            for c in range(4):
                last = pe.transpose(bank[2 + k][:, c * D:(c + 1) * D], raw[:, c, :], core.ident[:, :])
            last.then_inc(ffn0_turned, 1)

    return early, late


def attention(nc, core, layer, banks, scratch, ctx, x_dram=None, before=None):
    n = core.n
    first = layer == 0
    sides = 2 if first else 1
    scale = float(1.0 / np.sqrt(np.float32(HD))) if first else 1.0
    half_heads = HEADS // 2
    b = [core.bank[k] for k in banks]
    s1, s2, pv, m0, m1 = b[0:2], b[2:4], b[4:6], b[6], b[7]
    groups = HEADS // 4
    slots = Slots(first)

    def sb(name, shape, dt=FP32):
        return ctx.enter_context(nc.sbuf_tensor(f"{name}_{layer}", shape, dt))

    phase = Phase(core, f"attn{layer}")
    sem = phase.sem

    x_in = [sb(f"x_in{k}", [P, TILES, D]) for k in range(2)]
    x_t = [sb(f"x_t{k}", [P, TOK]) for k in range(2)]
    turned = sb("turned", [P, sides, 2, TOK]) if first else None
    exact = sb("exact", [P, sides, TOK])
    rest = sb("rest", [P, sides, TOK])
    parts = sb("parts", [P, 3, sides, TOK], BF16)
    shifts = sb("shifts", [P, TILES, 2, half_heads], BF16)
    shift_rows = [sb(f"shift_rows{k}", [half_heads, TOK], BF16) for k in range(2)]
    probs = sb("probs", [P, RING, TILES, TOK])
    added = sb("added", [P, TILES, D]) if first else None
    y = sb("y", [P, TILES, D])
    stats = sb("stats", [P, TILES, 6])
    moments = sb("moments", [P, TILES, 2])
    shifted_var = sb("shifted_var", [P, TILES])
    rstd = sb("rstd", [P, TILES])
    o_t = sb("o_t", [P, TOK])
    if first:
        values = [sb(f"values{k}", [P, TILES, HEADS, VW]) for k in range(2)]
        heads_t = [sb(f"heads_t{k}", [P, groups, TOK]) for k in range(2)]
        recips = sb("recips", [P, 2, TILES, half_heads])
        o = sb("o", [P, TILES, D])
        x_v = sb("x_v", [P, TOK])
    else:
        v_in = sb("v_in", [P, TILES, D])
        values = [sb(f"values{k}", [P, TILES, HEADS, D + 1]) for k in range(2)]
        recips = sb("recips", [P, 2, TILES])
        o_even = [sb(f"o_even{k}", [P, TILES, D]) for k in range(2)]
        o_odd = [sb(f"o_odd{k}", [P, TILES, D]) for k in range(2)]
        scaled = sb("scaled", [P, 4, TILES, D])
        o = sb("o", [P, TILES, D])

    ones_ready = sem("ones_ready")
    x_loaded = [sem(f"x_loaded{k}") for k in range(2)]
    xt_in_psum = sem("xt_in_psum")
    xt_ready = sem("xt_ready")
    x_v_ready = sem("x_v_ready")
    qk_in_psum = sem("qk_in_psum")
    qk_taken = sem("qk_taken")
    exact_ready = sem("exact_ready")
    part0_ready = sem("part0_ready")
    rest_ready = sem("rest_ready")
    part1_ready = sem("part1_ready")
    var_ready = sem("var_ready")
    parts_ready = sem("parts_ready")
    parts_written = sem("parts_written")
    stacked = [sem(f"stacked{k}") for k in range(2)]
    v_in_psum = sem("v_in_psum")
    v_taken = sem("v_taken")
    values_ready = sem("values_ready")
    max_in_psum = sem("max_in_psum")
    max_done = sem("max_done")
    shifts_in_psum = sem("shifts_in_psum")
    shift_rows_ready = sem("shift_rows_ready")
    shifted = [sem(f"shifted{k}") for k in range(2)]
    s_in_psum = sem("s_in_psum")
    exp_done = sem("exp_done")
    pv_done = sem("pv_done")
    pv_taken = sem("pv_taken")
    scaled_ready = sem("scaled_ready")
    odd_added = sem("odd_added")
    heads_in_psum = sem("heads_in_psum")
    recips_ready = sem("recips_ready")
    o_ready = sem("o_ready")
    ot_in_psum = sem("ot_in_psum")
    ot_ready = sem("ot_ready")
    out_in_psum = sem("out_in_psum")
    added_ready = sem("added_ready")
    y_ready = sem("y_ready")
    stats_ready = sem("stats_ready")
    moments_ready = sem("moments_ready")
    rstd_ready = sem("rstd_ready")
    x_ready = sem("x_ready")

    def stack_rows(parity):
        return slice(parity * HEAD_ROWS, (parity + 1) * HEAD_ROWS)

    @phase.engine("sync")
    def _(sp):
        source = x_dram.rearrange("b (t p) d -> b p t d", p=P) if first else None

        def shift_rows_in(b, hf):
            wait_apart(sp, shift_rows_ready, b.number() * 2 + (hf + 1))
            for parity in range(2):
                sp.dma_start(core.q_stack[b.odd][SHIFT_ROW:SHIFT_ROW + 1, parity, 4 * hf:4 * hf + 4, :].rearrange("q r n -> q (r n)"),
                             shift_rows[hf][4 * parity:4 * parity + 4, :]).then_inc(shifted[hf], 16)

        def stack_in(b, i, on, hf):
            if on(0):
                wait_apart(sp, s_in_psum, i.number() * HEADS + half_heads * (hf + 1))
            prs = slice(4 * hf, 4 * hf + 4)
            for parity in range(2):
                for side, to in ((0, core.k_stack[b.odd][stack_rows(parity), prs, :]),
                                 (1, core.q_stack[b.odd][stack_rows(parity), parity, prs, :])):
                    src = scratch[side, :, parity * 64:(parity + 1) * 64, :].rearrange(
                        "s (d r) n -> s d r n", r=PAIRS)[:, :, prs, :].rearrange("s d r n -> s d (r n)")
                    sp.dma_start(to.rearrange("q r n -> q (r n)"), src).then_inc(stacked[hf], 16)

        def step(i, on):
            if on(4):
                b = i.plus(4)
                if before:
                    wait_for_x(sp, before, 2 * TILES, b)
                wait_apart(sp, xt_in_psum, times(i, 2, n))
                src = source[b.number(), :, :, :] if first else core.xh_all[:, b.number(), :, :]
                sp.dma_start(x_in[b.odd][:, :, :], src).then_inc(x_loaded[b.odd], 16)
            if on(0):
                shift_rows_in(i, 1)
            if on(2):
                b = i.plus(2)
                wait_apart(sp, parts_ready, times(i, 2, n))
                wait_apart(sp, stacked[0], times(i, 1, n) * 64)
                wait_apart(sp, stacked[1], times(i, 1, n) * 64)
                for s, m in RUNS:
                    k = K_PART[s]
                    src = parts[:, k:k + 1, sides - 1, :]
                    if m > 1:
                        src = src.broadcast_to([P, m, TOK])
                    sp.dma_start(scratch[0, s:s + m, :, :].rearrange("s r n -> r s n"), src).then_inc(parts_written, 16)
                    sp.dma_start(scratch[1, s:s + m, :, :].rearrange("s r n -> r s n"),
                                 parts[:, Q_PART[s]:Q_PART[s] + m, 0, :]).then_inc(parts_written, 16)
                wait_apart(sp, parts_written, times(i, 2, n) * (32 * len(RUNS)))
                stack_in(b, i, on, 0)
            if on(1):
                shift_rows_in(i.plus(1), 0)
            if on(2):
                stack_in(i.plus(2), i, on, 1)

        return step

    @phase.engine("gpsimd")
    def _(pool):
        def add_bias(i):
            pool.wait_ge(core.x_all_loaded, 16 * core.x_all_loads)
            wait(pool, y_ready, times(i, -2, n))
            pool.tensor_tensor(added[:, :, :], core.x_all[:, i.plus(-1).number(), :, :],
                               core.b0_out[:, :].unsqueeze(1).broadcast_to([P, TILES, D]),
                               op=ALU.add).then_inc(added_ready, 1)

        def mix_values(i, t, k):
            if t == 0 and k == 0:
                pool.wait_ge(v_taken, times(i, 1, n))
                wait(pool, pv_done, times(i, -1, n) * HEADS)
            heads = slice(k * half_heads, (k + 1) * half_heads)
            pool.tensor_tensor(values[i.plus(1).odd][:, t, heads, 0:D], core.mix[:, heads, :],
                               v_in[:, t, :].unsqueeze(1).broadcast_to([P, half_heads, D]),
                               op=ALU.mult).then_inc(values_ready, 1)

        def add_odd(b, h):
            pool.wait_ge(scaled_ready, (b.number() * half_heads + (h + 1) // 2) * TILES)
            wait(pool, odd_added, b.number() * (half_heads - 1) + (h - 3) // 2)
            pool.tensor_tensor(o_odd[b.odd][:, :, :], o_odd[b.odd][:, :, :], scaled[:, h // 2 % 4, :, :],
                               op=ALU.add).then_inc(odd_added, 1)

        def add_both(b):
            pool.wait_ge(pv_taken, (b.number() + 1) * (half_heads * TILES))
            wait(pool, odd_added, (b.number() + 1) * (half_heads - 1))
            wait(pool, ot_in_psum, times(b, -1, n))
            pool.tensor_tensor(o[:, :, :], o_even[b.odd][:, :, :], o_odd[b.odd][:, :, :], op=ALU.add).then_inc(o_ready, 1)

        def norm_factor(i):
            pool.wait_ge(moments_ready, times(i, -1, n) * TILES)
            pool.tensor_tensor(shifted_var[:, :], moments[:, :, 1], core.ln_shift[:, 0, :], op=ALU.add).then_inc(var_ready, 1)
            pool.wait_ge(var_ready, times(i, -1, n))
            pool.tensor_tensor(rstd[:, :], shifted_var[:, :], core.minus_half[:, 0, :], op=ALU.pow).then_inc(rstd_ready, 1)

        def step0(i, on):
            if on(-1):
                add_bias(i)
            if on(slots.split):
                split(i.plus(slots.split))
            if on(-1):
                norm_factor(i)

        def step1(i, on):
            for s in range(HEADS):
                if s == slots.out + 3 and on(-1):
                    norm_factor(i)
                if s % 2 and s >= 5 and on(0):
                    add_odd(i, s - 2)
                if s == 1 and on(-1):
                    add_odd(i.plus(-1), HEADS - 1)
                    add_both(i.plus(-1))
                if s == 2 and on(slots.split):
                    split(i.plus(slots.split))
                if s in (4, 6, 8, 10) and on(1):
                    mix_values(i, (s - 4) // 4, s // 2 % 2)

        def split(b):
            zeros = core.zeros[:, :].unsqueeze(1).broadcast_to([P, sides, TOK])
            pool.wait_ge(qk_taken, times(b, 0, n) * sides)
            if first:
                pool.tensor_tensor(exact[:, :, :], turned[:, :, 0, :], turned[:, :, 1, :], op=ALU.add).then_inc(exact_ready, 1)
                pool.wait_ge(exact_ready, times(b, 0, n))
            wait(pool, parts_written, times(b, -1, n) * (32 * len(RUNS)))
            pool.tensor_tensor(parts[:, 0, :, :], exact[:, :, :], zeros, op=ALU.add).then_inc(part0_ready, 1)
            pool.wait_ge(part0_ready, times(b, 0, n))
            pool.tensor_tensor(rest[:, :, :], exact[:, :, :], parts[:, 0, :, :], op=ALU.subtract).then_inc(rest_ready, 1)
            pool.wait_ge(rest_ready, times(b, 0, n))
            pool.tensor_tensor(parts[:, 1, :, :], rest[:, :, :], zeros, op=ALU.add).then_inc(part1_ready, 1)
            pool.wait_ge(part1_ready, times(b, 0, n))
            pool.tensor_tensor(parts[:, 2, :, :], rest[:, :, :], parts[:, 1, :, :], op=ALU.subtract).then_inc(parts_ready, 1)

        return step0 if first else step1

    @phase.engine("scalar")
    def _(act):
        def shift_rows_out(b, hf):
            act.wait_ge(shifts_in_psum, b.number() * 2 + (hf + 1))
            wait(act, shifted[hf], b.number() * 32)
            act.activation(shift_rows[hf][:, :], m0[:, :].bitcast(BF16)[0:half_heads, 0:TOK], ACT.Copy).then_inc(shift_rows_ready, 1)

        def take_heads(b, g):
            act.wait_ge(pv_done, b.number() * groups + (g + 1))
            act.activation(heads_t[b.odd][:, g, :], pv[g % 2][:, 0:TOK], ACT.Copy).then_inc(pv_taken, 1)

        def scale_head(b, h):
            act.wait_ge(recips_ready, b.number() * HEADS + (h + 1))
            if h > 8:
                wait(act, odd_added, b.number() * (half_heads - 1) + (h - 9) // 2)
            else:
                wait(act, odd_added, b.number() * (half_heads - 1))
            for t in range(TILES):
                to = o_odd[b.odd][:, t, :] if h == 1 else scaled[:, h // 2 % 4, t, :]
                act.activation(to, pv[h % 2][:, t * (D + 1):t * (D + 1) + D], ACT.Copy,
                               scale=recips[:, h % 2, t:t + 1]).then_inc(scaled_ready, 1)

        def step(i, on):
            for s in range(HEADS):
                if s == slots.shifts1 and on(0):
                    shift_rows_out(i, 1)
                if s == 3 and first and on(-1):
                    take_heads(i.plus(-1), 3)
                if s == slots.v and on(1):
                    b = i.plus(1)
                    act.wait_ge(v_in_psum, times(i, 1, n))
                    if first:
                        wait(act, pv_done, times(i, -1, n) * groups)
                        act.activation(values[b.odd][:, :, :, 0:HD],
                                       m0[:, 0:TOK].rearrange("p (t h d) -> p t h d", t=TILES, d=HD),
                                       ACT.Copy).then_inc(v_taken, 1)
                    else:
                        wait(act, values_ready, times(i, 0, n) * (2 * TILES))
                        act.activation(v_in[:, :, :].rearrange("p t d -> p (t d)"), m0[:, 0:TOK], ACT.Copy).then_inc(v_taken, 1)
                if s in (7, 11, 15) and first and on(0):
                    take_heads(i, (s - 7) // 4)
                if s == slots.ot and on(-1):
                    act.wait_ge(ot_in_psum, times(i, -1, n))
                    act.activation(o_t[:, :], m1[:, 0:TOK], ACT.Copy).then_inc(ot_ready, 1)
                if s == slots.shifts0 and on(1):
                    shift_rows_out(i.plus(1), 0)
                if s == slots.xt and first and on(1):
                    act.activation(x_v[:, :], x_t[i.plus(1).odd][:, :], ACT.Copy).then_inc(x_v_ready, 1)
                if s == slots.xt and on(3):
                    b = i.plus(3)
                    act.wait_ge(xt_in_psum, times(i, 3, n))
                    if first:
                        wait(act, x_v_ready, times(i, 1, n))
                        act.activation(x_t[b.odd][:, :], m1[:, 0:TOK], ACT.Copy).then_inc(xt_ready, 1)
                    else:
                        act.activation(x_t[b.odd][:, :], m1[:, 0:TOK], ACT.Identity, scale=core.cols[:, 8:9],
                                       bias=core.cols[:, 9:10]).then_inc(xt_ready, 1)
                if on(0):
                    act.wait_ge(s_in_psum, i.number() * HEADS + (s + 1))
                    if first and s % 4 == 0:
                        wait(act, pv_done, i.number() * groups + (s // 4 - 1))
                    if not first:
                        wait(act, pv_done, i.number() * HEADS + (s + 1 - RING))
                    act.activation(probs[:, s % RING, :, :].rearrange("p t n -> p (t n)"), s2[s % 2][:, :], ACT.Exp,
                                   scale=scale).then_inc(exp_done, 1)
                if not first and s % 2 and on(0 if s > 1 else -1):
                    scale_head(i if s > 1 else i.plus(-1), (s - 2) % HEADS)

        return step

    @phase.engine("vector")
    def _(dve):
        def sum_head(b, h):
            dve.wait_ge(recips_ready, b.number() * HEADS + (h + 1))
            wait(dve, pv_taken, (b.number() * half_heads + h // 2) * TILES)
            for t in range(TILES):
                part = pv[h % 2][:, t * (D + 1):t * (D + 1) + D]
                if h == 0:
                    dve.tensor_scalar(o_even[b.odd][:, t, :], part, recips[:, h % 2, t:t + 1], None,
                                      ALU.mult).then_inc(pv_taken, 1)
                else:
                    dve.scalar_tensor_tensor(o_even[b.odd][:, t, :], part, recips[:, h % 2, t:t + 1],
                                             o_even[b.odd][:, t, :], op0=ALU.mult, op1=ALU.add).then_inc(pv_taken, 1)

        def heads_of(k):
            return (m0, m1)[k][:, :].rearrange("p (t h c) -> p t h c", t=TILES, c=VW)

        def recip_heads(i, k):
            dve.wait_ge(heads_in_psum, times(i, -2, n) * 2 + (2 - k))
            dve.reciprocal(recips[:, k, :, :], heads_of(k)[:, :, :, HD]).then_inc(recips_ready, 1)

        def scale_heads(i, k):
            dve.wait_ge(recips_ready, times(i, -2, n) * 2 + (2 - k))
            dve.tensor_tensor(o[:, :, k * 64:(k + 1) * 64].rearrange("p t (h d) -> p t h d", d=HD),
                              heads_of(k)[:, :, :, 0:HD],
                              recips[:, k, :, :].unsqueeze(3).broadcast_to([P, TILES, half_heads, HD]),
                              op=ALU.mult).then_inc(o_ready, 1)

        def recip_head(b, h):
            dve.wait_ge(pv_done, b.number() * HEADS + (h + 1))
            if h % 2:
                wait(dve, scaled_ready, (b.number() * half_heads + h // 2) * TILES)
            else:
                wait(dve, pv_taken, (b.number() * half_heads + h // 2) * TILES)
            sums = pv[h % 2][:, 0:TILES * (D + 1)].rearrange("p (t c) -> p t c", t=TILES)[:, :, D]
            dve.reciprocal(recips[:, h % 2, :], sums).then_inc(recips_ready, 1)

        def step(i, on):
            for s in range(HEADS):
                if s in slots.heads and on(-1):
                    recip_heads(i, slots.heads.index(s))
                if on(1):
                    b = i.plus(1)
                    hf, col = s // half_heads, s % 2 * 4 + s // 2 % 4
                    dve.wait_ge(max_in_psum, b.number() * HEADS + (s + 1))
                    dve.tensor_reduce(shifts[:, :, hf, col], s1[s % 2][:, :].rearrange("p (t n) -> p t n", t=TILES),
                                      op=ALU.max, axis=AX.X, negate=True).then_inc(max_done, 1)
                if not first and on(0 if s >= 2 else -1):
                    b, h = (i, s - 2) if s >= 2 else (i.plus(-1), s + HEADS - 2)
                    recip_head(b, h)
                    if h % 2 == 0:
                        sum_head(b, h)
                if s in slots.heads and on(-1):
                    scale_heads(i, slots.heads.index(s))
                if first and s in (slots.q, slots.k) and on(3):
                    side = int(s == slots.k)
                    dve.wait_ge(qk_in_psum, times(i, 2, n) * 2 + (side + 1))
                    wait(dve, exact_ready, times(i, 2, n))
                    dve.tensor_tensor(turned[:, side, :, :], (m1, m0)[side][:, :].rearrange("p (v n) -> p v n", v=2),
                                      core.rope[:, :, :], op=ALU.mult).then_inc(qk_taken, 1)
                if not first and s == slots.q and on(3):
                    dve.wait_ge(qk_in_psum, times(i, 3, n))
                    wait(dve, rest_ready, times(i, 2, n))
                    dve.tensor_copy(exact[:, 0, :], m1[:, 0:TOK]).then_inc(qk_taken, 1)
                if s == slots.out and on(-1):
                    b = i.plus(-1)
                    wait(dve, x_ready, times(i, -2, n) * TILES)
                    if first:
                        dve.wait_ge(added_ready, times(i, -1, n))
                    dve.wait_ge(out_in_psum, times(i, -1, n))
                    dve.tensor_tensor(y[:, :, :], m1[:, 0:TOK].rearrange("p (t d) -> p t d", t=TILES),
                                      added[:, :, :] if first else core.x_all[:, b.number(), :, :],
                                      op=ALU.add).then_inc(y_ready, 1)
                if s == slots.out + 1 and on(-1):
                    wait_apart(dve, y_ready, times(i, -1, n))
                    for t in range(TILES):
                        dve.bn_stats(stats[:, t, :], y[:, t, :]).then_inc(stats_ready, 1)
                if s == slots.out + 2 and on(-1):
                    wait_apart(dve, var_ready, times(i, -2, n))
                    wait_apart(dve, stats_ready, times(i, -1, n) * TILES)
                    for t in range(TILES):
                        dve.bn_aggr(moments[:, t, :], stats[:, t, :]).then_inc(moments_ready, 1)
                if s == slots.norm and on(-slots.norm_lag):
                    b = i.plus(-slots.norm_lag)
                    dve.wait_ge(rstd_ready, times(b, 0, n))
                    dve.wait_ge(moments_ready, times(b, 0, n) * TILES)
                    for t in range(TILES):
                        dve.tensor_scalar(core.x_all[:, b.number(), t, :], y[:, t, :], moments[:, t, 0:1],
                                          rstd[:, t:t + 1], ALU.subtract, ALU.mult).then_inc(x_ready, 1)

        for v in values:
            if first:
                dve.memset(v[:, :, :, HD:VW], 0.0).then_inc(ones_ready, 1)
            else:
                dve.memset(v[:, :, :, D:D + 1], 1.0).then_inc(ones_ready, 1)
        if first:
            for k, v in enumerate(values):
                dve.wait_ge(ones_ready, k + 1)
                dve.memset(v[:, :, :, HD:HD + 1], 1.0).then_inc(ones_ready, 1)
        return step

    @phase.engine("tensor")
    def _(pe):
        def shifts_turned(b, hf):
            pe.wait_ge(max_done, b.number() * HEADS + half_heads * (hf + 1))
            for t in range(TILES):
                last = pe.transpose(m0[:, :].bitcast(BF16)[0:half_heads, t * P:(t + 1) * P], shifts[:, t, hf, :],
                                    core.ident_bf[:, :])
            last.then_inc(shifts_in_psum, 1)

        def products_by_group(b, g, t):
            if t == 0:
                if g == 0:
                    pe.wait_ge(v_taken, b.number() + 1)
                pe.wait_ge(exp_done, b.number() * HEADS + 4 * (g + 1))
                wait(pe, pv_taken, b.number() * groups + (g - 1))
            for a in range(4):
                h = 4 * g + a
                last = pe.matmul(pv[g % 2][VW * a:VW * (a + 1), 0:TOK], values[b.odd][:, t, h, :],
                                 probs[:, h % RING, t, :], start=(t == 0), stop=(t == TILES - 1),
                                 skip_group_check=True)
            if t == TILES - 1:
                last.then_inc(pv_done, 1)

        def products_of_head(b, h):
            if h == 0:
                pe.wait_ge(values_ready, (b.number() + 1) * (2 * TILES))
            pe.wait_ge(exp_done, b.number() * HEADS + (h + 1))
            wait(pe, scaled_ready if h % 2 else pv_taken, (b.number() * half_heads + h // 2) * TILES)
            for q in range(TILES):
                for t in range(TILES):
                    last = pe.matmul(pv[h % 2][:, q * (D + 1):(q + 1) * (D + 1)], probs[:, h % RING, t, q * P:(q + 1) * P],
                                     values[b.odd][:, t, h, :], start=(t == 0), stop=(t == TILES - 1))
            last.then_inc(pv_done, 1)

        def step(i, on):
            for s in range(HEADS):
                if s == slots.shifts1 and on(0):
                    pe.wait_ge(shift_rows_ready, i.number() * 2 + 1)
                    if first:
                        wait(pe, v_taken, times(i, 0, n))
                    shifts_turned(i, 1)
                if s == slots.v and on(1):
                    b = i.plus(1)
                    if first:
                        pe.wait_ge(x_v_ready, times(i, 1, n))
                        wait(pe, shift_rows_ready, b.number() * 2 + 1)
                    else:
                        wait(pe, shift_rows_ready, times(i, 0, n) * 2)
                    x_turned = x_v if first else x_t[b.odd]
                    w_v = core.w0_v[:, :] if first else core.w1_kv[:, 1, :]
                    for t in range(TILES):
                        last = pe.matmul(m0[:, t * P:(t + 1) * P], x_turned[:, t * P:(t + 1) * P], w_v,
                                         start=True, stop=True)
                    last.then_inc(v_in_psum, 1)
                if s in slots.heads and on(-1):
                    b = i.plus(-1)
                    k = slots.heads.index(s)
                    pe.wait_ge(pv_taken, times(i, -1, n) * groups)
                    if k == 0:
                        wait(pe, qk_taken, times(i, 3, n) * 2)
                        wait(pe, shift_rows_ready, times(i, 0, n) * 2)
                    else:
                        wait(pe, qk_taken, times(i, 3, n) * 2 - 1)
                        wait(pe, y_ready, times(i, -2, n))
                    for t in range(TILES):
                        for g in range(2):
                            last = pe.transpose((m0, m1)[k][:, (2 * t + g) * P:(2 * t + g + 1) * P],
                                                heads_t[b.odd][:, 2 * k + g, t * P:(t + 1) * P], core.ident[:, :])
                    last.then_inc(heads_in_psum, 1)
                if s == slots.ot and on(-1):
                    b = i.plus(-1)
                    if first:
                        pe.wait_ge(o_ready, times(i, -1, n) * 2)
                    else:
                        pe.wait_ge(o_ready, times(i, -1, n))
                        wait(pe, qk_taken, times(i, 2, n))
                        wait(pe, y_ready, times(i, -2, n))
                    for t in range(TILES):
                        last = pe.transpose(m1[:, t * P:(t + 1) * P], o[:, t, :], core.ident[:, :])
                    last.then_inc(ot_in_psum, 1)
                if s == slots.shifts0 and on(1):
                    if first:
                        wait(pe, o_ready, times(i, -1, n) * 2)
                        wait(pe, qk_taken, times(i, 3, n) * 2)
                    else:
                        wait(pe, v_taken, times(i, 1, n))
                    wait(pe, shift_rows_ready, times(i, 0, n) * 2)
                    shifts_turned(i.plus(1), 0)
                if s == slots.out and on(-1):
                    pe.wait_ge(ot_ready, times(i, -1, n))
                    w_out = core.w0_out if first else core.w1_out
                    for t in range(TILES):
                        last = pe.matmul(m1[:, t * P:(t + 1) * P], o_t[:, t * P:(t + 1) * P], w_out[:, :],
                                         start=True, stop=True)
                    last.then_inc(out_in_psum, 1)
                if s == slots.xt and on(3):
                    b = i.plus(3)
                    pe.wait_ge(x_loaded[b.odd], (b.half + 1) * 16)
                    wait(pe, y_ready, times(i, -2 if first else -1, n))
                    wait(pe, qk_taken, times(i, 2, n) * sides)
                    for t in range(TILES):
                        last = pe.transpose(m1[:, t * P:(t + 1) * P], x_in[b.odd][:, t, :], core.ident[:, :])
                    last.then_inc(xt_in_psum, 1)
                if s in (slots.q, slots.k) and on(3):
                    b = i.plus(3)
                    side = int(s == slots.k)
                    if side == 0:
                        pe.wait_ge(xt_ready, times(i, 3, n))
                    else:
                        wait(pe, shift_rows_ready, times(i, 0, n) * 2)
                        wait(pe, v_taken, times(i, 0, n))
                        wait(pe, qk_taken, times(i, 2, n) * 2)
                    if first:
                        for v in range(2):
                            last = pe.matmul((m1, m0)[side][:, v * TOK:(v + 1) * TOK], core.w0_qk[:, side, v, :],
                                             x_t[b.odd][:, :], start=True, stop=True)
                    else:
                        last = pe.matmul(m1[:, 0:TOK], core.w1_qk[:, :], x_t[b.odd][:, :], start=True, stop=True)
                    last.then_inc(qk_in_psum, 1)
                if on(0):
                    b = i
                    if s % half_heads == 0:
                        pe.wait_ge(shifted[s // half_heads], b.number() * 32 + 32)
                    wait(pe, exp_done, b.number() * HEADS + (s - 1))
                    for t in range(TILES):
                        last = pe.matmul(s2[s % 2][:, t * TOK:(t + 1) * TOK],
                                         core.k_stack[b.odd][0:SHIFT_ROW + 1, s // 2, t * P:(t + 1) * P],
                                         core.q_stack[b.odd][0:SHIFT_ROW + 1, s % 2, s // 2, :], start=True, stop=True)
                    last.then_inc(s_in_psum, 1)
                if on(1):
                    b = i.plus(1)
                    if s % half_heads == 0:
                        pe.wait_ge(stacked[s // half_heads], b.number() * 64 + 64)
                    wait(pe, max_done, b.number() * HEADS + (s - 1))
                    for t in range(TILES):
                        last = pe.matmul(s1[s % 2][:, t * TOK:(t + 1) * TOK],
                                         core.q_stack[b.odd][0:PAIR_ROWS, s % 2, s // 2, t * P:(t + 1) * P],
                                         core.k_stack[b.odd][0:PAIR_ROWS, s // 2, :], start=True, stop=True)
                    last.then_inc(max_in_psum, 1)
                if first:
                    if s in (1, 2) and on(-1):
                        products_by_group(i.plus(-1), 3, s - 1)
                    if s >= 5 and s % 4 in (1, 2) and on(0):
                        products_by_group(i, (s - 5) // 4, s % 4 - 1)
                elif s >= 2:
                    if on(0):
                        products_of_head(i, s - 2)
                elif on(-1):
                    products_of_head(i.plus(-1), s + HEADS - 2)

        return step

    return phase


def ffn0(nc, core, before, ctx):
    n = core.n
    chunks = 4
    xt_bank, out_bank = core.bank[0], core.bank[1]
    up_banks = (core.bank[2:4], core.bank[4:6])
    turn_banks = core.bank[6:8]

    def sb(name, shape, dt=FP32):
        return ctx.enter_context(nc.sbuf_tensor(f"{name}_f0", shape, dt, side="right"))

    phase = Phase(core, "ffn0")
    sem = phase.sem

    x_in = [sb(f"x_in{k}", [P, TILES, D]) for k in range(2)]
    x_t = [sb(f"x_t{k}", [P, TOK]) for k in range(2)]
    h = [sb(f"h{k}", [P, TILES, chunks * D]) for k in range(2)]
    h_t = sb("h_t", [P, chunks, TOK])
    y = [sb(f"y{k}", [P, TILES, D]) for k in range(2)]
    h_stats, y_stats = (sb(f"{v}_stats", [P, TILES, 6]) for v in "hy")
    h_moments, y_moments = (sb(f"{v}_moments", [P, TILES, 2]) for v in "hy")
    h_var, h_rstd = sb("h_var", [P, TILES]), sb("h_rstd", [P, TILES])
    y_scaled, y_var, y_rstd = (sb(v, [P, 2, TILES]) for v in ("y_scaled", "y_var", "y_rstd"))

    x_loaded = [sem(f"x_loaded{k}") for k in range(2)]
    xt_in_psum = sem("xt_in_psum")
    xt_ready = sem("xt_ready")
    up_in_psum = sem("up_in_psum")
    h_ready = sem("h_ready")
    h_norm_ready = sem("h_norm_ready")
    turned_in_psum = sem("turned_in_psum")
    h_t_ready = sem("h_t_ready")
    out_in_psum = sem("out_in_psum")
    y_ready = sem("y_ready")
    y_scaled_ready = sem("y_scaled_ready")
    x_ready = sem("x_ready")
    h_sems, y_sems = ({k: sem(f"{v}_{k}") for k in ("stats", "moments", "var", "rstd")} for v in "hy")

    @phase.engine("sync")
    def _(sp):
        def step(i, on):
            if on(4):
                b = i.plus(4)
                wait_for_x(sp, before, TILES, b)
                wait_apart(sp, xt_in_psum, times(i, 2, n))
                sp.dma_start(x_in[b.odd][:, :, :], core.x_all[:, b.number(), :, :]).then_inc(x_loaded[b.odd], 16)

        return step

    @phase.engine("gpsimd")
    def _(pool):
        def step(i, on):
            if on(2):
                pool.wait_ge(h_sems["moments"], times(i, 2, n) * TILES)
                pool.tensor_tensor(h_var[:, :], h_moments[:, :, 1], core.ln_shift[:, 0, :], op=ALU.add).then_inc(h_sems["var"], 1)
                pool.wait_ge(h_sems["var"], times(i, 2, n))
                pool.tensor_tensor(h_rstd[:, :], h_var[:, :], core.minus_half[:, 0, :], op=ALU.pow).then_inc(h_sems["rstd"], 1)
            if on(0):
                pool.wait_ge(y_sems["moments"], times(i, 0, n) * TILES)
                pool.tensor_tensor(y_scaled[:, :, :], y_moments[:, :, 1].unsqueeze(1).broadcast_to([P, 2, TILES]),
                                   core.ln_scale[:, :, :], op=ALU.mult).then_inc(y_scaled_ready, 1)
                pool.wait_ge(y_scaled_ready, times(i, 0, n))
                pool.tensor_tensor(y_var[:, :, :], y_scaled[:, :, :], core.ln_shift[:, :, :], op=ALU.add).then_inc(y_sems["var"], 1)
                pool.wait_ge(y_sems["var"], times(i, 0, n))
                pool.tensor_tensor(y_rstd[:, :, :], y_var[:, :, :], core.minus_half[:, :, :], op=ALU.pow).then_inc(y_sems["rstd"], 1)

        return step

    @phase.engine("scalar")
    def _(act):
        def step(i, on):
            if on(3):
                b = i.plus(3)
                act.wait_ge(xt_in_psum, times(i, 3, n))
                wait(act, up_in_psum, times(i, 1, n) * TILES)
                act.activation(x_t[b.odd][:, :], xt_bank[:, 0:TOK], ACT.Copy).then_inc(xt_ready, 1)
            if on(0):
                for c in range(chunks):
                    if c % 2 == 0:
                        act.wait_ge(turned_in_psum, times(i, -1, n) * 2 + (c // 2 + 1))
                    act.activation(h_t[:, c, :], turn_banks[c // 2][:, c % 2 * TOK:(c % 2 + 1) * TOK], ACT.Identity,
                                   scale=core.cols[:, c:c + 1], bias=core.cols[:, 4 + c:5 + c]).then_inc(h_t_ready, 1)
            if on(2):
                b = i.plus(2)
                wait(act, turned_in_psum, times(i, 0, n) * 2)
                for t in range(TILES):
                    act.wait_ge(up_in_psum, times(i, 1, n) * TILES + (t + 1))
                    act.activation(h[b.odd][:, t, :], up_banks[b.odd][t][:, :], ACT.Gelu).then_inc(h_ready, 1)

        return step

    @phase.engine("vector")
    def _(dve):
        def step(i, on):
            late, last = i.plus(2), i.plus(-1)
            if on(2):
                wait_apart(dve, h_ready, times(i, 2, n) * TILES)
                wait_apart(dve, h_sems["moments"], times(i, 1, n) * TILES)
                for t in range(TILES):
                    dve.bn_stats(h_stats[:, t, :], h[late.odd][:, t, :]).then_inc(h_sems["stats"], 1)
            if on(0):
                dve.wait_ge(out_in_psum, times(i, 0, n))
                dve.tensor_tensor(y[i.odd][:, :, :], out_bank[:, 0:TOK].rearrange("p (t d) -> p t d", t=TILES),
                                  core.x_all[:, i.number(), :, :], op=ALU.add).then_inc(y_ready, 1)
            if on(2):
                wait_apart(dve, h_sems["var"], times(i, 1, n))
                wait_apart(dve, h_norm_ready, times(i, 1, n) * TILES)
                wait_apart(dve, h_sems["stats"], times(i, 2, n) * TILES)
                for t in range(TILES):
                    dve.bn_aggr(h_moments[:, t, :], h_stats[:, t, :]).then_inc(h_sems["moments"], 1)
            if on(0):
                wait_apart(dve, y_ready, times(i, 0, n))
                for t in range(TILES):
                    dve.bn_stats(y_stats[:, t, :], y[i.odd][:, t, :]).then_inc(y_sems["stats"], 1)
            if on(-1):
                dve.wait_ge(y_sems["rstd"], times(i, -1, n))
                dve.wait_ge(y_sems["moments"], times(i, -1, n) * TILES)
                for k, to in enumerate((core.x_all, core.xh_all)):
                    for t in range(TILES):
                        dve.tensor_scalar(to[:, last.number(), t, :], y[last.odd][:, t, :], y_moments[:, t, 0:1],
                                          y_rstd[:, k, t:t + 1], ALU.subtract, ALU.mult).then_inc(x_ready, 1)
            if on(0):
                wait_apart(dve, y_scaled_ready, times(i, -1, n))
                wait_apart(dve, x_ready, times(i, -1, n) * (2 * TILES))
                wait_apart(dve, y_sems["stats"], times(i, 0, n) * TILES)
                for t in range(TILES):
                    dve.bn_aggr(y_moments[:, t, :], y_stats[:, t, :]).then_inc(y_sems["moments"], 1)
            if on(2):
                dve.wait_ge(h_sems["rstd"], times(i, 2, n))
                dve.wait_ge(h_sems["moments"], times(i, 2, n) * TILES)
                for t in range(TILES):
                    dve.tensor_scalar(h[late.odd][:, t, :], h[late.odd][:, t, :], h_moments[:, t, 0:1], h_rstd[:, t:t + 1],
                                      ALU.subtract, ALU.mult).then_inc(h_norm_ready, 1)

        return step

    @phase.engine("tensor")
    def _(pe):
        def step(i, on):
            if on(3):
                b = i.plus(3)
                pe.wait_ge(x_loaded[b.odd], (b.half + 1) * 16)
                wait(pe, xt_ready, times(i, 2, n))
                for t in range(TILES):
                    last = pe.transpose(xt_bank[:, t * P:(t + 1) * P], x_in[b.odd][:, t, :], core.ident[:, :])
                last.then_inc(xt_in_psum, 1)
            if on(0):
                pe.wait_ge(h_norm_ready, times(i, 0, n) * TILES)
                wait(pe, h_t_ready, times(i, -1, n) * chunks)
                for k in range(2):
                    for c in range(2):
                        for t in range(TILES):
                            last = pe.transpose(turn_banks[k][:, (2 * c + t) * P:(2 * c + t + 1) * P],
                                                h[i.odd][:, t, (2 * k + c) * D:(2 * k + c + 1) * D],
                                                core.ident[:, :])
                    last.then_inc(turned_in_psum, 1)
            if on(2):
                b = i.plus(2)
                pe.wait_ge(xt_ready, times(i, 2, n))
                wait(pe, h_ready, times(i, 0, n) * TILES)
                for t in range(TILES):
                    pe.matmul(up_banks[b.odd][t][:, :], x_t[b.odd][:, t * P:(t + 1) * P],
                              core.w0_fc[:, :, :].rearrange("p c d -> p (c d)"), start=True, stop=True).then_inc(up_in_psum, 1)
            if on(0):
                pe.wait_ge(h_t_ready, times(i, 0, n) * chunks)
                wait(pe, y_ready, times(i, -1, n))
                for t in range(TILES):
                    for c in range(chunks):
                        last = pe.matmul(out_bank[:, t * P:(t + 1) * P], h_t[:, c, t * P:(t + 1) * P],
                                         core.w0_proj[:, c, :], start=(c == 0), stop=(c == chunks - 1))
                last.then_inc(out_in_psum, 1)

        return step

    return phase


def ffn1(nc, core, out, before, ctx):
    n = core.n
    chunks = 3
    xt_bank, out_bank = core.bank[2], core.bank[0]
    up_banks = tuple(tuple(core.bank[k] for k in ks) for ks in ((3, 5, 6), (7, 1, 4)))
    out_v = out.rearrange("b (t p) d -> b p t d", p=P)

    def sb(name, shape, dt=FP32):
        return ctx.enter_context(nc.sbuf_tensor(f"{name}_f1", shape, dt, side="right"))

    phase = Phase(core, "ffn1")
    sem = phase.sem

    x_in = [sb(f"x_in{k}", [P, TILES, D]) for k in range(2)]
    x_t = [sb(f"x_t{k}", [P, TOK]) for k in range(2)]
    gate = sb("gate", [P, chunks, TOK])
    h_t = [sb(f"h_t{k}", [P, chunks, TOK]) for k in range(2)]
    y = sb("y", [P, TILES, D])
    stats = sb("stats", [P, TILES, 6])
    moments = sb("moments", [P, TILES, 2])
    var = sb("var", [P, TILES])
    rstd = sb("rstd", [P, TILES])
    x_out = [sb(f"x_out{k}", [P, TILES, D]) for k in range(2)]

    x_loaded = [sem(f"x_loaded{k}") for k in range(2)]
    xt_in_psum = sem("xt_in_psum")
    xt_ready = sem("xt_ready")
    up_in_psum = sem("up_in_psum")
    gate_ready = sem("gate_ready")
    h_ready = sem("h_ready")
    out_in_psum = sem("out_in_psum")
    y_ready = sem("y_ready")
    stats_ready = sem("stats_ready")
    moments_ready = sem("moments_ready")
    var_ready = sem("var_ready")
    rstd_ready = sem("rstd_ready")
    x_out_ready = sem("x_out_ready")
    stored = [sem(f"stored{k}") for k in range(2)]

    @phase.engine("sync")
    def _(sp):
        def step(i, on):
            if on(3):
                b = i.plus(3)
                wait_for_x(sp, before, TILES, b)
                wait_apart(sp, xt_in_psum, times(i, 1, n))
                sp.dma_start(x_in[b.odd][:, :, :], core.x_all[:, b.number(), :, :]).then_inc(x_loaded[b.odd], 16)
            if on(-1):
                b = i.plus(-1)
                wait_apart(sp, x_out_ready, times(i, -1, n) * TILES)
                sp.dma_start(out_v[b.number(), :, :, :], x_out[b.odd][:, :, :]).then_inc(stored[b.odd], 16)

        return step

    @phase.engine("gpsimd")
    def _(pool):
        def step(i, on):
            if on(0):
                pool.wait_ge(moments_ready, times(i, 0, n) * TILES)
                pool.tensor_tensor(var[:, :], moments[:, :, 1], core.ln_shift[:, 0, :], op=ALU.add).then_inc(var_ready, 1)
                pool.wait_ge(var_ready, times(i, 0, n))
                pool.tensor_tensor(rstd[:, :], var[:, :], core.minus_half[:, 0, :], op=ALU.pow).then_inc(rstd_ready, 1)

        return step

    @phase.engine("scalar")
    def _(act):
        def step(i, on):
            if on(2):
                b = i.plus(2)
                act.wait_ge(xt_in_psum, times(i, 2, n))
                wait(act, up_in_psum, times(i, 0, n) * chunks)
                act.activation(x_t[b.odd][:, :], xt_bank[:, 0:TOK], ACT.Copy).then_inc(xt_ready, 1)
            if on(1):
                b = i.plus(1)
                wait(act, h_ready, times(i, 0, n) * chunks)
                for c in range(chunks):
                    act.wait_ge(up_in_psum, times(i, 0, n) * chunks + (c + 1))
                    act.activation(gate[:, c, :], up_banks[b.odd][c][:, 0:TOK], ACT.Silu).then_inc(gate_ready, 1)

        return step

    @phase.engine("vector")
    def _(dve):
        def step(i, on):
            if on(-1):
                b = i.plus(-1)
                dve.wait_ge(rstd_ready, times(i, -1, n))
                dve.wait_ge(moments_ready, times(i, -1, n) * TILES)
                wait(dve, stored[b.odd], b.half * 16)
                for t in range(TILES):
                    dve.tensor_scalar(x_out[b.odd][:, t, :], y[:, t, :], moments[:, t, 0:1], rstd[:, t:t + 1],
                                      ALU.subtract, ALU.mult).then_inc(x_out_ready, 1)
            if on(1):
                b = i.plus(1)
                for c in range(chunks):
                    dve.wait_ge(gate_ready, times(i, 0, n) * chunks + (c + 1))
                    dve.tensor_tensor(h_t[b.odd][:, c, :], up_banks[b.odd][c][:, TOK:2 * TOK], gate[:, c, :],
                                      op=ALU.mult).then_inc(h_ready, 1)
            if on(0):
                wait(dve, x_out_ready, times(i, -1, n) * TILES)
                dve.wait_ge(out_in_psum, times(i, 0, n))
                dve.tensor_tensor(y[:, :, :], out_bank[:, 0:TOK].rearrange("p (t d) -> p t d", t=TILES),
                                  core.x_all[:, i.number(), :, :], op=ALU.add).then_inc(y_ready, 1)
                wait_apart(dve, y_ready, times(i, 0, n))
                for t in range(TILES):
                    dve.bn_stats(stats[:, t, :], y[:, t, :]).then_inc(stats_ready, 1)
                wait_apart(dve, var_ready, times(i, -1, n))
                wait_apart(dve, stats_ready, times(i, 0, n) * TILES)
                for t in range(TILES):
                    dve.bn_aggr(moments[:, t, :], stats[:, t, :]).then_inc(moments_ready, 1)

        return step

    @phase.engine("tensor")
    def _(pe):
        def step(i, on):
            if on(2):
                b = i.plus(2)
                pe.wait_ge(x_loaded[b.odd], (b.half + 1) * 16)
                wait(pe, xt_ready, times(i, 1, n))
                for t in range(TILES):
                    last = pe.transpose(xt_bank[:, t * P:(t + 1) * P], x_in[b.odd][:, t, :], core.ident[:, :])
                last.then_inc(xt_in_psum, 1)
            if on(1):
                b = i.plus(1)
                pe.wait_ge(xt_ready, times(i, 1, n))
                wait(pe, h_ready, times(i, -1, n) * chunks)
                for c in range(chunks):
                    pe.matmul(up_banks[b.odd][c][:, 0:TOK], core.w1_gate[:, c, :], x_t[b.odd][:, :], start=True, stop=True)
                    pe.matmul(up_banks[b.odd][c][:, TOK:2 * TOK], core.w1_up[:, c, :], x_t[b.odd][:, :],
                              start=True, stop=True).then_inc(up_in_psum, 1)
            if on(0):
                pe.wait_ge(h_ready, times(i, 0, n) * chunks)
                wait(pe, y_ready, times(i, -1, n))
                for t in range(TILES):
                    for c in range(chunks):
                        last = pe.matmul(out_bank[:, t * P:(t + 1) * P], h_t[i.odd][:, c, t * P:(t + 1) * P],
                                         core.w1_down[:, c, :], start=(c == 0), stop=(c == chunks - 1))
                last.then_inc(out_in_psum, 1)

        return step

    return phase


_WEIGHTS = {"w_qkv": "L0_attn_w_qkv", "w_out0": "L0_attn_w_out", "b_out": "L0_attn_b_out", "w_fc": "L0_ffn_W_fc",
            "ln_w": "L0_ffn_ln_w", "ln_b": "L0_ffn_ln_b", "w_proj": "L0_ffn_W_proj", "ln_g1": "L1_attn_ln_g",
            "ln_b1": "L1_attn_ln_b", "w_kv": "L1_attn_W_kv", "w_x": "L1_attn_W_x", "w_out1": "L1_attn_W_out",
            "w_gate": "L1_ffn_w_gate", "w_up": "L1_ffn_w_up", "w_down": "L1_ffn_w_down"}


def program(core, kind, eng, phases):
    early, late, attn0, ffn0_, attn1, ffn1_ = phases
    n = core.n
    assert n % 2 == 0 and n >= 8

    def final(on_kind, phase, **counts):
        if kind == on_kind:
            for name, count in counts.items():
                eng.wait_ge(phase.sems[name], count)

    early.begin(kind, eng)
    attn0.begin(kind, eng)
    attn0.at(-4, -3)
    if kind in ("sync", "scalar"):
        late.begin(kind, eng)
        final("sync", late, q_stacks_set=2)
        attn0.at(-2)
    else:
        attn0.at(-2)
        late.begin(kind, eng)
    final("tensor", late, late_taken=1)
    attn0.at(-1)
    final("tensor", attn0, ones_ready=4)
    attn0.at(0, 1)
    attn0.loop()
    attn0.at(n - 4, n - 3, n - 2)

    ffn0_.begin(kind, eng)
    final("tensor", attn0, max_done=n * HEADS)
    ffn0_.at(-4, -3)
    attn0.at(n - 1)
    final("tensor", attn0, exp_done=n * HEADS)
    ffn0_.at(-2)
    attn0.at(n)
    final("tensor", attn0, pv_taken=n * (HEADS // 4))
    ffn0_.at(-1)
    attn0.at(n + 1)
    final("tensor", attn0, y_ready=n, o_ready=2 * n)
    final("vector", attn0, x_ready=n * TILES)
    ffn0_.at(0, 1)
    final("sync", attn0, x_ready=n * TILES)
    ffn0_.loop()
    ffn0_.at(n - 4)

    attn1.begin(kind, eng)
    final("tensor", ffn0_, xt_ready=n)
    attn1.at(-4, -3)
    final("sync", attn0, s_in_psum=n * HEADS, stacked0=n * 64, stacked1=n * 64)
    if kind == "gpsimd":
        attn1.at(-2)
        ffn0_.at(n - 3)
    else:
        ffn0_.at(n - 3)
        attn1.at(-2)
    ffn0_.at(n - 2, n - 1)
    final("tensor", ffn0_, h_ready=n * TILES)
    attn1.at(-1)
    ffn0_.at(n)
    final("tensor", ffn0_, h_t_ready=n * 4, y_ready=n)
    final("tensor", attn1, ones_ready=2)
    final("vector", ffn0_, x_ready=n * 2 * TILES)
    attn1.at(0, 1)
    final("sync", ffn0_, x_ready=n * 2 * TILES)
    attn1.loop()
    attn1.at(n - 4, n - 3, n - 2)

    ffn1_.begin(kind, eng)
    final("tensor", attn1, max_done=n * HEADS)
    ffn1_.at(-3, -2)
    attn1.at(n - 1)
    final("tensor", attn1, exp_done=n * HEADS)
    ffn1_.at(-1)
    attn1.at(n)
    final("tensor", attn1, pv_taken=n * HEADS, scaled_ready=n * HEADS, y_ready=n, shift_rows_ready=2 * n)
    final("vector", attn1, x_ready=n * TILES)
    ffn1_.at(0, 1)
    final("sync", attn1, x_ready=n * TILES)
    ffn1_.loop()
    ffn1_.at(n - 4, n - 3, n - 2, n - 1, n)
    final("sync", ffn1_, stored0=n // 2 * 16, stored1=n // 2 * 16)


def build(nc, x, weights, out):
    n = x.shape[0]
    scratch = nc.dram_tensor("score_parts", (2, SLOTS, P, TOK), BF16, kind="Internal").ap()
    w = dict(weights, x=x)
    w["rope"] = nc.inline_tensor(rope_tables(), name="rope_tables").ap()
    with ExitStack() as ctx:
        core = Core(nc, ctx, n)
        places = [ExitStack() for _ in range(5)]
        attn0 = attention(nc, core, 0, (0, 1, 2, 3, 4, 5, 6, 7), scratch, places[0], x_dram=x)
        early, late = prepare(nc, core, w, places[1])
        places[1].close()
        ffn0_ = ffn0(nc, core, attn0, places[2])
        places[0].close()
        attn1 = attention(nc, core, 1, (2, 3, 5, 6, 7, 1, 4, 0), scratch, places[3], before=ffn0_)
        places[2].close()
        ffn1_ = ffn1(nc, core, out, attn1, places[4])
        phases = (early, late, attn0, ffn0_, attn1, ffn1_)

        with nc.Block() as block:
            @block.sync
            def _(sp):
                program(core, "sync", sp, phases)

            @block.gpsimd
            def _(pool):
                program(core, "gpsimd", pool, phases)

            @block.scalar
            def _(act):
                program(core, "scalar", act, phases)

            @block.vector
            def _(dve):
                program(core, "vector", dve, phases)

            @block.tensor
            def _(pe):
                program(core, "tensor", pe, phases)

        places[3].close()
        places[4].close()


def kernel(**inputs):
    import numpy as _np
    import concourse.bacc as _bacc
    from concourse import mybir as _mybir
    from concourse.bass_utils import run_bass_kernel_spmd as _run

    nc = _bacc.Bacc("TRN2", target_bir_lowering=False, num_devices=1)
    arrays, aps = {}, {}
    for name in ["L0_attn_x", *_WEIGHTS.values()]:
        a = _np.ascontiguousarray(inputs[name])
        arrays[f"in_{name}"] = a
        aps[name] = nc.dram_tensor(f"in_{name}", a.shape, _mybir.dt.from_np(a.dtype), kind="ExternalInput").ap()
    shape = arrays["in_L0_attn_x"].shape
    out = nc.dram_tensor("out_x", shape, _mybir.dt.float32, kind="ExternalOutput").ap()
    build(nc, aps["L0_attn_x"], {k: aps[v] for k, v in _WEIGHTS.items()}, out)
    r = _run(nc, [arrays], core_ids=[0])
    return r.results[0]["out_x"]
```
